# Optimizing a Trainium2 kernel written in Bass

```python
import numpy as np
import jax
import jax.numpy as jnp

def _softmax(x, axis=-1):
    return jax.nn.softmax(x, axis=axis)

def _gelu(x):
    return jax.nn.gelu(x, approximate=True)

def _silu(x):
    return jax.nn.silu(x)

def _sigmoid(x):
    return jax.nn.sigmoid(x)

def _layernorm(x, axis=-1, eps=1e-05):
    m = jnp.mean(x, axis=axis, keepdims=True)
    v = jnp.var(x, axis=axis, keepdims=True)
    return (x - m) / jnp.sqrt(v + eps)

def _scatter_add(tgt, idx, src, axis=0):
    return tgt.at[idx].add(src)

def _segment_sum(src, seg, n):
    return jax.ops.segment_sum(src, seg, n)
kernel_name = 'mk_flamingo_gated_d2_seqx_r8_4f32b3'

def setup_inputs(seed: int=0):
    np.random.seed(seed)
    _w = jnp.asarray

    def _rec_inputs():
        import jax
        import jax.numpy as jnp
        _rk = jax.random.key(seed)
        x = -0.0002928 + 1 * jax.random.normal(jax.random.fold_in(_rk, 1), (16, 256, 128), jnp.float32)
        _lenS = 256 - jax.random.randint(jax.random.fold_in(_rk, 7), (16,), 0, max(1, 256 // 4) + 1, jnp.int32)
        _lenS2 = 1601 - jax.random.randint(jax.random.fold_in(_rk, 8), (16,), 0, max(1, 1601 // 4) + 1, jnp.int32)
        _ctx_512P = jax.random.normal(jax.random.fold_in(_rk, 11), (16, 16, 64), jnp.float32)
        _ctx_512c = jax.random.dirichlet(jax.random.fold_in(_rk, 511), 0.3 * jnp.ones((16,), jnp.float32), (16, 1601))
        _ctx_512t = jnp.einsum('bsk,bkd->bsd', _ctx_512c, _ctx_512P)
        _ctx_512t = _ctx_512t * jax.lax.rsqrt(jnp.mean(jnp.square(_ctx_512t)) + 1e-12) * 0.953939
        ctx_512 = 0.00222621 + 0.99962 * (_ctx_512t + 0.3 * jax.random.normal(jax.random.fold_in(_rk, 611), (16, 1601, 64), jnp.float32))
        _g = jax.random.normal(jax.random.fold_in(_rk, 9001), (2, 2), jnp.float32)
        _g = jnp.sign(_g) * jnp.maximum(jnp.abs(_g), 1.0) + (_g == 0) * 1.0
        g_xattn = _g[0]
        g_ffn = _g[1]
        return (x, ctx_512, g_xattn, g_ffn)
    x, ctx_512, g_xattn, g_ffn = _rec_inputs()

    def _L0_xattn_setup():
        import jax, jax.numpy as jnp
        import numpy as np
        B, T, TC, C, CC, H = (2, 256, 64, 128, 64, 16)
        D = C // H

        def _heads(t):
            b, l, _ = t.shape
            return t.reshape(b, l, H, D).transpose(0, 2, 1, 3)
        key = jax.random.key(seed)
        ks = jax.random.split(key, 18)
        w = lambda k, i, o: jax.random.normal(k, (i, o), jnp.float32) / np.sqrt(i).astype(np.float32)
        return {'x': jax.random.normal(ks[0], (B, T, C), jnp.float32), 'cross_input': jax.random.normal(ks[1], (B, TC, CC), jnp.float32), 'Wk': w(ks[2], C, C), 'bk': jnp.zeros((C,), jnp.float32), 'Wq': w(ks[3], C, C), 'bq': jnp.zeros((C,), jnp.float32), 'Wv': w(ks[4], C, C), 'bv': jnp.zeros((C,), jnp.float32), 'Wck': w(ks[5], CC, C), 'bck': jnp.zeros((C,), jnp.float32), 'Wcq': w(ks[6], C, C), 'bcq': jnp.zeros((C,), jnp.float32), 'Wcv': w(ks[7], CC, C), 'bcv': jnp.zeros((C,), jnp.float32), 'Wp': w(ks[8], C, C), 'bp': jnp.zeros((C,), jnp.float32)}
    _L0_xattn_all = _L0_xattn_setup()
    _L0_xattn_in = {k: v for k, v in _L0_xattn_all.items() if k in ('Wk', 'bk', 'Wq', 'bq', 'Wv', 'bv', 'Wck', 'bck', 'Wcq', 'bcq', 'Wcv', 'bcv', 'Wp', 'bp')}
    del _L0_xattn_all

    def _L0_ffn_setup():
        import jax, jax.numpy as jnp
        import numpy as np
        EPS_NORM = 1e-08
        EPS_Q = 1e-05

        def rmsnorm(x, w):
            v = jnp.mean(jnp.square(x.astype(jnp.float32)), axis=-1, keepdims=True)
            x_hat = x * jax.lax.rsqrt(v + EPS_NORM)
            return (x_hat * w).astype(x.dtype)

        def activation_quant(x):
            scale = 127.0 / jnp.clip(jnp.max(jnp.abs(x), axis=-1, keepdims=True), EPS_Q, None)
            return jnp.clip(jnp.round(x * scale), -128, 127) / scale

        def weight_quant(w):
            scale = 1.0 / jnp.clip(jnp.mean(jnp.abs(w)), EPS_Q, None)
            return jnp.clip(jnp.round(w * scale), -1, 1) / scale

        def bitlinear(x, norm_w, w):
            x_norm = rmsnorm(x, norm_w)
            x_q = x_norm + jax.lax.stop_gradient(activation_quant(x_norm) - x_norm)
            w_q = w + jax.lax.stop_gradient(weight_quant(w) - w)
            return jnp.einsum('bsd,hd->bsh', x_q, w_q)
        key = jax.random.key(seed)
        k1, k2, k3 = jax.random.split(key, 3)
        dim, hidden = (128, 512)
        return {'x': jax.random.normal(k1, (4, 256, dim), dtype=jnp.float32), 'norm1_w': jnp.ones((dim,), jnp.float32), 'w1': jax.random.normal(k2, (hidden, dim), jnp.float32) * 0.02, 'act_scale': jnp.ones((1,), jnp.float32), 'act_bias': jnp.zeros((1,), jnp.float32), 'norm2_w': jnp.ones((hidden,), jnp.float32), 'w2': jax.random.normal(k3, (dim, hidden), jnp.float32) * 0.02}
    _L0_ffn_all = _L0_ffn_setup()
    _L0_ffn_in = {k: v for k, v in _L0_ffn_all.items() if k in ('norm1_w', 'w1', 'act_scale', 'act_bias', 'norm2_w', 'w2')}
    del _L0_ffn_all

    def _L1_xattn_setup():
        import jax, jax.numpy as jnp
        import numpy as np
        HEADS = 16
        D_MODEL = 128
        IMG_MODEL = 64
        D_K = D_MODEL // HEADS
        key = jax.random.key(seed)
        ks = jax.random.split(key, 12)
        B, LQ, LKV = (8, 256, 128)
        s_dm = 1.0 / np.sqrt(D_MODEL)
        s_im = 1.0 / np.sqrt(IMG_MODEL)
        return {'q': jax.random.normal(ks[0], (B, LQ, D_MODEL), jnp.float32), 'k': jax.random.normal(ks[1], (B, LKV, IMG_MODEL), jnp.float32), 'v': jax.random.normal(ks[2], (B, LKV, IMG_MODEL), jnp.float32), 'Wq': jax.random.normal(ks[3], (D_MODEL, D_MODEL), jnp.float32) * s_dm, 'bq': jnp.zeros((D_MODEL,), jnp.float32), 'Wk': jax.random.normal(ks[4], (IMG_MODEL, D_MODEL), jnp.float32) * s_im, 'bk': jnp.zeros((D_MODEL,), jnp.float32), 'Wv': jax.random.normal(ks[5], (IMG_MODEL, D_MODEL), jnp.float32) * s_im, 'bv': jnp.zeros((D_MODEL,), jnp.float32), 'Wo': jax.random.normal(ks[6], (D_MODEL, D_MODEL), jnp.float32) * s_dm, 'bo': jnp.zeros((D_MODEL,), jnp.float32)}
    _L1_xattn_all = _L1_xattn_setup()
    _L1_xattn_in = {k: v for k, v in _L1_xattn_all.items() if k in ('Wq', 'bq', 'Wk', 'bk', 'Wv', 'bv', 'Wo', 'bo')}
    del _L1_xattn_all

    def _L1_ffn_setup():
        import jax, jax.numpy as jnp
        import numpy as np
        D_MODEL, D_FF, N_EXPERTS, TOP_K = (128, 256, 8, 2)
        B, S = (2, 256)
        key = jax.random.key(seed)
        ks = jax.random.split(key, 6)
        sd = 1.0 / np.sqrt(D_MODEL)
        sf = 1.0 / np.sqrt(D_FF)
        return {'x': jax.random.normal(ks[0], (B, S, D_MODEL), jnp.float32), 'router_w': jax.random.normal(ks[1], (N_EXPERTS, D_MODEL), jnp.float32) * sd, 'gate_w': jax.random.normal(ks[2], (N_EXPERTS, D_MODEL, D_FF), jnp.float32) * sd, 'gate_b': jnp.zeros((N_EXPERTS, D_FF), jnp.float32), 'up_w': jax.random.normal(ks[3], (N_EXPERTS, D_MODEL, D_FF), jnp.float32) * sd, 'up_b': jnp.zeros((N_EXPERTS, D_FF), jnp.float32), 'down_w': jax.random.normal(ks[4], (N_EXPERTS, D_FF, D_MODEL), jnp.float32) * sf, 'down_b': jnp.zeros((N_EXPERTS, D_MODEL), jnp.float32)}
    _L1_ffn_all = _L1_ffn_setup()
    _L1_ffn_in = {k: v for k, v in _L1_ffn_all.items() if k in ('router_w', 'gate_w', 'gate_b', 'up_w', 'up_b', 'down_w', 'down_b')}
    del _L1_ffn_all
    return {'x': x, 'ctx_512': ctx_512, 'g_xattn': g_xattn, 'g_ffn': g_ffn, 'L0_xattn_Wk': _L0_xattn_in['Wk'], 'L0_xattn_bk': _L0_xattn_in['bk'], 'L0_xattn_Wq': _L0_xattn_in['Wq'], 'L0_xattn_bq': _L0_xattn_in['bq'], 'L0_xattn_Wv': _L0_xattn_in['Wv'], 'L0_xattn_bv': _L0_xattn_in['bv'], 'L0_xattn_Wck': _L0_xattn_in['Wck'], 'L0_xattn_bck': _L0_xattn_in['bck'], 'L0_xattn_Wcq': _L0_xattn_in['Wcq'], 'L0_xattn_bcq': _L0_xattn_in['bcq'], 'L0_xattn_Wcv': _L0_xattn_in['Wcv'], 'L0_xattn_bcv': _L0_xattn_in['bcv'], 'L0_xattn_Wp': _L0_xattn_in['Wp'], 'L0_xattn_bp': _L0_xattn_in['bp'], 'L0_ffn_norm1_w': _L0_ffn_in['norm1_w'], 'L0_ffn_w1': _L0_ffn_in['w1'], 'L0_ffn_act_scale': _L0_ffn_in['act_scale'], 'L0_ffn_act_bias': _L0_ffn_in['act_bias'], 'L0_ffn_norm2_w': _L0_ffn_in['norm2_w'], 'L0_ffn_w2': _L0_ffn_in['w2'], 'L1_xattn_Wq': _L1_xattn_in['Wq'], 'L1_xattn_bq': _L1_xattn_in['bq'], 'L1_xattn_Wk': _L1_xattn_in['Wk'], 'L1_xattn_bk': _L1_xattn_in['bk'], 'L1_xattn_Wv': _L1_xattn_in['Wv'], 'L1_xattn_bv': _L1_xattn_in['bv'], 'L1_xattn_Wo': _L1_xattn_in['Wo'], 'L1_xattn_bo': _L1_xattn_in['bo'], 'L1_ffn_router_w': _L1_ffn_in['router_w'], 'L1_ffn_gate_w': _L1_ffn_in['gate_w'], 'L1_ffn_gate_b': _L1_ffn_in['gate_b'], 'L1_ffn_up_w': _L1_ffn_in['up_w'], 'L1_ffn_up_b': _L1_ffn_in['up_b'], 'L1_ffn_down_w': _L1_ffn_in['down_w'], 'L1_ffn_down_b': _L1_ffn_in['down_b']}

def reference(x, ctx_512, g_xattn, g_ffn, L0_xattn_Wk, L0_xattn_bk, L0_xattn_Wq, L0_xattn_bq, L0_xattn_Wv, L0_xattn_bv, L0_xattn_Wck, L0_xattn_bck, L0_xattn_Wcq, L0_xattn_bcq, L0_xattn_Wcv, L0_xattn_bcv, L0_xattn_Wp, L0_xattn_bp, L0_ffn_norm1_w, L0_ffn_w1, L0_ffn_act_scale, L0_ffn_act_bias, L0_ffn_norm2_w, L0_ffn_w2, L1_xattn_Wq, L1_xattn_bq, L1_xattn_Wk, L1_xattn_bk, L1_xattn_Wv, L1_xattn_bv, L1_xattn_Wo, L1_xattn_bo, L1_ffn_router_w, L1_ffn_gate_w, L1_ffn_gate_b, L1_ffn_up_w, L1_ffn_up_b, L1_ffn_down_w, L1_ffn_down_b):
    import jax
    import jax.numpy as jnp

    def _L0_xattn_ref(x, cross_input, Wk, bk, Wq, bq, Wv, bv, Wck, bck, Wcq, bcq, Wcv, bcv, Wp, bp):
        import jax, jax.numpy as jnp
        import numpy as np
        B, T, TC, C, CC, H = (2, 256, 64, 128, 64, 16)
        D = C // H

        def _heads(t):
            b, l, _ = t.shape
            return t.reshape(b, l, H, D).transpose(0, 2, 1, 3)
        scale = np.float32(1.0 / np.sqrt(D))
        q = _heads(x @ Wq + bq)
        k = _heads(x @ Wk + bk)
        v = _heads(x @ Wv + bv)
        att = jnp.einsum('bhqd,bhkd->bhqk', q, k) * scale
        causal = jnp.tril(jnp.ones((T, T), bool))
        att = jnp.where(causal[None, None], att, -jnp.inf)
        y = jnp.einsum('bhqk,bhkd->bhqd', jax.nn.softmax(att, axis=-1), v)
        qc = _heads(x @ Wcq + bcq)
        kc = _heads(cross_input @ Wck + bck)
        vc = _heads(cross_input @ Wcv + bcv)
        attc = jnp.einsum('bhqd,bhkd->bhqk', qc, kc) * scale
        y = y + jnp.einsum('bhqk,bhkd->bhqd', jax.nn.softmax(attc, axis=-1), vc)
        y = y.transpose(0, 2, 1, 3).reshape(x.shape[0], T, C)
        return y @ Wp + bp

    def _L0_ffn_ref(x, norm1_w, w1, act_scale, act_bias, norm2_w, w2):
        import jax, jax.numpy as jnp
        import numpy as np
        EPS_NORM = 1e-08
        EPS_Q = 1e-05

        def rmsnorm(x, w):
            v = jnp.mean(jnp.square(x.astype(jnp.float32)), axis=-1, keepdims=True)
            x_hat = x * jax.lax.rsqrt(v + EPS_NORM)
            return (x_hat * w).astype(x.dtype)

        def activation_quant(x):
            scale = 127.0 / jnp.clip(jnp.max(jnp.abs(x), axis=-1, keepdims=True), EPS_Q, None)
            return jnp.clip(jnp.round(x * scale), -128, 127) / scale

        def weight_quant(w):
            scale = 1.0 / jnp.clip(jnp.mean(jnp.abs(w)), EPS_Q, None)
            return jnp.clip(jnp.round(w * scale), -1, 1) / scale

        def bitlinear(x, norm_w, w):
            x_norm = rmsnorm(x, norm_w)
            x_q = x_norm + jax.lax.stop_gradient(activation_quant(x_norm) - x_norm)
            w_q = w + jax.lax.stop_gradient(weight_quant(w) - w)
            return jnp.einsum('bsd,hd->bsh', x_q, w_q)
        h = bitlinear(x, norm1_w, w1)
        h = act_scale * jnp.square(jax.nn.relu(h)) + act_bias
        y = bitlinear(h, norm2_w, w2)
        return y

    def _L1_xattn_ref(q, k, v, Wq, bq, Wk, bk, Wv, bv, Wo, bo):
        import jax, jax.numpy as jnp
        import numpy as np
        HEADS = 16
        D_MODEL = 128
        IMG_MODEL = 64
        D_K = D_MODEL // HEADS
        B, LQ, _ = q.shape
        LKV = k.shape[1]
        qh = (q @ Wq + bq).reshape(B, LQ, HEADS, D_K).transpose(0, 2, 1, 3)
        kh = (k @ Wk + bk).reshape(B, LKV, HEADS, D_K).transpose(0, 2, 1, 3)
        vh = (v @ Wv + bv).reshape(B, LKV, HEADS, D_K).transpose(0, 2, 1, 3)
        scale = 1.0 / np.sqrt(D_K)
        scores = jnp.einsum('bhqd,bhkd->bhqk', qh, kh) * scale
        attn = jax.nn.softmax(scores, axis=-1)
        out = jnp.einsum('bhqk,bhkd->bhqd', attn, vh)
        concat = out.transpose(0, 2, 1, 3).reshape(B, LQ, D_MODEL)
        return concat @ Wo + bo

    def _L1_ffn_ref(x, router_w, gate_w, gate_b, up_w, up_b, down_w, down_b):
        import jax, jax.numpy as jnp
        import numpy as np
        D_MODEL, D_FF, N_EXPERTS, TOP_K = (128, 256, 8, 2)
        B, S = (2, 256)
        b, s, d = x.shape
        xf = x.reshape(b * s, d)
        n = xf.shape[0]
        router_logits = xf @ router_w.T
        probs = jax.nn.softmax(router_logits, axis=-1)
        topv, topi = jax.lax.top_k(probs, TOP_K)
        mask = jnp.zeros_like(probs).at[jnp.arange(n)[:, None], topi].set(1.0)
        probs = probs * mask
        probs = probs / (probs.sum(axis=-1, keepdims=True) + 1e-09)
        g = jnp.einsum('nd,edf->nef', xf, gate_w) + gate_b
        u = jnp.einsum('nd,edf->nef', xf, up_w) + up_b
        h = jax.nn.silu(g) * u
        expert_out = jnp.einsum('nef,efd->ned', h, down_w) + down_b
        y = jnp.einsum('ne,ned->nd', probs, expert_out)
        return y.reshape(b, s, d)
    x = x + jnp.tanh(g_xattn[0]) * _L0_xattn_ref(_layernorm(x, axis=-1), ctx_512, L0_xattn_Wk, L0_xattn_bk, L0_xattn_Wq, L0_xattn_bq, L0_xattn_Wv, L0_xattn_bv, L0_xattn_Wck, L0_xattn_bck, L0_xattn_Wcq, L0_xattn_bcq, L0_xattn_Wcv, L0_xattn_bcv, L0_xattn_Wp, L0_xattn_bp)
    x = x + jnp.tanh(g_ffn[0]) * _L0_ffn_ref(_layernorm(x, axis=-1), L0_ffn_norm1_w, L0_ffn_w1, L0_ffn_act_scale, L0_ffn_act_bias, L0_ffn_norm2_w, L0_ffn_w2)
    x = x + jnp.tanh(g_xattn[1]) * _L1_xattn_ref(_layernorm(x, axis=-1), ctx_512, ctx_512, L1_xattn_Wq, L1_xattn_bq, L1_xattn_Wk, L1_xattn_bk, L1_xattn_Wv, L1_xattn_bv, L1_xattn_Wo, L1_xattn_bo)
    x = x + jnp.tanh(g_ffn[1]) * _L1_ffn_ref(_layernorm(x, axis=-1), L1_ffn_router_w, L1_ffn_gate_w, L1_ffn_gate_b, L1_ffn_up_w, L1_ffn_up_b, L1_ffn_down_w, L1_ffn_down_b)
    return x

_drawn_inputs = setup_inputs


def setup_inputs(seed=0):
    import zlib

    import numpy as np

    out = dict(_drawn_inputs(seed))
    spreads = {'g_ffn': (-1.0, 0.6),
     'L0_xattn_bk': (0.0, 0.8),
     'L0_xattn_bq': (0.0, 0.302),
     'L0_xattn_bv': (0.0, 0.1),
     'L0_xattn_bck': (0.0, 0.8),
     'L0_xattn_bcq': (0.0, 0.1),
     'L0_xattn_bcv': (0.0, 0.1),
     'L0_xattn_bp': (0.0, 0.1),
     'L0_ffn_norm1_w': (1.0, 0.2),
     'L0_ffn_norm2_w': (1.0, 0.2),
     'L1_xattn_bq': (0.0, 0.1),
     'L1_xattn_bk': (0.0, 0.8),
     'L1_xattn_bv': (0.0, 0.1),
     'L1_xattn_bo': (0.0, 0.1),
     'L1_ffn_gate_b': (0.0, 0.276),
     'L1_ffn_up_b': (0.0, 0.277),
     'L1_ffn_down_b': (0.0, 0.1)}
    factors = {}
    for name, (base, spread) in spreads.items():
        noise = np.random.default_rng([zlib.crc32(name.encode()), seed]).standard_normal(out[name].shape)
        drawn = base * np.exp(spread * noise) if base else spread * noise
        out[name] = jnp.asarray(drawn.astype(out[name].dtype))
    for name, factor in factors.items():
        out[name] = (out[name] * factor).astype(out[name].dtype)
    return out
```

```python
from contextlib import ExitStack

import numpy as np

import concourse.bass as bass
from concourse import mybir

F32 = mybir.dt.float32
BF16 = mybir.dt.bfloat16
ALU = mybir.AluOpType
ACT = mybir.ActivationFunctionType
AX_X = mybir.AxisListType.X

P = 128
NB = 16
T = 256
QT = T // P
C = 128
H = 16
D = C // H
NK = 1601
CC = 64
KT = 13
FULL = KT - 1
TAIL = NK - FULL * P
HID = 512
HT = HID // P
NE = 8
FF = 256
FT = FF // P
QUADS = 4
HQ = H // QUADS
PARTS = 3
TERMS = PARTS * PARTS * D
ROWS = TERMS + PARTS
SCALE = float(np.float32(1.0 / np.sqrt(D)))
MASKED = -1e30
LOWEST = -3e38
MAGIC = 12582912.0
EPS_LN, EPS_NORM, EPS_Q = 1e-5, 1e-8, 1e-5
CHUNK = 512
CHUNKS = [(c * CHUNK, min(CHUNK, NK - c * CHUNK)) for c in range(4)]
MXW = [401, 401, 401, 398]
MX0 = [0, 401, 802, 1203]
P_RING, ST_RING, MX_RING = 2, 2, 2
BASE = 1


class Job:

    def __init__(self, cross, layer, quad, number, tile0, mx0, cross_number):
        self.cross, self.layer, self.quad, self.number = cross, layer, quad, number
        self.tiles = KT if cross else QT
        self.maxima = HQ * QT * (4 if cross else 1)
        self.tile0, self.mx0, self.cross_number = tile0, mx0, cross_number


def plan():
    jobs, tile, mx, xn = [[], []], 0, 0, 0
    for layer in range(2):
        for quad in range(QUADS):
            for cross in ((True, False) if layer == 0 else (True,)):
                j = Job(cross, layer, quad, sum(map(len, jobs)), tile, mx, xn)
                jobs[layer].append(j)
                tile, mx, xn = tile + j.tiles, mx + j.maxima, xn + cross
    return jobs, tile, mx, xn


JOBS, TILES, MAXIMA, CROSSES = plan()
NJ = sum(map(len, JOBS))
assert TILES % P_RING == 0 and TILES % ST_RING == 0 and MAXIMA % MX_RING == 0 and NJ % 2 == 0


def share(job, slots, slot):
    return range(job.maxima * slot // slots, job.maxima * (slot + 1) // slots)


def misc_order():
    out = []

    def context(layer):
        for what in ("ctxT", "key", "val"):
            out.extend(f"{what}{layer}.{c}" for c in range(4))

    def attention(layer):
        jobs = JOBS[layer]
        out.append(f"nT{jobs[0].number}")
        for n, job in enumerate(jobs):
            for slot in range(job.tiles):
                if slot == 1 and n:
                    out.append(f"Y{jobs[n - 1].number}")
                if slot == min(4, job.tiles - 1) and n + 1 < len(jobs):
                    out.append(f"nT{jobs[n + 1].number}")
        out.append(f"Y{jobs[-1].number}")
        out.extend([f"yT{layer}", f"proj{layer}"])

    context(0)
    out.extend(["xT0", "qc0", "q0", "k0", "v0"])
    attention(0)
    out.extend(["a1T", "hid.0", "hid.1", "a2T.0", "a2T.1", "ffn"])
    context(1)
    out.extend(["xT1", "qc1"])
    attention(1)
    out.extend(["xT2", "router", "prT"])
    for e in range(NE):
        out.extend([f"gate{e}", f"up{e}", f"down{e}"])
    out.append("downb")
    return {name: n for n, name in enumerate(out)}


MISC = misc_order()
NM = len(MISC)
DVE_STEPS, ACT_STEPS, POOL_STEPS = 56, 0, 66


class Link:

    def __init__(self, eng, sem, per_turn, then=None):
        self.eng, self.sem, self.per_turn, self.n, self.base, self.turn = eng, sem, per_turn, 0, 0, None
        self.then = then

    def start_turn(self, b):
        self.base, self.turn, self.n = self.base + self.n, b, 0

    def __call__(self, ins):
        self.n += 1
        ins.then_inc(self.sem, 1)
        v = self.base + self.n
        self.eng.wait_ge(self.sem, v if self.turn is None else self.turn * self.per_turn + v)
        if self.then and self.turn is not None:
            self.then()

    def end_turn(self):
        assert self.n == self.per_turn, ("linked steps", self.sem, self.n, self.per_turn)


def flamingo_gated_blocks(nc, w, x_d, ctx_d, out_d):
    x_v = x_d.rearrange("b (t p) c -> b p t c", p=P)
    out_v = out_d.rearrange("b (t p) c -> b p t c", p=P)
    ctx_main = ctx_d[:, 0:FULL * P, :].rearrange("b (p t) c -> b p (t c)", t=FULL)
    ctx_tail = ctx_d[:, FULL * P:NK, :]

    with ExitStack() as stack:
        def sb(name, shape, dt=F32):
            return stack.enter_context(nc.sbuf_tensor(name, shape, dt))

        def sem(name):
            return stack.enter_context(nc.semaphore(name))

        ident = sb("ident", [P, P])
        ident_b = sb("ident_b", [P, P], BF16)
        causal = sb("causal", [P, 2 * P])
        minus_half = sb("minus_half", [P, 4])
        index_score = sb("index_score", [P, NE])
        gx = sb("gx", [P, 2])
        gf = sb("gf", [P, 2])
        tx = sb("tx", [P, 2])
        tf = sb("tf", [P, 2])
        tf_half = sb("tf_half", [P, 1])
        wq0, wk0, wv0, wcq0, wp0 = (sb(n, [P, C]) for n in ("wq0", "wk0", "wv0", "wcq0", "wp0"))
        wq1, wo1 = (sb(n, [P, C]) for n in ("wq1", "wo1"))
        wck = [sb(f"wck{i}", [CC + 1, C]) for i in range(2)]
        wcv = [sb(f"wcv{i}", [CC + 1, C]) for i in range(2)]
        bias_col = sb("bias_col", [P, 4])
        bv0 = sb("bv0", [P, C])
        bp = [sb(f"bp{i}", [P, C]) for i in range(2)]
        nw1 = sb("nw1", [P, C])
        nw2 = sb("nw2", [P, HID])
        act_s = sb("act_s", [P, 1])
        act_b = sb("act_b", [P, 1])
        wide_a = sb("wide_a", [P, 2, HID])
        wide_b = sb("wide_b", [P, 2, HID])
        ones = wide_b[:, 0, 0:P]
        wraw = wide_a
        wabs = sb("wabs", [P, 2])
        wstat = sb("wstat", [P, 4])
        a2 = sb("a2", [P, QT, HID], BF16)
        wtern = a2
        t1T = sb("t1T", [P, HID], BF16)
        t2T = sb("t2T", [P, HT, C], BF16)
        ma2t = sb("ma2t", [P, 1])
        rw = sb("rw", [NE, C])
        rwT = sb("rwT", [P, NE])
        gate = sb("gate", [P, NE, FF])
        up = sb("up", [P, NE, FF])
        down = sb("down", [P, NE * FT, C])
        bias_rows = sb("bias_rows", [2 * NE * FT, P])
        bias_gu = sb("bias_gu", [P, 2 * NE * FT])
        bias_gh = sb("bias_gh", [P, NE * FT])
        down_b = sb("down_b", [NE, C])

        ctx = sb("ctx", [P, KT * CC])
        ctxT = sb("ctxT", [CC + 1, NK])
        kf = sb("kf", [P, CHUNK])
        kres = sb("kres", [P, CHUNK])
        kpart = [sb(f"kpart{i}", [P, NK], BF16) for i in range(PARTS)]
        KX = sb("KX", [ROWS, H, NK], BF16)
        VX = [sb(f"VX{i}", [P, KT, H, D + 1]) for i in range(2)]
        KS = sb("KS", [ROWS, H, T], BF16)
        VS = sb("VS", [P, QT, H, D + 1])
        QX = [sb(f"QX{i}", [ROWS, H, T], BF16) for i in range(2)]
        QS = sb("QS", [ROWS, H, T], BF16)
        qf = sb("qf", [P, 2, T])
        qres = sb("qres", [P, T])
        qpart = sb("qpart", [P, 3, PARTS, T], BF16)
        x0 = sb("x0", [P, QT, C])
        x1 = sb("x1", [P, QT, C])
        x2 = sb("x2", [P, QT, C])
        x3 = x1
        xb = sb("xb", [P, 2, QT, C])
        stats = sb("stats", [P, 4, QT, 6])
        mv = sb("mv", [P, 4, QT, 2])
        rstd = sb("rstd", [P, 4, QT])
        xn = sb("xn", [P, 2, QT, C])
        xnT = sb("xnT", [P, 3, T])
        probs = sb("probs", [P, P_RING, HQ * T])
        mx = sb("mx", [P, 2, HQ * QT * 4])
        mxs = sb("mxs", [P, T], BF16)
        nm = sb("nm", [P, 2, QT, HQ])
        nres = sb("nres", [P, 2, QT, HQ])
        npart = sb("npart", [P, 2, QT, PARTS, HQ], BF16)
        nT = sb("nT", [PARTS * HQ, 2, T], BF16)
        yt = sb("yt", [P, 2, T])
        rden = sb("rden", [P, QT, HQ])
        yx = [sb(f"yx{i}", [P, QT, H, D]) for i in range(2)]
        ys = sb("ys", [P, QT, H, D])
        yT = sb("yT", [P, T])
        ssq = sb("ssq", [P, 2, QT])
        rms = sb("rms", [P, 2, QT])
        amax = sb("amax", [P, 2, QT])
        qs = sb("qs", [P, 2, QT])
        dq = sb("dq", [P, 2, QT])
        xh1 = sb("xh1", [P, QT, C])
        a1 = sb("a1", [P, QT, C], BF16)
        a1T = sb("a1T", [P, T], BF16)
        hr, h2 = wide_a, wide_b
        a2T = wide_b[:, 1, :].bitcast(BF16).rearrange("p (t k q) -> p t k q", t=QT, k=HT)
        lg = sb("lg", [P, QT, NE])
        pr = sb("pr", [P, QT, NE])
        pick = sb("pick", [P, QT, NE])
        hot = sb("hot", [P, 2, QT, NE])
        rest = sb("rest", [P, QT, NE])
        wts = sb("wts", [P, QT, NE])
        r1 = sb("r1", [P, 6, QT])
        prT = wide_b[0:NE, 1, 0:T]
        tg, gb, hh = (ap.rearrange("p (t n) -> p t n", t=FT) for ap in (wide_a[:, 0, :], wide_a[:, 1, :], wide_b[:, 0, :]))
        acc = sb("acc", [P, QT, C])

        ST = [stack.enter_context(nc.psum_tensor(f"ST{i}", [P, 2 * CHUNK], F32)) for i in range(ST_RING)]
        MX = [stack.enter_context(nc.psum_tensor(f"MX{i}", [P, CHUNK], F32)) for i in range(MX_RING)]
        PV = stack.enter_context(nc.psum_tensor("PV", [P, CHUNK], F32))
        MS = stack.enter_context(nc.psum_tensor("MS", [P, CHUNK], F32))
        MSB = MS[:, :].bitcast(BF16)

        loaded = sem("loaded")
        pool_set, dve_set, act_set, pe_set = sem("pool_set"), sem("dve_set"), sem("act_set"), sem("pe_set")
        dve_step, act_step, pool_step = sem("dve_step"), sem("act_step"), sem("pool_step")
        passed = sem("passed")
        misc_full = sem("misc_full")
        misc_free = sem("misc_free")
        ctx_in, x_in, stored = sem("ctx_in"), sem("x_in"), sem("stored")
        kparts_ready = sem("kparts_ready")
        kx_in = [sem(f"kx_in{g}") for g in range(QUADS)]
        q_in = [sem(f"q_in{i}") for i in range(4)]
        qparts_ready = sem("qparts_ready")
        quad_scored = sem("quad_scored")
        self_scored = sem("self_scored")
        mean_ready, rstd_ready, xn_ready = sem("mean_ready"), sem("rstd_ready"), sem("xn_ready")
        mx_full, mx_free = sem("mx_full"), sem("mx_free")
        nm_ready, nparts_ready = sem("nm_ready"), sem("nparts_ready")
        max_in = [sem(f"max_in{i}") for i in range(2)]
        st_full, exp_done, masked, probs_free = sem("st_full"), sem("exp_done"), sem("masked"), sem("probs_free")
        yt_ready, y_ready = sem("yt_ready"), sem("y_ready")
        xb_ready = sem("xb_ready")
        ssq_ready, rms_ready = sem("ssq_ready"), sem("rms_ready")
        a1_ready, a2_ready, sq_ready, h2_ready = sem("a1_ready"), sem("a2_ready"), sem("sq_ready"), sem("h2_ready")
        lg_ready, e_ready, wts_ready = sem("lg_ready"), sem("e_ready"), sem("wts_ready")

        counted = [misc_full, misc_free, ctx_in, x_in, stored, kparts_ready, *kx_in, *q_in, qparts_ready, quad_scored,
                   self_scored, mean_ready, rstd_ready, xn_ready, mx_full, mx_free, nm_ready, nparts_ready, *max_in,
                   st_full, exp_done, masked, probs_free, yt_ready, y_ready, xb_ready, ssq_ready, rms_ready, a1_ready,
                   a2_ready, sq_ready, h2_ready, lg_ready, e_ready, wts_ready]
        key_rows = nc.dram_tensor("key_rows", [2, PARTS, P, NK], BF16, kind="Internal").ap()
        query_rows = nc.dram_tensor("query_rows", [4, PARTS, P, T], BF16, kind="Internal").ap()
        max_rows = nc.dram_tensor("max_rows", [2, PARTS * HQ, T], BF16, kind="Internal").ap()
        key_out, max_out = sem("key_out"), [sem(f"max_out{i}") for i in range(2)]
        q_out = [sem(f"q_out{i}") for i in range(4)]

        counted += [key_out, *max_out, *q_out]
        block = stack.enter_context(nc.Block())

        def stand_alone(eng):
            eng.sem_inc(passed, 1)

        def use(b, name):
            return NM * b + MISC[name] + 1

        loads = [
            (gx[:, :], w["g_xattn"].partition_broadcast(P)), (gf[:, :], w["g_ffn"].partition_broadcast(P)),
            (wq0[:, :], w["L0_xattn_Wq"]), (wk0[:, :], w["L0_xattn_Wk"]), (wv0[:, :], w["L0_xattn_Wv"]),
            (wcq0[:, :], w["L0_xattn_Wcq"]), (wp0[:, :], w["L0_xattn_Wp"]),
            (wq1[:, :], w["L1_xattn_Wq"]), (wo1[:, :], w["L1_xattn_Wo"]),
            (wck[0][0:CC, :], w["L0_xattn_Wck"]), (wck[0][CC:CC + 1, :], w["L0_xattn_bck"].unsqueeze(0)),
            (wcv[0][0:CC, :], w["L0_xattn_Wcv"]), (wcv[0][CC:CC + 1, :], w["L0_xattn_bcv"].unsqueeze(0)),
            (wck[1][0:CC, :], w["L1_xattn_Wk"]), (wck[1][CC:CC + 1, :], w["L1_xattn_bk"].unsqueeze(0)),
            (wcv[1][0:CC, :], w["L1_xattn_Wv"]), (wcv[1][CC:CC + 1, :], w["L1_xattn_bv"].unsqueeze(0)),
            (bias_col[:, 0:1], w["L0_xattn_bcq"].unsqueeze(1)), (bias_col[:, 1:2], w["L0_xattn_bq"].unsqueeze(1)),
            (bias_col[:, 2:3], w["L0_xattn_bk"].unsqueeze(1)), (bias_col[:, 3:4], w["L1_xattn_bq"].unsqueeze(1)),
            (bv0[:, :], w["L0_xattn_bv"].partition_broadcast(P)),
            (bp[0][:, :], w["L0_xattn_bp"].partition_broadcast(P)), (bp[1][:, :], w["L1_xattn_bo"].partition_broadcast(P)),
            (nw1[:, :], w["L0_ffn_norm1_w"].partition_broadcast(P)), (nw2[:, :], w["L0_ffn_norm2_w"].partition_broadcast(P)),
            (act_s[:, :], w["L0_ffn_act_scale"].partition_broadcast(P)), (act_b[:, :], w["L0_ffn_act_bias"].partition_broadcast(P)),
            (wraw[:, 0, :].rearrange("p (t d) -> p t d", t=HT), w["L0_ffn_w1"].rearrange("(t p) d -> p t d", p=P)),
            (wraw[:, 1, :], w["L0_ffn_w2"]),
            (rw[:, :], w["L1_ffn_router_w"]),
            (gate[:, :, :], w["L1_ffn_gate_w"].rearrange("e d f -> d e f")),
            (up[:, :, :], w["L1_ffn_up_w"].rearrange("e d f -> d e f")),
            (down[:, :, :], w["L1_ffn_down_w"].rearrange("e (t p) d -> p (e t) d", p=P)),
            (bias_rows[0:NE * FT, :], w["L1_ffn_gate_b"].rearrange("e (t p) -> (e t) p", p=P)),
            (bias_rows[NE * FT:2 * NE * FT, :], w["L1_ffn_up_b"].rearrange("e (t p) -> (e t) p", p=P)),
            (down_b[:, :], w["L1_ffn_down_b"]),
        ]
        LOADED = 16 * len(loads)
        POOL_SET, DVE_SET, ACT_SET, PE_SET = 9, 6, 4, 2
        SENT = 16 * PARTS * PARTS

        @block.sync
        def _(sp):
            for s in counted:
                sp.sem_inc(s, BASE)
            for dst, src in loads:
                sp.dma_start(dst, src).then_inc(loaded, 16)
            sp.wait_ge(pool_set, POOL_SET)

            def load_context(b, layer):
                sp.wait_ge(misc_full, (use(b, "ctxT0.3") if layer else NM * b) + BASE)
                stand_alone(sp)
                sp.dma_start(ctx[:, 0:FULL * CC], ctx_main[b]).then_inc(ctx_in, 16)
                sp.dma_start(ctx[0:TAIL, FULL * CC:KT * CC], ctx_tail[b]).then_inc(ctx_in, 16)

            def send_keys(b, layer):
                sp.wait_ge(kparts_ready, len(CHUNKS) * (2 * b + layer + 1) + BASE)
                stand_alone(sp)
                for g in range(QUADS):
                    sp.wait_ge(kx_in[g], SENT * (2 * b + layer) + BASE)
                    stand_alone(sp)
                for i in range(PARTS):
                    sp.dma_start(key_rows[layer, i], kpart[i][:, :]).then_inc(key_out, 16)
                sp.wait_ge(key_out, 16 * PARTS * (2 * b + layer + 1) + BASE)
                stand_alone(sp)
                for g in range(QUADS):
                    sp.wait_ge(quad_scored, CROSSES * b + layer * QUADS + g + 1 + BASE)
                    stand_alone(sp)
                    for i in range(PARTS):
                        src = key_rows[layer, i, g * HQ * D:(g + 1) * HQ * D, :].rearrange("(h d) n -> d h n", d=D)
                        for r in range(PARTS):
                            row = (i * PARTS + r) * D
                            sp.dma_start(KX[row:row + D, g * HQ:(g + 1) * HQ, :], src).then_inc(kx_in[g], 16)

            def send_queries(b, which, dst, key_side):
                sp.wait_ge(qparts_ready, 4 * b + which + 1 + BASE)
                stand_alone(sp)
                sp.wait_ge(q_in[which], SENT * b + BASE)
                stand_alone(sp)
                sp.dma_start(query_rows[which].rearrange("r p n -> p r n"), qpart[:, which % 3, :, :]).then_inc(q_out[which], 16)
                sp.wait_ge(q_out[which], 16 * b + 16 + BASE)
                stand_alone(sp)
                if which in (1, 2):
                    sp.wait_ge(self_scored, QUADS * b + BASE)
                    stand_alone(sp)
                else:
                    sp.wait_ge(quad_scored, (CROSSES * b + (QUADS if which == 3 else 0)) + BASE)
                    stand_alone(sp)
                for j in range(PARTS):
                    src = query_rows[which, j].rearrange("(h d) n -> d h n", d=D)
                    for i in range(PARTS):
                        row = ((j * PARTS + i) if key_side else (i * PARTS + j)) * D
                        sp.dma_start(dst[row:row + D, :, :], src).then_inc(q_in[which], 16)

            def send_maximum(b, job):
                sp.wait_ge(misc_free, use(b, f"nT{job.number}") + BASE)
                stand_alone(sp)
                k, before = job.number % 2, NJ // 2 * b + job.number // 2
                q = QX[job.layer] if job.cross else QS
                sp.wait_ge(max_in[k], 16 * before + BASE)
                stand_alone(sp)
                sp.dma_start(max_rows[k], nT[:, k, :]).then_inc(max_out[k], 16)
                sp.wait_ge(max_out[k], 16 * before + 16 + BASE)
                stand_alone(sp)
                sp.dma_start(q[TERMS:ROWS, job.quad * HQ:(job.quad + 1) * HQ, :],
                             max_rows[k].rearrange("(r h) n -> r h n", h=HQ)).then_inc(max_in[k], 16)

            with sp.Fori(0, NB) as b:
                load_context(b, 0)
                sp.wait_ge(xb_ready, 2 * b + BASE)
                stand_alone(sp)
                sp.wait_ge(xn_ready, 4 * b + BASE)
                stand_alone(sp)
                sp.dma_start(x0[:, :, :], x_v[b]).then_inc(x_in, 16)
                send_keys(b, 0)
                send_queries(b, 0, QX[0], False)
                send_queries(b, 1, QS, False)
                send_queries(b, 2, KS, True)
                for job in JOBS[0]:
                    send_maximum(b, job)
                load_context(b, 1)
                send_keys(b, 1)
                send_queries(b, 3, QX[1], False)
                for job in JOBS[1]:
                    send_maximum(b, job)
                sp.wait_ge(misc_free, use(b, "downb") + BASE)
                stand_alone(sp)
                sp.dma_start(out_v[b], acc[:, :, :]).then_inc(stored, 16)
            sp.wait_ge(stored, 16 * NB + BASE)

        @block.gpsimd
        def _(pool):
            link = Link(pool, pool_step, POOL_STEPS, lambda: stand_alone(pool))
            g = nc.gpsimd
            link(g.memset(ident[:, :], 0.0))
            link(g.memset(causal[:, :], 0.0))
            link(g.affine_select(out=ident[:, :], in_=ident[:, :], pattern=[[1, P]], compare_op=ALU.not_equal, fill=1.0,
                                 base=0, channel_multiplier=-1))
            g.tensor_copy(ident_b[:, :], ident[:, :]).then_inc(pool_set, 1)
            g.affine_select(out=causal[:, P:2 * P], in_=causal[:, P:2 * P], pattern=[[-1, P]], compare_op=ALU.is_ge,
                            fill=MASKED, base=0, channel_multiplier=1).then_inc(pool_set, 1)
            g.memset(ones[:, :], 1.0).then_inc(pool_set, 1)
            g.memset(minus_half[:, :], -0.5).then_inc(pool_set, 1)
            for e in range(NE):
                m = g.memset(index_score[:, e:e + 1], float(NE - e))
            m.then_inc(pool_set, 1)
            pool.wait_ge(pool_set, 5)
            g.memset(ctxT[CC:CC + 1, :], 1.0).then_inc(pool_set, 1)
            pool.wait_ge(pool_set, 6)
            link(g.memset(KX[64:ROWS, :, :], 1.0))
            g.memset(KS[64:ROWS, :, :], 1.0).then_inc(pool_set, 1)
            pool.wait_ge(pool_set, 7)
            g.memset(VX[0][:, :, :, D:D + 1], 1.0)
            g.memset(VX[1][:, :, :, D:D + 1], 1.0).then_inc(pool_set, 1)
            g.memset(VS[:, :, :, D:D + 1], 1.0).then_inc(pool_set, 1)
            pool.wait_ge(pool_set, POOL_SET)
            pool.wait_ge(loaded, LOADED)
            pool.wait_ge(act_set, ACT_SET)
            pool.wait_ge(dve_set, DVE_SET)

            def rsqrt_norm(b, site):
                pool.wait_ge(mean_ready, 4 * b + site + 1 + BASE)
                stand_alone(pool)
                link(g.tensor_scalar(rstd[:, site, :], mv[:, site, :, 1], EPS_LN, 1.0, ALU.add, ALU.mult))
                g.tensor_tensor(rstd[:, site, :], rstd[:, site, :], minus_half[:, 0:QT], ALU.pow).then_inc(rstd_ready, 1)

            def rsqrt_rms(b, site):
                pool.wait_ge(ssq_ready, 2 * b + site + 1 + BASE)
                stand_alone(pool)
                link(g.tensor_scalar(rms[:, site, :], ssq[:, site, :], 1.0 / (HID if site else C), EPS_NORM,
                                     ALU.mult, ALU.add))
                g.tensor_tensor(rms[:, site, :], rms[:, site, :], minus_half[:, 0:QT], ALU.pow).then_inc(rms_ready, 1)

            def split_keys(b, layer):
                for c, (at, n) in enumerate(CHUNKS):
                    s = slice(at, at + n)
                    pool.wait_ge(misc_free, use(b, f"key{layer}.{c}") + BASE)
                    stand_alone(pool)
                    link(g.tensor_tensor(kres[:, 0:n], kf[:, 0:n], kpart[0][:, s], ALU.subtract))
                    link(g.tensor_copy(kpart[1][:, s], kres[:, 0:n]))
                    g.tensor_tensor(kpart[2][:, s], kres[:, 0:n], kpart[1][:, s], ALU.subtract).then_inc(kparts_ready, 1)
                    pool.wait_ge(kparts_ready, len(CHUNKS) * (2 * b + layer) + c + 1 + BASE)
                    stand_alone(pool)

            def split_queries(b, which):
                pool.wait_ge(misc_free, use(b, ("qc0", "q0", "k0", "qc1")[which]) + BASE)
                stand_alone(pool)
                w = which % 3
                link(g.tensor_tensor(qres[:, :], qf[:, which % 2, :], qpart[:, w, 0, :], ALU.subtract))
                link(g.tensor_copy(qpart[:, w, 1, :], qres[:, :]))
                g.tensor_tensor(qpart[:, w, 2, :], qres[:, :], qpart[:, w, 1, :], ALU.subtract).then_inc(qparts_ready, 1)
                pool.wait_ge(qparts_ready, 4 * b + which + 1 + BASE)
                stand_alone(pool)

            def split_maximum(b, job):
                k = job.number % 2
                pool.wait_ge(nm_ready, NJ * b + job.number + 1 + BASE)
                stand_alone(pool)
                pool.wait_ge(misc_full, (use(b, f"nT{job.number - 2}") if job.number >= 2 else NM * b) + BASE)
                stand_alone(pool)
                link(g.tensor_copy(npart[:, k, :, 0, :], nm[:, k, :, :]))
                link(g.tensor_tensor(nres[:, k, :, :], nm[:, k, :, :], npart[:, k, :, 0, :], ALU.subtract))
                link(g.tensor_copy(npart[:, k, :, 1, :], nres[:, k, :, :]))
                g.tensor_tensor(npart[:, k, :, 2, :], nres[:, k, :, :], npart[:, k, :, 1, :],
                                ALU.subtract).then_inc(nparts_ready, 1)

            def mask_probs(b, job, t):
                k = job.tile0 + t
                pool.wait_ge(exp_done, TILES * b + k + 1 + ST_RING + BASE)
                stand_alone(pool)
                v = probs[:, k % P_RING, :]
                if t == 0:
                    v = v.rearrange("p (j q) -> p j q", j=HQ)[:, :, 0:P]
                else:
                    v = v[:, 0:HQ * P].rearrange("p (j q) -> p j q", j=HQ)
                g.affine_select(out=v, in_=v, pattern=[[0, HQ], [1, P]], compare_op=ALU.is_ge, fill=0.0, base=0,
                                channel_multiplier=-1).then_inc(masked, 1)

            def attention(b, layer):
                jobs = JOBS[layer]
                split_maximum(b, jobs[0])
                split_maximum(b, jobs[1])
                for n, job in enumerate(jobs):
                    if not job.cross:
                        for t in range(job.tiles):
                            mask_probs(b, job, t)
                    if n + 2 < len(jobs):
                        split_maximum(b, jobs[n + 2])

            def residual_bias(b, layer):
                if layer == 0:
                    pool.wait_ge(x_in, 16 * b + 16 + BASE)
                    stand_alone(pool)
                else:
                    pool.wait_ge(misc_free, use(b, "ffn") + BASE)
                    stand_alone(pool)
                src = x2 if layer else x0
                bb = bp[layer][:, :].unsqueeze(1).broadcast_to([P, QT, C])
                g.tensor_tensor(xb[:, layer, :, :], src[:, :, :], bb, ALU.add).then_inc(xb_ready, 1)

            with pool.Fori(0, NB) as b:
                link.start_turn(b)
                split_keys(b, 0)
                rsqrt_norm(b, 0)
                residual_bias(b, 0)
                for which in range(3):
                    split_queries(b, which)
                attention(b, 0)
                rsqrt_norm(b, 1)
                rsqrt_rms(b, 0)
                pool.wait_ge(sq_ready, b + 1 + BASE)
                stand_alone(pool)
                g.tensor_scalar(h2[:, :, :], h2[:, :, :], act_s[:, 0:1], act_b[:, 0:1], ALU.mult,
                                ALU.add).then_inc(h2_ready, 1)
                rsqrt_rms(b, 1)
                split_keys(b, 1)
                residual_bias(b, 1)
                rsqrt_norm(b, 2)
                split_queries(b, 3)
                attention(b, 1)
                rsqrt_norm(b, 3)
                link.end_turn()

        @block.scalar
        def _(act):
            a = nc.scalar
            link = Link(act, act_step, ACT_STEPS)
            act.sem_inc(exp_done, ST_RING)
            act.wait_ge(loaded, LOADED)
            act.wait_ge(pool_set, POOL_SET)
            link(a.activation(tx[:, :], gx[:, :], ACT.Tanh))
            link(a.activation(tf[:, :], gf[:, :], ACT.Tanh))
            act.wait_ge(dve_set, DVE_SET)
            for wt in (wq0, wcq0, wq1):
                a.mul(wt[:, :], wt[:, :], SCALE)
            for n in (0, 1, 3):
                a.mul(bias_col[:, n:n + 1], bias_col[:, n:n + 1], SCALE)
            a.mul(wp0[:, :], wp0[:, :], tx[:, 0:1])
            link(a.mul(wo1[:, :], wo1[:, :], tx[:, 1:2]))
            a.mul(bp[0][:, :], bp[0][:, :], tx[:, 0:1]).then_inc(act_set, 1)
            a.mul(bp[1][:, :], bp[1][:, :], tx[:, 1:2]).then_inc(act_set, 1)
            link(a.mul(tf_half[:, :], tf[:, 1:2], 0.5))
            link(a.mul(down[:, :, :], down[:, :, :], tf_half[:, 0:1]))
            a.mul(down_b[:, :], down_b[:, :], tf[0:NE, 1:2]).then_inc(act_set, 1)
            a.mul(ma2t[:, :], wstat[:, 1:2], tf[:, 0:1]).then_inc(act_set, 1)
            act.wait_ge(act_set, ACT_SET)

            def filled(b, name):
                act.wait_ge(misc_full, use(b, name) + BASE)

            def context(b, layer):
                for c, (at, n) in enumerate(CHUNKS):
                    filled(b, f"ctxT{layer}.{c}")
                    a.copy(ctxT[0:CC, at:at + n], MS[0:CC, 0:n]).then_inc(misc_free, 1)
                for c, (at, n) in enumerate(CHUNKS):
                    filled(b, f"key{layer}.{c}")
                    act.wait_ge(kparts_ready, len(CHUNKS) * (2 * b + layer) + c + BASE)
                    if c == 0:
                        for g in range(QUADS):
                            act.wait_ge(kx_in[g], SENT * (2 * b + layer) + BASE)
                    a.copy(kf[:, 0:n], MS[:, 0:n])
                    a.copy(kpart[0][:, at:at + n], MS[:, 0:n]).then_inc(misc_free, 1)
                for c in range(len(CHUNKS)):
                    filled(b, f"val{layer}.{c}")
                    t0, rows = 4 * c, (P if c < 3 else TAIL)
                    t1 = min(t0 + 4, KT)
                    a.copy(VX[layer][0:rows, t0:t1, :, 0:D],
                           MS[0:rows, 0:(t1 - t0) * C].rearrange("p (t h d) -> p t h d", h=H, d=D)).then_inc(misc_free, 1)

            def turned(b, name, dst, src):
                filled(b, name)
                a.copy(dst, src).then_inc(misc_free, 1)

            def queries(b, which, name, bias):
                filled(b, name)
                act.wait_ge(qparts_ready, 4 * b + max(which - 1, 0) + BASE)
                act.wait_ge(q_in[which], SENT * b + BASE)
                if which in (0, 3):
                    act.wait_ge(q_in[3 - which], SENT * (b + (which == 3)) + BASE)
                v = bias_col[:, bias:bias + 1]
                a.activation(qf[:, which % 2, :], MS[:, 0:T], ACT.Identity, bias=v)
                a.activation(qpart[:, which % 3, 0, :], MS[:, 0:T], ACT.Identity, bias=v).then_inc(misc_free, 1)

            def turn_maximum(b, job):
                filled(b, f"nT{job.number}")
                act.wait_ge(max_in[job.number % 2], 16 * (NJ // 2 * b + job.number // 2) + BASE)
                a.copy(nT[:, job.number % 2, :], MSB[0:PARTS * HQ, 0:T]).then_inc(misc_free, 1)

            def take_values(b, job):
                act.wait_ge(probs_free, TILES * b + job.tile0 + job.tiles + P_RING + BASE)
                act.wait_ge(misc_full, (use(b, f"Y{job.number - 2}") if job.number >= 2 else NM * b) + BASE)
                a.copy(yt[:, job.number % 2, :], PV[:, 0:T]).then_inc(yt_ready, 1)

            def attention(b, layer):
                jobs = JOBS[layer]
                turn_maximum(b, jobs[0])
                for n, job in enumerate(jobs):
                    for t in range(job.tiles):
                        k = job.tile0 + t
                        rows = TAIL if job.cross and t == FULL else P
                        cols = HQ * T if job.cross or t == 0 else HQ * P
                        act.wait_ge(st_full, TILES * b + k + 1 + BASE)
                        act.wait_ge(probs_free, TILES * b + k + 1 + BASE)
                        a.activation(probs[0:rows, k % P_RING, 0:cols], ST[k % ST_RING][0:rows, 0:cols],
                                     ACT.Exp).then_inc(exp_done, 1)
                        if t == 0 and n:
                            take_values(b, jobs[n - 1])
                        if t == min(4, job.tiles - 1) and n + 1 < len(jobs):
                            turn_maximum(b, jobs[n + 1])
                take_values(b, jobs[-1])

            with act.Fori(0, NB) as b:
                link.start_turn(b)
                context(b, 0)
                turned(b, "xT0", xnT[:, 0, :], MS[:, 0:T])
                queries(b, 0, "qc0", 0)
                queries(b, 1, "q0", 1)
                queries(b, 2, "k0", 2)
                attention(b, 0)
                turned(b, "yT0", yT[:, :], MS[:, 0:T])
                act.wait_ge(xn_ready, 4 * b + 2 + BASE)
                for t in range(QT):
                    sq = a.activation(h2[:, t, 0:C], xn[:, 1, t, :], ACT.Square, accum_out=ssq[:, 0, t:t + 1])
                sq.then_inc(ssq_ready, 1)
                turned(b, "a1T", a1T[:, :], MSB[:, 0:T])
                act.wait_ge(misc_free, use(b, "hid.1") + BASE)
                a.activation(h2[:, :, :], hr[:, :, :], ACT.Square).then_inc(sq_ready, 1)
                act.wait_ge(h2_ready, b + 1 + BASE)
                for t in range(QT):
                    sq = a.activation(hr[:, t, :], h2[:, t, :], ACT.Square, accum_out=ssq[:, 1, t:t + 1])
                sq.then_inc(ssq_ready, 1)
                for t in range(QT):
                    turned(b, f"a2T.{t}", a2T[:, t, :, :], MSB[:, 0:HID].rearrange("p (k q) -> p k q", k=HT))
                context(b, 1)
                turned(b, "xT1", xnT[:, 1, :], MS[:, 0:T])
                queries(b, 3, "qc1", 3)
                attention(b, 1)
                turned(b, "yT1", yT[:, :], MS[:, 0:T])
                turned(b, "xT2", xnT[:, 2, :], MS[:, 0:T])
                act.wait_ge(lg_ready, b + 1 + BASE)
                a.activation(lg[:, :, :], lg[:, :, :], ACT.Exp).then_inc(e_ready, 1)
                turned(b, "prT", prT, MS[0:NE, 0:T])
                for e in range(NE):
                    filled(b, f"gate{e}")
                    for t in range(FT):
                        n = e * FT + t
                        a.activation(tg[:, t, :], MS[:, t * T:(t + 1) * T], ACT.Tanh, bias=bias_gh[:, n:n + 1], scale=0.5)
                        last = a.activation(gb[:, t, :], MS[:, t * T:(t + 1) * T], ACT.Identity, bias=bias_gu[:, n:n + 1])
                    last.then_inc(misc_free, 1)
                link.end_turn()

        @block.vector
        def _(dve):
            v = nc.vector
            link = Link(dve, dve_step, DVE_STEPS)
            dve.sem_inc(mx_free, MX_RING)
            v.memset(PV[:, :], 0.0).then_inc(dve_set, 1)
            dve.wait_ge(loaded, LOADED)
            v.tensor_reduce(wabs[:, :], wraw[:, :, :], AX_X, ALU.add, apply_absolute_value=True).then_inc(dve_set, 1)
            dve.wait_ge(pe_set, 1)
            link(v.tensor_scalar(wstat[:, 0:2], MX[0][:, 0:2], 1.0 / (HID * C), EPS_Q, ALU.mult, ALU.max))
            link(v.reciprocal(wstat[:, 2:4], wstat[:, 0:2]))
            for i in range(2):
                link(v.tensor_scalar(wraw[:, i, :], wraw[:, i, :], wstat[:, 2 + i:3 + i], MAGIC, ALU.mult, ALU.add))
                link(v.tensor_scalar(wraw[:, i, :], wraw[:, i, :], MAGIC, 1.0, ALU.subtract, ALU.min))
                v.tensor_scalar(wtern[:, i, :], wraw[:, i, :], -1.0, None, ALU.max).then_inc(dve_set, 1)
            dve.wait_ge(pe_set, PE_SET)
            v.tensor_copy(t1T[:, :], ST[0][:, :].bitcast(BF16)[:, 0:HID])
            v.tensor_copy(t2T[:, :, :], ST[0][:, :].bitcast(BF16)[:, 2 * CHUNK:2 * CHUNK + HID].rearrange("p (k c) -> p k c", k=HT))
            v.tensor_copy(rwT[:, :], ST[1][:, 0:NE]).then_inc(dve_set, 1)
            link(v.tensor_copy(bias_gu[:, :], ST[1][:, CHUNK:CHUNK + 2 * NE * FT]))
            v.tensor_scalar(bias_gh[:, :], bias_gu[:, 0:NE * FT], 0.5, None, ALU.mult).then_inc(dve_set, 1)
            dve.wait_ge(dve_set, DVE_SET)
            dve.wait_ge(pool_set, POOL_SET)
            dve.wait_ge(act_set, ACT_SET)

            def layer_norm(b, site, src):
                for t in range(QT):
                    s = v.bn_stats(stats[:, site, t, :], src[:, t, :])
                link(s)
                stand_alone(dve)
                for t in range(QT):
                    s = v.bn_aggr(mv[:, site, t, :], stats[:, site, t, :])
                s.then_inc(mean_ready, 1)
                dve.wait_ge(rstd_ready, 4 * b + site + 1 + BASE)
                for t in range(QT):
                    s = v.tensor_scalar(xn[:, site % 2, t, :], src[:, t, :], mv[:, site, t, 0:1], rstd[:, site, t:t + 1],
                                        ALU.subtract, ALU.mult)
                s.then_inc(xn_ready, 1)

            def maximum(b, job, n):
                k = job.mx0 + n
                dve.wait_ge(mx_full, MAXIMA * b + k + 1 + BASE)
                bank = MX[k % MX_RING]
                if job.cross:
                    ins = v.reduce_max(mx[:, job.number % 2, n:n + 1], bank[:, 0:MXW[n % 4]], AX_X)
                else:
                    t = n % QT
                    keys = (t + 1) * P
                    stand_alone(dve)
                    ins = v.tensor_tensor_reduce(out=mxs[:, 0:keys], in0=bank[:, 0:keys], in1=causal[:, 2 * P - keys:2 * P],
                                                 scale=1.0, scalar=LOWEST, op0=ALU.add, op1=ALU.max,
                                                 accum_out=mx[:, job.number % 2, n:n + 1])
                ins.then_inc(mx_free, 1)
                if not job.cross:
                    dve.wait_ge(mx_free, MAXIMA * b + k + 1 + MX_RING + BASE)

            def negate_maximum(b, job):
                k = job.number % 2
                dve.wait_ge(mx_free, MAXIMA * b + job.mx0 + job.maxima + MX_RING + BASE)
                dve.wait_ge(nparts_ready, NJ * b + max(job.number - 1, 0) + BASE)
                out = nm[:, k, :, :].rearrange("p t h -> p h t")
                if job.cross:
                    v.tensor_reduce(out, mx[:, k, :].rearrange("p (h t c) -> p h t c", h=HQ, t=QT), AX_X, ALU.max,
                                    negate=True).then_inc(nm_ready, 1)
                else:
                    v.tensor_scalar(out, mx[:, k, 0:HQ * QT].rearrange("p (h t) -> p h t", t=QT), -1.0, None,
                                    ALU.mult).then_inc(nm_ready, 1)

            def divide(b, job):
                dve.wait_ge(misc_full, use(b, f"Y{job.number}") + BASE)
                y = MS[:, 0:QT * P].rearrange("p (t j r) -> p t j r", t=QT, j=HQ)
                link(v.reciprocal(rden[:, :, :], y[:, :, :, D]))
                dst = yx[job.layer] if job.cross else ys
                v.tensor_tensor(dst[:, :, job.quad * HQ:(job.quad + 1) * HQ, :], y[:, :, :, 0:D],
                                rden[:, :, :].unsqueeze(3).broadcast_to([P, QT, HQ, D]), ALU.mult).then_inc(misc_free, 1)

            def attention(b, layer):
                jobs = JOBS[layer]
                for job in jobs[0:2]:
                    for n in range(job.maxima):
                        maximum(b, job, n)
                    negate_maximum(b, job)
                for n, job in enumerate(jobs):
                    for t in range(job.tiles):
                        if n + 2 < len(jobs):
                            for m in share(jobs[n + 2], job.tiles, t):
                                maximum(b, jobs[n + 2], m)
                        if t == 1 and n:
                            divide(b, jobs[n - 1])
                    if n + 2 < len(jobs):
                        negate_maximum(b, jobs[n + 2])
                divide(b, jobs[-1])

            def project(b, layer, dst):
                dve.wait_ge(misc_full, use(b, f"proj{layer}") + BASE)
                dve.wait_ge(xb_ready, 2 * b + layer + 1 + BASE)
                v.tensor_tensor(dst[:, :, :], MS[:, 0:T].rearrange("p (t c) -> p t c", t=QT), xb[:, layer, :, :],
                                ALU.add).then_inc(misc_free, 1)
                dve.wait_ge(misc_free, use(b, f"proj{layer}") + BASE)

            def quantise(b, site, xh, q, ready):
                link(v.tensor_reduce(amax[:, site, :], xh, AX_X, ALU.max, apply_absolute_value=True))
                link(v.tensor_scalar(amax[:, site, :], amax[:, site, :], EPS_Q, None, ALU.max))
                link(v.reciprocal(qs[:, site, :], amax[:, site, :]))
                link(v.tensor_scalar(qs[:, site, :], qs[:, site, :], 127.0, None, ALU.mult))
                back = wstat[:, 0:1] if site == 0 else ma2t[:, 0:1]
                v.tensor_scalar(dq[:, site, :], amax[:, site, :], 1.0 / 127.0, back, ALU.mult, ALU.mult)
                for t in range(QT):
                    s = v.tensor_scalar(xh[:, t, :], xh[:, t, :], qs[:, site, t:t + 1], MAGIC, ALU.mult, ALU.add)
                link(s)
                v.tensor_scalar(q, xh, MAGIC, None, ALU.subtract).then_inc(ready, 1)

            def route(b):
                dve.wait_ge(misc_full, use(b, "router") + BASE)
                L = MS[:, 0:QT * NE].rearrange("p (t e) -> p t e", t=QT)

                def wide(ap):
                    return ap.unsqueeze(2).broadcast_to([P, QT, NE])

                index = index_score[:, :].unsqueeze(1).broadcast_to([P, QT, NE])
                link(v.tensor_reduce(r1[:, 0, :], L, AX_X, ALU.max))
                v.tensor_tensor(lg[:, :, :], L, wide(r1[:, 0, :]), ALU.subtract).then_inc(lg_ready, 1)
                dve.wait_ge(e_ready, b + 1 + BASE)
                link(v.tensor_reduce(r1[:, 1, :], lg[:, :, :], AX_X, ALU.add))
                link(v.reciprocal(r1[:, 2, :], r1[:, 1, :]))
                link(v.tensor_tensor(pr[:, :, :], lg[:, :, :], wide(r1[:, 2, :]), ALU.mult))
                src = pr
                for n in range(2):
                    link(v.tensor_reduce(r1[:, 3, :], src[:, :, :], AX_X, ALU.max))
                    link(v.tensor_tensor(pick[:, :, :], src[:, :, :], wide(r1[:, 3, :]), ALU.is_ge))
                    link(v.tensor_tensor(pick[:, :, :], pick[:, :, :], index, ALU.mult))
                    link(v.tensor_reduce(r1[:, 4, :], pick[:, :, :], AX_X, ALU.max))
                    link(v.tensor_tensor(hot[:, n, :, :], pick[:, :, :], wide(r1[:, 4, :]), ALU.is_equal))
                    if n == 0:
                        link(v.scalar_tensor_tensor(out=rest[:, :, :], in0=hot[:, 0, :, :], scalar=-2.0, in1=pr[:, :, :],
                                                    op0=ALU.mult, op1=ALU.add))
                        src = rest
                link(v.tensor_tensor(hot[:, 0, :, :], hot[:, 0, :, :], hot[:, 1, :, :], ALU.add))
                link(v.tensor_tensor(pr[:, :, :], pr[:, :, :], hot[:, 0, :, :], ALU.mult))
                link(v.tensor_reduce(r1[:, 1, :], pr[:, :, :], AX_X, ALU.add))
                link(v.tensor_scalar(r1[:, 1, :], r1[:, 1, :], 1e-9, None, ALU.add))
                link(v.reciprocal(r1[:, 2, :], r1[:, 1, :]))
                v.tensor_tensor(wts[:, :, :], pr[:, :, :], wide(r1[:, 2, :]), ALU.mult).then_inc(misc_free, 1)
                dve.wait_ge(misc_free, use(b, "router") + BASE)

            with dve.Fori(0, NB) as b:
                link.start_turn(b)
                dve.wait_ge(x_in, 16 * b + 16 + BASE)
                layer_norm(b, 0, x0)
                dve.wait_ge(misc_full, use(b, "v0") + BASE)
                for t in range(QT):
                    s = v.tensor_tensor(VS[:, t, :, 0:D], MS[:, t * C:(t + 1) * C].rearrange("p (h d) -> p h d", d=D),
                                        bv0[:, :].rearrange("p (h d) -> p h d", d=D), ALU.add)
                s.then_inc(misc_free, 1)
                attention(b, 0)
                dve.wait_ge(misc_free, use(b, f"Y{JOBS[0][-1].number}") + BASE)
                v.tensor_tensor(yx[0][:, :, :, :], yx[0][:, :, :, :], ys[:, :, :, :], ALU.add).then_inc(y_ready, 1)
                project(b, 0, x1)
                layer_norm(b, 1, x1)
                dve.wait_ge(rms_ready, 2 * b + 1 + BASE)
                for t in range(QT):
                    s = v.scalar_tensor_tensor(out=xh1[:, t, :], in0=xn[:, 1, t, :], scalar=rms[:, 0, t:t + 1],
                                               in1=nw1[:, :], op0=ALU.mult, op1=ALU.mult)
                link(s)
                quantise(b, 0, xh1[:, :, :], a1[:, :, :], a1_ready)
                for t in range(QT):
                    dve.wait_ge(misc_full, use(b, f"hid.{t}") + BASE)
                    v.tensor_scalar(hr[:, t, :], MS[:, :], 0.0, dq[:, 0, t:t + 1], ALU.max, ALU.mult).then_inc(misc_free, 1)
                dve.wait_ge(rms_ready, 2 * b + 2 + BASE)
                for t in range(QT):
                    s = v.scalar_tensor_tensor(out=hr[:, t, :], in0=h2[:, t, :], scalar=rms[:, 1, t:t + 1],
                                               in1=nw2[:, :], op0=ALU.mult, op1=ALU.mult)
                link(s)
                quantise(b, 1, hr[:, :, :], a2[:, :, :], a2_ready)
                dve.wait_ge(misc_full, use(b, "ffn") + BASE)
                for t in range(QT):
                    s = v.scalar_tensor_tensor(out=x2[:, t, :], in0=MS[:, t * C:(t + 1) * C], scalar=dq[:, 1, t:t + 1],
                                               in1=x1[:, t, :], op0=ALU.mult, op1=ALU.add)
                s.then_inc(misc_free, 1)
                dve.wait_ge(misc_free, use(b, "ffn") + BASE)
                layer_norm(b, 2, x2)
                attention(b, 1)
                project(b, 1, x3)
                layer_norm(b, 3, x3)
                route(b)
                for e in range(NE):
                    dve.wait_ge(misc_free, use(b, f"gate{e}") + BASE)
                    link(v.scalar_tensor_tensor(out=tg, in0=tg, scalar=1.0, in1=gb,
                                                op0=ALU.add, op1=ALU.mult))
                    dve.wait_ge(misc_full, use(b, f"up{e}") + BASE)
                    for t in range(FT):
                        n = NE * FT + e * FT + t
                        s = v.scalar_tensor_tensor(out=hh[:, t, :], in0=MS[:, t * T:(t + 1) * T],
                                                   scalar=bias_gu[:, n:n + 1], in1=tg[:, t, :], op0=ALU.add, op1=ALU.mult)
                    s.then_inc(misc_free, 1)
                    dve.wait_ge(misc_full, use(b, f"down{e}") + BASE)
                    src = acc if e else x3
                    for t in range(QT):
                        s = v.scalar_tensor_tensor(out=acc[:, t, :], in0=MS[:, t * C:(t + 1) * C],
                                                   scalar=wts[:, t, e:e + 1], in1=src[:, t, :], op0=ALU.mult, op1=ALU.add)
                    s.then_inc(misc_free, 1)
                    dve.wait_ge(misc_free, use(b, f"down{e}") + BASE)
                dve.wait_ge(misc_full, use(b, "downb") + BASE)
                dve.wait_ge(stored, 16 * b + BASE)
                v.tensor_tensor(acc[:, :, :], MS[:, 0:T].rearrange("p (t c) -> p t c", t=QT), acc[:, :, :],
                                ALU.add).then_inc(misc_free, 1)
                link.end_turn()

        @block.tensor
        def _(pe):
            t_ = nc.tensor
            pe.sem_inc(probs_free, P_RING)
            pe.sem_inc(quad_scored, QUADS)
            pe.wait_ge(loaded, LOADED)
            pe.wait_ge(pool_set, POOL_SET)
            pe.wait_ge(dve_set, 2)
            t_.matmul(MX[0][:, 0:2], ones[:, :], wabs[:, :], start=True, stop=True).then_inc(pe_set, 1)
            pe.wait_ge(dve_set, 4)
            tern = ST[0][:, :].bitcast(BF16)
            for i in range(2):
                for k in range(HT):
                    at = 2 * CHUNK * i + k * P
                    t_.transpose(tern[:, at:at + P], wtern[:, i, k * P:(k + 1) * P], ident_b[:, :])
            t_.transpose(ST[1][:, 0:NE], rw[:, :], ident[0:NE, 0:NE])
            t_.transpose(ST[1][:, CHUNK:CHUNK + 2 * NE * FT], bias_rows[:, :],
                         ident[0:2 * NE * FT, 0:2 * NE * FT]).then_inc(pe_set, 1)
            pe.wait_ge(dve_set, DVE_SET)
            pe.wait_ge(act_set, ACT_SET)

            def open_misc(b, name):
                pe.wait_ge(misc_free, NM * b + MISC[name] + BASE)

            def context(b, layer):
                pe.wait_ge(ctx_in, 32 * (2 * b + layer + 1) + BASE)
                for c in range(len(CHUNKS)):
                    open_misc(b, f"ctxT{layer}.{c}")
                    stand_alone(pe)
                    for t in range(4 * c, min(4 * c + 4, KT)):
                        n = P if t < FULL else TAIL
                        last = t_.transpose(MS[0:CC, (t % 4) * P:(t % 4) * P + n], ctx[0:n, t * CC:(t + 1) * CC], ident[0:n, 0:n])
                    last.then_inc(misc_full, 1)
                for c, (at, n) in enumerate(CHUNKS):
                    open_misc(b, f"key{layer}.{c}")
                    t_.matmul(MS[:, 0:n], wck[layer][:, :], ctxT[:, at:at + n], start=True, stop=True).then_inc(misc_full, 1)
                for c in range(len(CHUNKS)):
                    open_misc(b, f"val{layer}.{c}")
                    for t in range(4 * c, min(4 * c + 4, KT)):
                        n = P if t < FULL else TAIL
                        last = t_.matmul(MS[0:n, (t % 4) * C:(t % 4 + 1) * C], ctxT[:, t * P:t * P + n], wcv[layer][:, :],
                                         start=True, stop=True)
                    last.then_inc(misc_full, 1)

            def turn_tokens(b, name, src):
                for t in range(QT):
                    last = t_.transpose(MS[:, t * P:(t + 1) * P], src[:, t, :], ident[:, :])
                last.then_inc(misc_full, 1)

            def by_channel(b, name, weight, site):
                open_misc(b, name)
                t_.matmul(MS[:, 0:T], weight[:, :], xnT[:, site, :], start=True, stop=True).then_inc(misc_full, 1)

            def maximum(b, job, n):
                k = job.mx0 + n
                if n == 0:
                    if job.cross:
                        pe.wait_ge(kx_in[job.quad], SENT * (2 * b + job.layer + 1) + BASE)
                        pe.wait_ge(q_in[3 if job.layer else 0], SENT * b + SENT + BASE)
                    elif job.quad == 0:
                        pe.wait_ge(q_in[1], SENT * b + SENT + BASE)
                        pe.wait_ge(q_in[2], SENT * b + SENT + BASE)
                pe.wait_ge(mx_free, MAXIMA * b + k + 1 + BASE)
                if job.cross:
                    j, t, c = n // (QT * 4), n // 4 % QT, n % 4
                    h, keys, at, q = job.quad * HQ + j, MXW[c], MX0[c], QX[job.layer]
                    rhs = KX[0:TERMS, h, at:at + keys]
                else:
                    j, t = n // QT, n % QT
                    h, keys, q = job.quad * HQ + j, (t + 1) * P, QS
                    rhs = KS[0:TERMS, h, 0:keys]
                t_.matmul(MX[k % MX_RING][:, 0:keys], q[0:TERMS, h, t * P:(t + 1) * P], rhs, start=True,
                          stop=True).then_inc(mx_full, 1)

            def turn_maximum(b, job):
                pe.wait_ge(nparts_ready, NJ * b + job.number + 1 + BASE)
                open_misc(b, f"nT{job.number}")
                for t in range(QT):
                    last = t_.transpose(MSB[0:PARTS * HQ, t * P:(t + 1) * P],
                                        npart[:, job.number % 2, t, :, :].rearrange("p r h -> p (r h)"), ident_b[:, :])
                last.then_inc(misc_full, 1)

            def score(b, job, t):
                k = job.tile0 + t
                if t == 0:
                    pe.wait_ge(max_in[job.number % 2], 16 * (NJ // 2 * b + job.number // 2 + 1) + BASE)
                pe.wait_ge(exp_done, TILES * b + k + 1 + BASE)
                for j in range(HQ):
                    h = job.quad * HQ + j
                    if job.cross:
                        n, lo, q, keys = (P if t < FULL else TAIL), 0, QX[job.layer], KX
                    else:
                        n, lo, q, keys = P, t * P, QS, KS
                    last = t_.matmul(ST[k % ST_RING][0:n, j * (T - lo):(j + 1) * (T - lo)], keys[:, h, t * P:t * P + n],
                                     q[:, h, lo:T], start=True, stop=True)
                last.then_inc(st_full, 1)

            def values(b, job, t):
                k = job.tile0 + t
                if t == 0:
                    pe.wait_ge(yt_ready, NJ * b + job.number + BASE)
                if job.cross:
                    pe.wait_ge(exp_done, TILES * b + k + 1 + ST_RING + BASE)
                else:
                    pe.wait_ge(masked, QUADS * QT * b + job.quad * QT + t + 1 + BASE)
                n = TAIL if job.cross and t == FULL else P
                lo = 0 if job.cross else t * P
                vals = VX[job.layer] if job.cross else VS
                for j in range(HQ):
                    h = job.quad * HQ + j
                    last = t_.matmul(PV[32 * j:32 * j + D + 1, lo:T], vals[0:n, t, h, :],
                                     probs[0:n, k % P_RING, j * (T - lo):(j + 1) * (T - lo)],
                                     start=(t == 0), stop=(t == job.tiles - 1))
                    if t == job.tiles - 1 and j == 0:
                        last.then_inc(quad_scored if job.cross else self_scored, 1)
                last.then_inc(probs_free, 1)

            def turn_values(b, job):
                open_misc(b, f"Y{job.number}")
                pe.wait_ge(yt_ready, NJ * b + job.number + 1 + BASE)
                for t in range(QT):
                    last = t_.transpose(MS[:, t * P:(t + 1) * P], yt[:, job.number % 2, t * P:(t + 1) * P], ident[:, :])
                last.then_inc(misc_full, 1)

            def attention(b, layer):
                jobs = JOBS[layer]
                for job in jobs[0:2]:
                    for n in range(job.maxima):
                        maximum(b, job, n)
                turn_maximum(b, jobs[0])
                before = None
                for n, job in enumerate(jobs):
                    for t in range(job.tiles):
                        score(b, job, t)
                        if before is not None:
                            values(b, *before)
                        before = (job, t)
                        if n + 2 < len(jobs):
                            for m in share(jobs[n + 2], job.tiles, t):
                                maximum(b, jobs[n + 2], m)
                        if t == 1 and n:
                            turn_values(b, jobs[n - 1])
                        if t == min(4, job.tiles - 1) and n + 1 < len(jobs):
                            turn_maximum(b, jobs[n + 1])
                values(b, *before)
                turn_values(b, jobs[-1])
                open_misc(b, f"yT{layer}")
                if layer == 0:
                    pe.wait_ge(y_ready, b + 1 + BASE)
                turn_tokens(b, f"yT{layer}", yx[layer][:, :, :, :].rearrange("p t h d -> p t (h d)"))
                open_misc(b, f"proj{layer}")
                for t in range(QT):
                    last = t_.matmul(MS[:, t * C:(t + 1) * C], yT[:, t * P:(t + 1) * P], (wo1 if layer else wp0)[:, :],
                                     start=True, stop=True)
                last.then_inc(misc_full, 1)

            with pe.Fori(0, NB) as b:
                context(b, 0)
                open_misc(b, "xT0")
                pe.wait_ge(xn_ready, 4 * b + 1 + BASE)
                turn_tokens(b, "xT0", xn[:, 0, :, :])
                by_channel(b, "qc0", wcq0, 0)
                by_channel(b, "q0", wq0, 0)
                by_channel(b, "k0", wk0, 0)
                open_misc(b, "v0")
                for t in range(QT):
                    last = t_.matmul(MS[:, t * C:(t + 1) * C], xnT[:, 0, t * P:(t + 1) * P], wv0[:, :], start=True, stop=True)
                last.then_inc(misc_full, 1)
                attention(b, 0)
                open_misc(b, "a1T")
                pe.wait_ge(a1_ready, b + 1 + BASE)
                for t in range(QT):
                    last = t_.transpose(MSB[:, t * P:(t + 1) * P], a1[:, t, :], ident_b[:, :])
                last.then_inc(misc_full, 1)
                for t in range(QT):
                    open_misc(b, f"hid.{t}")
                    t_.matmul(MS[:, :], a1T[:, t * P:(t + 1) * P], t1T[:, :], start=True, stop=True).then_inc(misc_full, 1)
                for t in range(QT):
                    open_misc(b, f"a2T.{t}")
                    pe.wait_ge(a2_ready, b + 1 + BASE)
                    for k in range(HT):
                        last = t_.transpose(MSB[:, k * P:(k + 1) * P], a2[:, t, k * P:(k + 1) * P], ident_b[:, :])
                    last.then_inc(misc_full, 1)
                open_misc(b, "ffn")
                for t in range(QT):
                    for k in range(HT):
                        last = t_.matmul(MS[:, t * C:(t + 1) * C], a2T[:, t, k, :], t2T[:, k, :], start=(k == 0),
                                         stop=(k == HT - 1))
                last.then_inc(misc_full, 1)
                context(b, 1)
                open_misc(b, "xT1")
                pe.wait_ge(xn_ready, 4 * b + 3 + BASE)
                turn_tokens(b, "xT1", xn[:, 0, :, :])
                by_channel(b, "qc1", wq1, 1)
                attention(b, 1)
                open_misc(b, "xT2")
                pe.wait_ge(xn_ready, 4 * b + 4 + BASE)
                turn_tokens(b, "xT2", xn[:, 1, :, :])
                open_misc(b, "router")
                for t in range(QT):
                    last = t_.matmul(MS[:, t * NE:(t + 1) * NE], xnT[:, 2, t * P:(t + 1) * P], rwT[:, :], start=True, stop=True)
                last.then_inc(misc_full, 1)
                open_misc(b, "prT")
                for t in range(QT):
                    last = t_.transpose(MS[0:NE, t * P:(t + 1) * P], wts[:, t, :], ident[:, :])
                last.then_inc(misc_full, 1)
                for e in range(NE):
                    for name, weight in (("gate", gate), ("up", up)):
                        open_misc(b, f"{name}{e}")
                        for t in range(FT):
                            last = t_.matmul(MS[:, t * T:(t + 1) * T], weight[:, e, t * P:(t + 1) * P], xnT[:, 2, :],
                                             start=True, stop=True)
                        last.then_inc(misc_full, 1)
                    open_misc(b, f"down{e}")
                    for t in range(QT):
                        for f in range(FT):
                            last = t_.matmul(MS[:, t * C:(t + 1) * C], hh[:, f, t * P:(t + 1) * P],
                                             down[:, e * FT + f, :], start=(f == 0), stop=(f == FT - 1))
                    last.then_inc(misc_full, 1)
                open_misc(b, "downb")
                for t in range(QT):
                    last = t_.matmul(MS[:, t * C:(t + 1) * C], prT[:, t * P:(t + 1) * P], down_b[:, :], start=True, stop=True)
                last.then_inc(misc_full, 1)


_INS = ["x", "ctx_512", "g_xattn", "g_ffn",
        "L0_xattn_Wk", "L0_xattn_bk", "L0_xattn_Wq", "L0_xattn_bq", "L0_xattn_Wv", "L0_xattn_bv",
        "L0_xattn_Wck", "L0_xattn_bck", "L0_xattn_Wcq", "L0_xattn_bcq", "L0_xattn_Wcv", "L0_xattn_bcv",
        "L0_xattn_Wp", "L0_xattn_bp", "L0_ffn_norm1_w", "L0_ffn_w1", "L0_ffn_act_scale", "L0_ffn_act_bias",
        "L0_ffn_norm2_w", "L0_ffn_w2", "L1_xattn_Wq", "L1_xattn_bq", "L1_xattn_Wk", "L1_xattn_bk",
        "L1_xattn_Wv", "L1_xattn_bv", "L1_xattn_Wo", "L1_xattn_bo", "L1_ffn_router_w", "L1_ffn_gate_w",
        "L1_ffn_gate_b", "L1_ffn_up_w", "L1_ffn_up_b", "L1_ffn_down_w", "L1_ffn_down_b"]


def kernel(**inputs):
    import numpy as _np
    import concourse.bacc as _bacc
    from concourse import mybir as _mybir
    from concourse.bass_utils import run_bass_kernel_spmd as _run

    nc = _bacc.Bacc("TRN2", target_bir_lowering=False, num_devices=1)
    arrays, args = {}, {}
    for name in _INS:
        a = _np.ascontiguousarray(inputs[name])
        arrays[f"in_{name}"] = a
        args[name] = nc.dram_tensor(f"in_{name}", a.shape, _mybir.dt.from_np(a.dtype), kind="ExternalInput").ap()
    out = nc.dram_tensor("out_x", arrays["in_x"].shape, _mybir.dt.float32, kind="ExternalOutput").ap()
    x_d, ctx_d = args.pop("x"), args.pop("ctx_512")
    flamingo_gated_blocks(nc, args, x_d, ctx_d, out)
    r = _run(nc, [arrays], core_ids=[0])
    return r.results[0]["out_x"]
```

```python
from contextlib import ExitStack

import numpy as np

import concourse.bass as bass
from concourse import mybir

F32 = mybir.dt.float32
BF16 = mybir.dt.bfloat16
ALU = mybir.AluOpType
ACT = mybir.ActivationFunctionType
AX_X = mybir.AxisListType.X

P = 128
NB = 16
T = 256
QT = T // P
C = 128
H = 16
D = C // H
NK = 1601
CC = 64
KT = 13
FULL = KT - 1
TAIL = NK - FULL * P
HID = 512
HT = HID // P
NE = 8
FF = 256
FT = FF // P
QUADS = 4
HQ = H // QUADS
PARTS = 3
TERMS = PARTS * PARTS * D
FILL = 96
ROWS = FILL + PARTS
SCALE = float(np.float32(1.0 / np.sqrt(D)))
MASKED = -1e30
LOWEST = -3e38
MAGIC = 12582912.0
EPS_LN, EPS_NORM, EPS_Q = 1e-5, 1e-8, 1e-5
CHUNK = 512
CHUNKS = [(c * CHUNK, min(CHUNK, NK - c * CHUNK)) for c in range(4)]
MXW = [401, 401, 401, 398]
MX0 = [0, 401, 802, 1203]
P_RING, ST_RING, MX_RING = 2, 2, 2
BASE = 1


class Job:

    def __init__(self, cross, layer, quad, number, tile0, mx0):
        self.cross, self.layer, self.quad, self.number = cross, layer, quad, number
        self.tiles = KT if cross else QT
        self.maxima = HQ * QT * (4 if cross else 1)
        self.tile0, self.mx0 = tile0, mx0


def plan():
    jobs = [[], []]
    for layer in range(2):
        tile = mx = 0
        for quad in range(QUADS):
            for cross in ((True, False) if layer == 0 else (True,)):
                j = Job(cross, layer, quad, len(jobs[layer]), tile, mx)
                jobs[layer].append(j)
                tile, mx = tile + j.tiles, mx + j.maxima
    return jobs


JOBS = plan()
SLOTS = [sum(j.tiles for j in jobs) for jobs in JOBS]
MAXIMA = [sum(j.maxima for j in jobs) for jobs in JOBS]
NJ = [len(jobs) for jobs in JOBS]
assert not any(n % 2 for n in SLOTS + MAXIMA + NJ)
LEAD = 9
TURN_AT = 6
LOOP = (2, NB - 1)
FIRST, LAST = -1, NB + 1


def maximum_steps():
    at = [[[] for _ in range(n)] for n in SLOTS]
    turn = sum(SLOTS)
    order, deadline = [], None
    jobs = JOBS[0] + JOBS[1]
    last = jobs[-1]
    before = SLOTS[0] + last.tile0 - LEAD - turn
    for job in jobs:
        order += [(job, n) for n in range(job.maxima)]
        if job.cross:
            deadline = SLOTS[0] * job.layer + job.tile0 - LEAD
            for n, step in enumerate(order):
                slot = (before + 1 + n * (deadline - before) // len(order)) % turn
                at[slot >= SLOTS[0]][slot - SLOTS[0] * (slot >= SLOTS[0])].append(step)
            order, before = [], deadline
    assert not order
    return at


MAXIMUM_AT = maximum_steps()

BESIDE = [{
    0: ["ctxT1.0", "ln2a"], 1: ["Y1.3"], 2: ["ctxT1.1", "ln2b"], 3: ["yT1"], 4: ["proj1"], 5: ["ctxT1.2", "ln3a"],
    6: ["ctxT1.3"], 8: ["xT1", "ln3b"], 10: ["qc1"], 11: ["xT2"], 12: ["router"], 13: ["val1.0"], 15: ["key1.0"],
    16: ["route1"], 17: ["val1.1"], 18: ["key1.1"], 19: ["val1.2", "route2"], 20: ["val1.3"], 21: ["key1.2"],
    22: ["route3"], 25: ["key1.3"], 26: ["prT"], 59: ["downb"]}, {
    0: ["ctxT0.0", "ln0a"], 1: ["Y0.7"], 2: ["ctxT0.1", "ln0b"], 3: ["yT0"], 4: ["proj0"], 5: ["ctxT0.2", "ln1a"],
    6: ["ctxT0.3", "xb0"], 8: ["key0.0", "ln1b"], 9: ["xT0"], 10: ["qc0"], 11: ["key0.1"], 12: ["q0", "quant0"], 13: ["k0"],
    15: ["key0.2"], 16: ["v0"], 17: ["a1T"], 18: ["key0.3"], 19: ["hid.0"], 21: ["hid.1"], 22: ["val0.0"],
    23: ["val0.1"], 24: ["val0.2"], 25: ["val0.3"], 29: ["quant1"], 34: ["a2T.0"], 35: ["a2T.1"], 36: ["ffn"]}]
for n, slot in enumerate((27, 28, 30, 32, 33, 34, 35, 36, 38, 40, 41, 42, 43, 45, 47, 48, 49, 50, 51, 53, 55, 56, 57, 58)):
    BESIDE[0].setdefault(slot, []).append(f"{('gate', 'up', 'down')[n % 3]}{n // 3}")
for _layer in range(2):
    for _job in JOBS[_layer]:
        if _job.number:
            BESIDE[_layer].setdefault(_job.tile0 + 1, []).insert(0, f"Y{_layer}.{_job.number - 1}")
        _slot, _phase = _job.tile0 - TURN_AT, _layer
        if _slot < 0:
            _phase = 1 - _layer
            _slot += SLOTS[_phase]
        BESIDE[_phase].setdefault(_slot, []).insert(0, f"nT{_layer}.{_job.number}")

SEND_AT = [{
    0: [], 1: ["keys0.3"], 7: ["ctx0", "x"], 12: ["q3"], 27: ["keys1"], 29: ["keys1.0"], 30: ["keys1.1"], 45: ["keys1.2"],
    59: ["keys1.3", "out"]}, {
    8: ["ctx1"], 12: ["q0"], 14: ["q1"], 16: ["q2"], 20: ["keys0"], 21: ["keys0.0"], 28: ["keys0.1"], 41: ["keys0.2"]}]
for _phase in range(2):
    for _s, _names in BESIDE[_phase].items():
        for _n in _names:
            if _n[0:2] == "nT":
                SEND_AT[_phase].setdefault(_s + 1, []).insert(0, "max_out" + _n[2:])
                SEND_AT[_phase].setdefault(_s + 2, []).insert(0, "max_in" + _n[2:])

OUT_NAMES = ("Y1.3", "yT1", "proj1", "ln3a", "ln3b", "xT2", "router", "route1", "route2", "route3", "prT", "downb", "out")
PRE1_NAMES = ("ln2a", "ln2b", "xT1", "qc1", "q3")
FFN_NAMES = ("Y0.7", "yT0", "proj0", "ln1a", "ln1b", "quant0", "quant1", "a1T", "hid.0", "hid.1", "a2T.0", "a2T.1", "ffn",
             "ctx1")
PRE0_NAMES = ("ln0a", "ln0b", "xT0", "qc0", "q0", "k0", "v0", "q1", "q2", "xb0", "ctx0", "x")


class Turn:

    def __init__(self, i, origin=0, uses_before=0):
        self.i, self.origin = i, origin
        self.looped = origin != 0
        n = LOOP[0] if self.looped else i
        self.number = n
        self.attention0 = 0 <= n < NB
        self.attention1 = 1 <= n <= NB
        self.experts = 2 <= n <= NB + 1
        self.next0 = n + 1 < NB
        self.names = [name for phase in range(2) for s in range(SLOTS[phase]) for name in self.beside(phase, s)
                      if self.in_bank(name)]
        self.uses_before, self.position = uses_before, {name: n for n, name in enumerate(self.names)}

    def value(self, scale, plus):
        if not self.looped:
            return scale * self.i + plus
        return scale * self.i + (scale * self.origin + plus)

    def done(self, off, scale=1, plus=0):
        if self.looped:
            return self.value(scale, scale * (off + 1) + plus)
        return scale * min(max(self.i + off + 1, 0), NB) + plus

    @staticmethod
    def in_bank(name):
        return name[0:2] not in ("ln", "xb") and name[0:5] not in ("route", "quant") or name == "router"

    def runs(self, name, phase):
        if name in OUT_NAMES or name[0:2] in ("ga", "up") or name[0:4] == "down":
            return self.experts
        if name in PRE1_NAMES:
            return self.attention1
        if name in FFN_NAMES:
            return self.attention0
        if name in PRE0_NAMES:
            return self.next0
        if name == "keys0.3":
            return self.attention0
        for start in ("ctxT", "keys", "key", "val"):
            if name[0:len(start)] == start:
                return self.attention1 if name[len(start)] == "1" else self.next0
        layer = int(name[-3])
        if name[0] == "Y" or layer == 1:
            return (self.attention0, self.attention1)[layer]
        return self.next0 if phase == 1 else self.attention0

    def beside(self, phase, slot):
        return [name for name in BESIDE[phase].get(slot, []) if self.runs(name, phase)]

    def sends(self, phase, slot):
        return [name for name in SEND_AT[phase].get(slot, []) if self.runs(name, phase)]

    def attends(self, phase):
        return (self.attention0, self.attention1)[phase]

    def at(self, phase, layer):
        return -1 if layer else phase

    def before(self, phase, layer, n0, n1, plus=0):
        off = self.at(phase, layer)
        if self.looped:
            l0, l1 = (1, -1) if layer else (off, off - 1)
            return self.value(n0 + n1, l0 * n0 + l1 * n1 + plus)
        b = self.i + off
        l0, l1 = (min(b + 2, NB), b) if layer else (b, max(b - 1, 0))
        return n0 * l0 + n1 * l1 + plus

    def use(self, name):
        return self.bank(self.position[name] + 1)

    def bank(self, plus=0):
        if not self.looped:
            return self.uses_before + plus + BASE
        return len(self.names) * self.i + (self.uses_before + plus + BASE)

    def maxima(self, phase, slot):
        return [(job, n) for job, n in MAXIMUM_AT[phase][slot]
                if (self.attention1 if job.layer else self.next0 if phase == 1 else self.attention0)]

    def job_before(self, phase, slot):
        for job in JOBS[phase]:
            if job.tile0 == slot and job.number and self.attends(phase):
                return JOBS[phase][job.number - 1]
        if slot == 0 and (self.attention0 if phase else self.experts):
            return JOBS[1 - phase][-1]
        return None


def count_done(t, phase, job, n0, n1, plus=0):
    if job.layer == phase:
        return t.before(phase, job.layer, n0, n1, plus)
    if phase == 1:
        return t.before(0, 0, n0, n1, plus)
    if t.looped:
        return t.value(n0 + n1, -2 * n1 + plus)
    b = t.i - 2
    return n0 * min(b + 2, NB) + n1 * b + plus


DVE_STEPS, ACT_STEPS, POOL_STEPS = 56, 0, 66


class Link:

    def __init__(self, eng, sem, per_turn, then=None):
        self.eng, self.sem, self.per_turn, self.base, self.n, self.turn = eng, sem, per_turn, 0, 0, None
        self.then = then

    def start_turn(self, turn):
        self.turn, self.base, self.n = turn, self.base + self.n, 0

    def __call__(self, ins):
        self.n += 1
        ins.then_inc(self.sem, 1)
        v = self.base + self.n
        looped = self.turn is not None and self.turn.looped
        self.eng.wait_ge(self.sem, self.turn.i * self.per_turn + v if looped else v)
        if self.then and looped:
            self.then()

    def end_turn(self):
        if self.turn.looped:
            assert self.n == self.per_turn, ("linked steps", self.sem, self.n, self.per_turn)
            self.n *= LOOP[1] - LOOP[0]


def run_turns(eng, turn, link=None):
    uses = 0

    def one(t):
        if link:
            link.start_turn(t)
        turn(t)
        if link:
            link.end_turn()

    for i in range(FIRST, LOOP[0]):
        t = Turn(i, uses_before=uses)
        one(t)
        uses += len(t.names)
    with eng.Fori(0, LOOP[1] - LOOP[0]) as i:
        t = Turn(i, origin=LOOP[0], uses_before=uses)
        one(t)
    uses += len(t.names) * (LOOP[1] - LOOP[0])
    for i in range(LOOP[1], LAST + 1):
        t = Turn(i, uses_before=uses)
        one(t)
        uses += len(t.names)


def flamingo_gated_blocks(nc, w, x_d, ctx_d, out_d):
    x_v = x_d.rearrange("b (t p) c -> b p t c", p=P)
    out_v = out_d.rearrange("b (t p) c -> b p t c", p=P)
    ctx_main = ctx_d[:, 0:FULL * P, :].rearrange("b (p t) c -> b p (t c)", t=FULL)
    ctx_tail = ctx_d[:, FULL * P:NK, :]

    with ExitStack() as stack:
        def sb(name, shape, dt=F32):
            return stack.enter_context(nc.sbuf_tensor(name, shape, dt))

        def sem(name):
            return stack.enter_context(nc.semaphore(name))

        ident = sb("ident", [P, P])
        ident_b = sb("ident_b", [P, P], BF16)
        causal = sb("causal", [P, 2 * P])
        minus_half = sb("minus_half", [P, 4])
        index_score = sb("index_score", [P, NE])
        gx = sb("gx", [P, 2])
        gf = sb("gf", [P, 2])
        tx = sb("tx", [P, 2])
        tf = sb("tf", [P, 2])
        tf_half = sb("tf_half", [P, 1])
        wq0, wk0, wv0, wcq0, wp0 = (sb(n, [P, C]) for n in ("wq0", "wk0", "wv0", "wcq0", "wp0"))
        wq1, wo1 = (sb(n, [P, C]) for n in ("wq1", "wo1"))
        wck = [sb(f"wck{i}", [CC + 1, C]) for i in range(2)]
        wcv = [sb(f"wcv{i}", [CC + 1, C]) for i in range(2)]
        bias_col = sb("bias_col", [P, 4])
        bv0 = sb("bv0", [P, C])
        bp = [sb(f"bp{i}", [P, C]) for i in range(2)]
        nw1 = sb("nw1", [P, C])
        nw2 = sb("nw2", [P, HID])
        act_s = sb("act_s", [P, 1])
        act_b = sb("act_b", [P, 1])
        wide_a = sb("wide_a", [P, 2, HID])
        wide_b = sb("wide_b", [P, 2, HID])
        ones = wide_b[:, 0, 0:P]
        wraw = wide_a
        wabs = sb("wabs", [P, 2])
        wstat = sb("wstat", [P, 4])
        a2 = sb("a2", [P, QT, HID], BF16)
        wtern = a2
        t1T = sb("t1T", [P, HID], BF16)
        t2T = sb("t2T", [P, HT, C], BF16)
        ma2t = sb("ma2t", [P, 1])
        rw = sb("rw", [NE, C])
        rwT = sb("rwT", [P, NE])
        gate = sb("gate", [P, NE, FF])
        up = sb("up", [P, NE, FF])
        down = sb("down", [P, NE * FT, C])
        bias_rows = sb("bias_rows", [2 * NE * FT, P])
        bias_gu = sb("bias_gu", [P, 2 * NE * FT])
        bias_gh = sb("bias_gh", [P, NE * FT])
        down_b = sb("down_b", [NE, C])

        ctx = sb("ctx", [P, KT * CC])
        ctxT = sb("ctxT", [CC + 1, NK])
        kf = sb("kf", [P, CHUNK])
        kres = sb("kres", [P, CHUNK])
        kpart = [sb(f"kpart{i}", [P, NK], BF16) for i in range(PARTS)]
        KX = sb("KX", [ROWS, H, NK], BF16)
        VX = [sb(f"VX{i}", [P, KT, H, D + 1]) for i in range(2)]
        KS = sb("KS", [ROWS, H, T], BF16)
        VS = sb("VS", [P, QT, H, D + 1])
        QX = [sb(f"QX{i}", [ROWS, H, T], BF16) for i in range(2)]
        QS = sb("QS", [ROWS, H, T], BF16)
        qf = sb("qf", [P, 2, T])
        qres = sb("qres", [P, T])
        qpart = sb("qpart", [P, 3, PARTS, T], BF16)
        x0 = sb("x0", [P, QT, C])
        x1 = sb("x1", [P, QT, C])
        x2 = sb("x2", [P, QT, C])
        x3 = x1
        xb = sb("xb", [P, 2, QT, C])
        stats = sb("stats", [P, 4, QT, 6])
        mv = sb("mv", [P, 4, QT, 2])
        rstd = sb("rstd", [P, 4, QT])
        xn = sb("xn", [P, 2, QT, C])
        xnT = sb("xnT", [P, 3, T])
        probs = sb("probs", [P, P_RING, HQ * T])
        mx = sb("mx", [P, 2, HQ * QT * 4])
        mxs = sb("mxs", [P, T], BF16)
        nm = sb("nm", [P, 2, QT, HQ])
        nres = sb("nres", [P, 2, QT, HQ])
        npart = sb("npart", [P, 2, QT, PARTS, HQ], BF16)
        nT = sb("nT", [PARTS * HQ, 2, T], BF16)
        yt = sb("yt", [P, 2, T])
        rden = sb("rden", [P, QT, HQ])
        yx = [sb(f"yx{i}", [P, QT, H, D]) for i in range(2)]
        ys = sb("ys", [P, QT, H, D])
        yT = sb("yT", [P, T])
        ssq = sb("ssq", [P, 2, QT])
        rms = sb("rms", [P, 2, QT])
        amax = sb("amax", [P, 2, QT])
        qs = sb("qs", [P, 2, QT])
        dq = sb("dq", [P, 2, QT])
        xh1 = sb("xh1", [P, QT, C])
        a1 = sb("a1", [P, QT, C], BF16)
        a1T = sb("a1T", [P, T], BF16)
        hr, h2 = wide_a, wide_b
        a2T = wide_b[:, 1, :].bitcast(BF16).rearrange("p (t k q) -> p t k q", t=QT, k=HT)
        lg = sb("lg", [P, QT, NE])
        pr = sb("pr", [P, QT, NE])
        pick = sb("pick", [P, QT, NE])
        hot = sb("hot", [P, 2, QT, NE])
        rest = sb("rest", [P, QT, NE])
        wts = sb("wts", [P, QT, NE])
        r1 = sb("r1", [P, 6, QT])
        prT = wide_b[0:NE, 1, 0:T]
        tg, gb, hh = (ap.rearrange("p (t n) -> p t n", t=FT) for ap in (wide_a[:, 0, :], wide_a[:, 1, :], wide_b[:, 0, :]))
        acc = sb("acc", [P, QT, C])

        ST = [stack.enter_context(nc.psum_tensor(f"ST{i}", [P, 2 * CHUNK], F32)) for i in range(ST_RING)]
        MX = [stack.enter_context(nc.psum_tensor(f"MX{i}", [P, CHUNK], F32)) for i in range(MX_RING)]
        PV = stack.enter_context(nc.psum_tensor("PV", [P, CHUNK], F32))
        MS = stack.enter_context(nc.psum_tensor("MS", [P, CHUNK], F32))
        MSB = MS[:, :].bitcast(BF16)

        loaded = sem("loaded")
        pool_set, dve_set, act_set, pe_set = sem("pool_set"), sem("dve_set"), sem("act_set"), sem("pe_set")
        dve_step, act_step, pool_step = sem("dve_step"), sem("act_step"), sem("pool_step")
        passed = sem("passed")
        misc_full = sem("misc_full")
        misc_free = sem("misc_free")
        ctx_in, x_in, stored = sem("ctx_in"), sem("x_in"), sem("stored")
        kparts_ready = sem("kparts_ready")
        kx_in = [sem(f"kx_in{g}") for g in range(QUADS)]
        q_in = [sem(f"q_in{i}") for i in range(4)]
        qparts_ready = [sem(f"qparts_ready{i}") for i in range(4)]
        quad_scored = sem("quad_scored")
        self_scored = sem("self_scored")
        mean_ready, rstd_ready, xn_ready = ([sem(f"{n}{i}") for i in range(4)] for n in ("mean_ready", "rstd_ready", "xn_ready"))
        mx_full, mx_free = sem("mx_full"), sem("mx_free")
        nm_ready, nparts_ready = sem("nm_ready"), sem("nparts_ready")
        max_in = [sem(f"max_in{i}") for i in range(2)]
        st_full, exp_done, masked, probs_free = sem("st_full"), sem("exp_done"), sem("masked"), sem("probs_free")
        yt_ready, y_ready = sem("yt_ready"), sem("y_ready")
        xb_ready = [sem(f"xb_ready{i}") for i in range(2)]
        ssq_ready, rms_ready = ([sem(f"{n}{i}") for i in range(2)] for n in ("ssq_ready", "rms_ready"))
        a1_ready, a2_ready, sq_ready, h2_ready = sem("a1_ready"), sem("a2_ready"), sem("sq_ready"), sem("h2_ready")
        e_ready, wts_ready = sem("e_ready"), sem("wts_ready")

        counted = [misc_full, misc_free, ctx_in, x_in, stored, kparts_ready, *kx_in, *q_in, *qparts_ready, quad_scored,
                   self_scored, *mean_ready, *rstd_ready, *xn_ready, mx_full, mx_free, nm_ready, nparts_ready, *max_in,
                   st_full, exp_done, masked, probs_free, yt_ready, y_ready, *xb_ready, *ssq_ready, *rms_ready, a1_ready,
                   a2_ready, sq_ready, h2_ready, e_ready, wts_ready]
        key_rows = nc.dram_tensor("key_rows", [2, PARTS, P, NK], BF16, kind="Internal").ap()
        query_rows = nc.dram_tensor("query_rows", [4, PARTS, P, T], BF16, kind="Internal").ap()
        max_rows = nc.dram_tensor("max_rows", [2, PARTS * HQ, T], BF16, kind="Internal").ap()
        key_out, max_out = sem("key_out"), [sem(f"max_out{i}") for i in range(2)]
        q_out = [sem(f"q_out{i}") for i in range(4)]

        counted += [key_out, *max_out, *q_out]
        block = stack.enter_context(nc.Block())

        def stand_alone(eng):
            eng.sem_inc(passed, 1)

        loads = [
            (gx[:, :], w["g_xattn"].partition_broadcast(P)), (gf[:, :], w["g_ffn"].partition_broadcast(P)),
            (wq0[:, :], w["L0_xattn_Wq"]), (wk0[:, :], w["L0_xattn_Wk"]), (wv0[:, :], w["L0_xattn_Wv"]),
            (wcq0[:, :], w["L0_xattn_Wcq"]), (wp0[:, :], w["L0_xattn_Wp"]),
            (wq1[:, :], w["L1_xattn_Wq"]), (wo1[:, :], w["L1_xattn_Wo"]),
            (wck[0][0:CC, :], w["L0_xattn_Wck"]), (wck[0][CC:CC + 1, :], w["L0_xattn_bck"].unsqueeze(0)),
            (wcv[0][0:CC, :], w["L0_xattn_Wcv"]), (wcv[0][CC:CC + 1, :], w["L0_xattn_bcv"].unsqueeze(0)),
            (wck[1][0:CC, :], w["L1_xattn_Wk"]), (wck[1][CC:CC + 1, :], w["L1_xattn_bk"].unsqueeze(0)),
            (wcv[1][0:CC, :], w["L1_xattn_Wv"]), (wcv[1][CC:CC + 1, :], w["L1_xattn_bv"].unsqueeze(0)),
            (bias_col[:, 0:1], w["L0_xattn_bcq"].unsqueeze(1)), (bias_col[:, 1:2], w["L0_xattn_bq"].unsqueeze(1)),
            (bias_col[:, 2:3], w["L0_xattn_bk"].unsqueeze(1)), (bias_col[:, 3:4], w["L1_xattn_bq"].unsqueeze(1)),
            (bv0[:, :], w["L0_xattn_bv"].partition_broadcast(P)),
            (bp[0][:, :], w["L0_xattn_bp"].partition_broadcast(P)), (bp[1][:, :], w["L1_xattn_bo"].partition_broadcast(P)),
            (nw1[:, :], w["L0_ffn_norm1_w"].partition_broadcast(P)), (nw2[:, :], w["L0_ffn_norm2_w"].partition_broadcast(P)),
            (act_s[:, :], w["L0_ffn_act_scale"].partition_broadcast(P)), (act_b[:, :], w["L0_ffn_act_bias"].partition_broadcast(P)),
            (wraw[:, 0, :].rearrange("p (t d) -> p t d", t=HT), w["L0_ffn_w1"].rearrange("(t p) d -> p t d", p=P)),
            (wraw[:, 1, :], w["L0_ffn_w2"]),
            (rw[:, :], w["L1_ffn_router_w"]),
            (gate[:, :, :], w["L1_ffn_gate_w"].rearrange("e d f -> d e f")),
            (up[:, :, :], w["L1_ffn_up_w"].rearrange("e d f -> d e f")),
            (down[:, :, :], w["L1_ffn_down_w"].rearrange("e (t p) d -> p (e t) d", p=P)),
            (bias_rows[0:NE * FT, :], w["L1_ffn_gate_b"].rearrange("e (t p) -> (e t) p", p=P)),
            (bias_rows[NE * FT:2 * NE * FT, :], w["L1_ffn_up_b"].rearrange("e (t p) -> (e t) p", p=P)),
            (down_b[:, :], w["L1_ffn_down_b"]),
        ]
        LOADED = 16 * len(loads)
        POOL_SET, DVE_SET, ACT_SET, PE_SET = 9, 6, 4, 2
        SENT = 16 * PARTS * PARTS

        @block.sync
        def _(sp):
            for s in counted:
                sp.sem_inc(s, BASE)
            for dst, src in loads:
                sp.dma_start(dst, src).then_inc(loaded, 16)
            sp.wait_ge(pool_set, POOL_SET)

            def hold(sem_, value):
                sp.wait_ge(sem_, value)
                stand_alone(sp)

            def load_context(t, layer):
                users = [name for name in ("ctxT1.3", "ctxT0.3")[:layer + 1] if name in t.position]
                hold(misc_full, t.use(users[-1]) if users else t.bank())
                b = t.value(1, 1 - layer)
                sp.dma_start(ctx[:, 0:FULL * CC], ctx_main[b]).then_inc(ctx_in, 16)
                sp.dma_start(ctx[0:TAIL, FULL * CC:KT * CC], ctx_tail[b]).then_inc(ctx_in, 16)

            def load_tokens(t):
                hold(xb_ready[0], t.done(0) + BASE)
                hold(xn_ready[0], t.done(0) + BASE)
                sp.dma_start(x0[:, :, :], x_v[t.value(1, 1)]).then_inc(x_in, 16)

            def send_keys(t, layer):
                phase = 1 - layer
                n = lambda scale, plus: t.before(phase, layer, scale, scale, plus)
                hold(kparts_ready, n(len(CHUNKS), len(CHUNKS) + BASE))
                turned = not t.looped and t.number in (FIRST, 0, NB)
                for g in range(QUADS):
                    hold(kx_in[g], n(SENT, (0 if turned else -SENT) + BASE))
                for i in range(PARTS):
                    sp.dma_start(key_rows[layer, i], kpart[i][:, :]).then_inc(key_out, 16)

            def send_quad(t, layer, g, phase):
                n = lambda scale, plus: t.before(phase, layer, scale, scale, plus)
                hold(key_out, n(16 * PARTS, 16 * PARTS + BASE))
                hold(quad_scored, n(QUADS, g + 1 + BASE))
                for i in range(PARTS):
                    src = key_rows[layer, i, g * HQ * D:(g + 1) * HQ * D, :].rearrange("(h d) n -> d h n", d=D)
                    for r in range(PARTS):
                        row = (i * PARTS + r) * D
                        sp.dma_start(KX[row:row + D, g * HQ:(g + 1) * HQ, :], src).then_inc(kx_in[g], 16)

            def send_queries(t, which):
                layer, off = which == 3, -1 if which == 3 else 1
                dst, key_side = (QX[0], QS, KS, QX[1])[which], which == 2
                hold(qparts_ready[which], t.done(off) + BASE)
                hold(q_in[which], t.done(off - 1, SENT) + BASE)
                sp.dma_start(query_rows[which].rearrange("r p n -> p r n"), qpart[:, which % 3, :, :]).then_inc(q_out[which], 16)
                hold(q_out[which], t.done(off, 16) + BASE)
                if which in (1, 2):
                    hold(self_scored, t.done(off - 1, QUADS) + BASE)
                elif t.looped or t.i + off > 0:
                    if which == 3:
                        hold(quad_scored, count_done(t, 0, JOBS[1][-1], QUADS, QUADS, 2 * QUADS + BASE))
                    else:
                        hold(quad_scored, t.before(0, 0, QUADS, QUADS, 2 * QUADS + BASE))
                for j in range(PARTS):
                    src = query_rows[which, j].rearrange("(h d) n -> d h n", d=D)
                    for i in range(PARTS):
                        row = ((j * PARTS + i) if key_side else (i * PARTS + j)) * D
                        sp.dma_start(dst[row:row + D, :, :], src).then_inc(q_in[which], 16)

            def maximum_out(t, phase, name, job):
                hold(misc_free, t.use(name))
                k = job.number % 2
                hold(max_in[k], t.before(phase, job.layer, 16 * NJ[0] // 2, 16 * NJ[1] // 2, 16 * (job.number // 2) + BASE))
                sp.dma_start(max_rows[k], nT[:, k, :]).then_inc(max_out[k], 16)

            def maximum_in(t, phase, job):
                k = job.number % 2
                hold(max_out[k], t.before(phase, job.layer, 16 * NJ[0] // 2, 16 * NJ[1] // 2, 16 * (job.number // 2 + 1) + BASE))
                q = QX[job.layer] if job.cross else QS
                sp.dma_start(q[FILL:ROWS, job.quad * HQ:(job.quad + 1) * HQ, :],
                             max_rows[k].rearrange("(r h) n -> r h n", h=HQ)).then_inc(max_in[k], 16)

            def turn(t):
                for phase in range(2):
                    for slot in range(SLOTS[phase]):
                        for name in t.sends(phase, slot):
                            if name[0:3] == "max":
                                job = JOBS[int(name[-3])][int(name[-1])]
                                if name[0:5] == "max_o":
                                    maximum_out(t, phase, f"nT{name[-3:]}", job)
                                else:
                                    maximum_in(t, phase, job)
                            elif name in ("ctx0", "ctx1"):
                                load_context(t, int(name[3]))
                            elif name == "x":
                                load_tokens(t)
                            elif name in ("keys0", "keys1"):
                                send_keys(t, int(name[4]))
                            elif name[0:4] == "keys":
                                send_quad(t, int(name[4]), int(name[6]), phase)
                            elif name[0] == "q":
                                send_queries(t, int(name[1]))
                            elif name == "out":
                                hold(misc_free, t.use("downb"))
                                sp.dma_start(out_v[t.value(1, -2)], acc[:, :, :]).then_inc(stored, 16)

            run_turns(sp, turn)
            sp.wait_ge(stored, 16 * NB + BASE)

        @block.gpsimd
        def _(pool):
            link = Link(pool, pool_step, POOL_STEPS, lambda: stand_alone(pool))
            g = nc.gpsimd
            link(g.memset(ident[:, :], 0.0))
            link(g.memset(causal[:, :], 0.0))
            link(g.affine_select(out=ident[:, :], in_=ident[:, :], pattern=[[1, P]], compare_op=ALU.not_equal, fill=1.0,
                                 base=0, channel_multiplier=-1))
            g.tensor_copy(ident_b[:, :], ident[:, :]).then_inc(pool_set, 1)
            g.affine_select(out=causal[:, P:2 * P], in_=causal[:, P:2 * P], pattern=[[-1, P]], compare_op=ALU.is_ge,
                            fill=MASKED, base=0, channel_multiplier=1).then_inc(pool_set, 1)
            g.memset(ones[:, :], 1.0).then_inc(pool_set, 1)
            g.memset(minus_half[:, :], -0.5).then_inc(pool_set, 1)
            for e in range(NE):
                m = g.memset(index_score[:, e:e + 1], float(NE - e))
            m.then_inc(pool_set, 1)
            pool.wait_ge(pool_set, 5)
            g.memset(ctxT[CC:CC + 1, :], 1.0).then_inc(pool_set, 1)
            pool.wait_ge(pool_set, 6)
            for rows in (KX, KS, QX[0], QX[1], QS):
                link(g.memset(rows[64:FILL, :, :], 0.0))
            link(g.memset(KX[FILL:ROWS, :, :], 1.0))
            g.memset(KS[FILL:ROWS, :, :], 1.0).then_inc(pool_set, 1)
            pool.wait_ge(pool_set, 7)
            g.memset(VX[0][:, :, :, D:D + 1], 1.0)
            g.memset(VX[1][:, :, :, D:D + 1], 1.0).then_inc(pool_set, 1)
            g.memset(VS[:, :, :, D:D + 1], 1.0).then_inc(pool_set, 1)
            pool.wait_ge(pool_set, POOL_SET)
            pool.wait_ge(loaded, LOADED)
            pool.wait_ge(act_set, ACT_SET)
            pool.wait_ge(dve_set, DVE_SET)

            OFF = (1, 0, -1, -2)

            def hold(sem_, value):
                pool.wait_ge(sem_, value)
                stand_alone(pool)

            def rsqrt_norm(t, site):
                hold(mean_ready[site], t.done(OFF[site]) + BASE)
                link(g.tensor_scalar(rstd[:, site, :], mv[:, site, :, 1], EPS_LN, 1.0, ALU.add, ALU.mult))
                g.tensor_tensor(rstd[:, site, :], rstd[:, site, :], minus_half[:, 0:QT], ALU.pow).then_inc(rstd_ready[site], 1)

            def rsqrt_rms(t, site):
                hold(ssq_ready[site], t.done(0) + BASE)
                link(g.tensor_scalar(rms[:, site, :], ssq[:, site, :], 1.0 / (HID if site else C), EPS_NORM,
                                     ALU.mult, ALU.add))
                g.tensor_tensor(rms[:, site, :], rms[:, site, :], minus_half[:, 0:QT], ALU.pow).then_inc(rms_ready[site], 1)

            def split_keys(t, layer, c):
                at, n = CHUNKS[c]
                s = slice(at, at + n)
                hold(misc_free, t.use(f"key{layer}.{c}"))
                link(g.tensor_tensor(kres[:, 0:n], kf[:, 0:n], kpart[0][:, s], ALU.subtract))
                link(g.tensor_copy(kpart[1][:, s], kres[:, 0:n]))
                g.tensor_tensor(kpart[2][:, s], kres[:, 0:n], kpart[1][:, s], ALU.subtract).then_inc(kparts_ready, 1)
                hold(kparts_ready, t.before(1 - layer, layer, len(CHUNKS), len(CHUNKS), c + 1 + BASE))

            def split_queries(t, which):
                off = -1 if which == 3 else 1
                hold(misc_free, t.use(("qc0", "q0", "k0", "qc1")[which]))
                w = which % 3
                link(g.tensor_tensor(qres[:, :], qf[:, which % 2, :], qpart[:, w, 0, :], ALU.subtract))
                link(g.tensor_copy(qpart[:, w, 1, :], qres[:, :]))
                g.tensor_tensor(qpart[:, w, 2, :], qres[:, :], qpart[:, w, 1, :], ALU.subtract).then_inc(qparts_ready[which], 1)
                hold(qparts_ready[which], t.done(off) + BASE)

            def split_maximum(t, phase, job):
                k = job.number % 2
                hold(nm_ready, t.before(phase, job.layer, *NJ, job.number + 1 + BASE))
                hold(max_out[k], t.before(phase, job.layer, 16 * NJ[0] // 2, 16 * NJ[1] // 2, 16 * (job.number // 2) + BASE))
                link(g.tensor_copy(npart[:, k, :, 0, :], nm[:, k, :, :]))
                link(g.tensor_tensor(nres[:, k, :, :], nm[:, k, :, :], npart[:, k, :, 0, :], ALU.subtract))
                link(g.tensor_copy(npart[:, k, :, 1, :], nres[:, k, :, :]))
                g.tensor_tensor(npart[:, k, :, 2, :], nres[:, k, :, :], npart[:, k, :, 1, :],
                                ALU.subtract).then_inc(nparts_ready, 1)

            def mask_probs(t, job, tile):
                k = job.tile0 + tile
                hold(exp_done, t.before(0, 0, *SLOTS, k + 1 + ST_RING + BASE))
                v = probs[:, k % P_RING, :]
                if tile == 0:
                    v = v.rearrange("p (j q) -> p j q", j=HQ)[:, :, 0:P]
                else:
                    v = v[:, 0:HQ * P].rearrange("p (j q) -> p j q", j=HQ)
                g.affine_select(out=v, in_=v, pattern=[[0, HQ], [1, P]], compare_op=ALU.is_ge, fill=0.0, base=0,
                                channel_multiplier=-1).then_inc(masked, 1)

            def residual_bias(t, layer):
                if layer == 0:
                    hold(x_in, t.done(1, 16) + BASE)
                else:
                    hold(misc_free, t.bank())
                before = f"proj{layer}"
                if before in t.position:
                    hold(misc_free, t.use(before))
                src = x2 if layer else x0
                bb = bp[layer][:, :].unsqueeze(1).broadcast_to([P, QT, C])
                g.tensor_tensor(xb[:, layer, :, :], src[:, :, :], bb, ALU.add).then_inc(xb_ready[layer], 1)

            def turn(t):
                for phase in range(2):
                    for slot in range(SLOTS[phase]):
                        if phase == 0 and t.attention0:
                            for job in JOBS[0]:
                                if not job.cross and job.tile0 <= slot < job.tile0 + job.tiles:
                                    mask_probs(t, job, slot - job.tile0)
                        for job, n in t.maxima(phase, slot):
                            if n == job.maxima - 1:
                                split_maximum(t, phase, job)
                        for name in t.beside(phase, slot):
                            if name[0:3] == "key":
                                split_keys(t, int(name[3]), int(name[5]))
                            elif name in ("qc0", "q0", "k0", "qc1"):
                                split_queries(t, ("qc0", "q0", "k0", "qc1").index(name))
                            elif name[0:2] == "ln" and name[3] == "a":
                                rsqrt_norm(t, int(name[2]))
                            elif name == "xb0":
                                residual_bias(t, 0)
                        if phase == 0 and slot == 6 and t.attention1:
                            residual_bias(t, 1)
                        if phase == 1 and t.attention0:
                            if slot == 9:
                                rsqrt_rms(t, 0)
                            elif slot == 22:
                                hold(sq_ready, t.done(0) + BASE)
                                g.tensor_scalar(h2[:, :, :], h2[:, :, :], act_s[:, 0:1], act_b[:, 0:1], ALU.mult,
                                                ALU.add).then_inc(h2_ready, 1)
                            elif slot == 26:
                                rsqrt_rms(t, 1)

            run_turns(pool, turn, link)

        @block.scalar
        def _(act):
            a = nc.scalar
            link = Link(act, act_step, ACT_STEPS)
            act.sem_inc(exp_done, ST_RING)
            act.wait_ge(loaded, LOADED)
            act.wait_ge(pool_set, POOL_SET)
            link(a.activation(tx[:, :], gx[:, :], ACT.Tanh))
            link(a.activation(tf[:, :], gf[:, :], ACT.Tanh))
            act.wait_ge(dve_set, DVE_SET)
            for wt in (wq0, wcq0, wq1):
                a.mul(wt[:, :], wt[:, :], SCALE)
            for n in (0, 1, 3):
                a.mul(bias_col[:, n:n + 1], bias_col[:, n:n + 1], SCALE)
            a.mul(wp0[:, :], wp0[:, :], tx[:, 0:1])
            link(a.mul(wo1[:, :], wo1[:, :], tx[:, 1:2]))
            a.mul(bp[0][:, :], bp[0][:, :], tx[:, 0:1]).then_inc(act_set, 1)
            a.mul(bp[1][:, :], bp[1][:, :], tx[:, 1:2]).then_inc(act_set, 1)
            link(a.mul(tf_half[:, :], tf[:, 1:2], 0.5))
            link(a.mul(down[:, :, :], down[:, :, :], tf_half[:, 0:1]))
            a.mul(down_b[:, :], down_b[:, :], tf[0:NE, 1:2]).then_inc(act_set, 1)
            a.mul(ma2t[:, :], wstat[:, 1:2], tf[:, 0:1]).then_inc(act_set, 1)
            act.wait_ge(act_set, ACT_SET)

            def filled(t, name):
                act.wait_ge(misc_full, t.use(name))

            def turned(t, name, dst, src):
                filled(t, name)
                a.copy(dst, src).then_inc(misc_free, 1)

            def context(t, what, layer, c):
                name = f"{what}{layer}.{c}"
                at, n = CHUNKS[c]
                phase = 1 - layer
                if what == "ctxT":
                    turned(t, name, ctxT[0:CC, at:at + n], MS[0:CC, 0:n])
                elif what == "key":
                    filled(t, name)
                    act.wait_ge(kparts_ready, t.before(phase, layer, len(CHUNKS), len(CHUNKS), c + BASE))
                    if c == 0:
                        act.wait_ge(key_out, t.before(phase, layer, 16 * PARTS, 16 * PARTS, BASE))
                    a.copy(kf[:, 0:n], MS[:, 0:n])
                    a.copy(kpart[0][:, at:at + n], MS[:, 0:n]).then_inc(misc_free, 1)
                else:
                    t0, rows = 4 * c, (P if c < 3 else TAIL)
                    t1 = min(t0 + 4, KT)
                    turned(t, name, VX[layer][0:rows, t0:t1, :, 0:D],
                           MS[0:rows, 0:(t1 - t0) * C].rearrange("p (t h d) -> p t h d", h=H, d=D))

            def queries(t, which, name, bias):
                filled(t, name)
                user, off = ((2, 0), (3, -1), (0, 1), (1, 0))[which]
                act.wait_ge(qparts_ready[user], t.done(off) + BASE)
                user, off = ((3, -1), (1, 0), (2, 0), (0, 0))[which]
                act.wait_ge(q_out[user], t.done(off, 16) + BASE)
                v = bias_col[:, bias:bias + 1]
                a.activation(qf[:, which % 2, :], MS[:, 0:T], ACT.Identity, bias=v)
                a.activation(qpart[:, which % 3, 0, :], MS[:, 0:T], ACT.Identity, bias=v).then_inc(misc_free, 1)

            def turn_maximum(t, phase, name):
                job = JOBS[int(name[-3])][int(name[-1])]
                filled(t, name)
                act.wait_ge(max_out[job.number % 2],
                            t.before(phase, job.layer, 16 * NJ[0] // 2, 16 * NJ[1] // 2, 16 * (job.number // 2) + BASE))
                a.copy(nT[:, job.number % 2, :], MSB[0:PARTS * HQ, 0:T]).then_inc(misc_free, 1)

            def take_values(t, phase, job):
                act.wait_ge(probs_free, count_done(t, phase, job, *SLOTS, job.tile0 + job.tiles + P_RING + BASE))
                a.copy(yt[:, job.number % 2, :], PV[:, 0:T]).then_inc(yt_ready, 1)

            def exponentials(t, phase, slot):
                job = [j for j in JOBS[phase] if j.tile0 <= slot][-1]
                tile = slot - job.tile0
                rows = TAIL if job.cross and tile == FULL else P
                cols = HQ * T if job.cross or tile == 0 else HQ * P
                act.wait_ge(st_full, t.before(phase, phase, *SLOTS, slot + 1 + BASE))
                act.wait_ge(probs_free, t.before(phase, phase, *SLOTS, slot + 1 + BASE))
                a.activation(probs[0:rows, slot % P_RING, 0:cols], ST[slot % ST_RING][0:rows, 0:cols],
                             ACT.Exp).then_inc(exp_done, 1)

            def turn(t):
                for phase in range(2):
                    for slot in range(SLOTS[phase]):
                        if t.attends(phase):
                            exponentials(t, phase, slot)
                        job = t.job_before(phase, slot)
                        if job:
                            take_values(t, phase, job)
                        for name in t.beside(phase, slot):
                            if name[0:2] == "nT":
                                turn_maximum(t, phase, name)
                            elif name[0:4] == "ctxT":
                                context(t, "ctxT", int(name[4]), int(name[6]))
                            elif name[0:3] in ("key", "val"):
                                context(t, name[0:3], int(name[3]), int(name[5]))
                            elif name in ("yT0", "yT1"):
                                turned(t, name, yT[:, :], MS[:, 0:T])
                            elif name in ("xT0", "xT1", "xT2"):
                                turned(t, name, xnT[:, int(name[2]), :], MS[:, 0:T])
                            elif name in ("qc0", "q0", "k0", "qc1"):
                                which = ("qc0", "q0", "k0", "qc1").index(name)
                                queries(t, which, name, which)
                            elif name == "a1T":
                                turned(t, name, a1T[:, :], MSB[:, 0:T])
                            elif name in ("a2T.0", "a2T.1"):
                                turned(t, name, a2T[:, int(name[4]), :, :], MSB[:, 0:HID].rearrange("p (k q) -> p k q", k=HT))
                            elif name == "ln1b":
                                act.wait_ge(xn_ready[1], t.done(0) + BASE)
                                for q in range(QT):
                                    sq = a.activation(h2[:, q, 0:C], xn[:, 1, q, :], ACT.Square, accum_out=ssq[:, 0, q:q + 1])
                                sq.then_inc(ssq_ready[0], 1)
                            elif name == "route1":
                                act.wait_ge(misc_free, t.use("router"))
                                a.activation(lg[:, :, :], lg[:, :, :], ACT.Exp).then_inc(e_ready, 1)
                            elif name == "prT":
                                turned(t, name, prT, MS[0:NE, 0:T])
                            elif name[0:4] == "gate":
                                filled(t, name)
                                for f in range(FT):
                                    n = int(name[4]) * FT + f
                                    a.activation(tg[:, f, :], MS[:, f * T:(f + 1) * T], ACT.Tanh, bias=bias_gh[:, n:n + 1],
                                                 scale=0.5)
                                    last = a.activation(gb[:, f, :], MS[:, f * T:(f + 1) * T], ACT.Identity,
                                                        bias=bias_gu[:, n:n + 1])
                                last.then_inc(misc_free, 1)
                        if phase == 1 and t.attention0:
                            if slot == 22:
                                act.wait_ge(misc_free, t.use("hid.1"))
                                a.activation(h2[:, :, :], hr[:, :, :], ACT.Square).then_inc(sq_ready, 1)
                            elif slot == 25:
                                act.wait_ge(h2_ready, t.done(0) + BASE)
                                for q in range(QT):
                                    sq = a.activation(hr[:, q, :], h2[:, q, :], ACT.Square, accum_out=ssq[:, 1, q:q + 1])
                                sq.then_inc(ssq_ready[1], 1)

            run_turns(act, turn, link)

        @block.vector
        def _(dve):
            v = nc.vector
            link = Link(dve, dve_step, DVE_STEPS)
            dve.sem_inc(mx_free, MX_RING)
            v.memset(PV[:, :], 0.0).then_inc(dve_set, 1)
            dve.wait_ge(loaded, LOADED)
            v.tensor_reduce(wabs[:, :], wraw[:, :, :], AX_X, ALU.add, apply_absolute_value=True).then_inc(dve_set, 1)
            dve.wait_ge(pe_set, 1)
            link(v.tensor_scalar(wstat[:, 0:2], MX[0][:, 0:2], 1.0 / (HID * C), EPS_Q, ALU.mult, ALU.max))
            link(v.reciprocal(wstat[:, 2:4], wstat[:, 0:2]))
            for i in range(2):
                link(v.tensor_scalar(wraw[:, i, :], wraw[:, i, :], wstat[:, 2 + i:3 + i], MAGIC, ALU.mult, ALU.add))
                link(v.tensor_scalar(wraw[:, i, :], wraw[:, i, :], MAGIC, 1.0, ALU.subtract, ALU.min))
                v.tensor_scalar(wtern[:, i, :], wraw[:, i, :], -1.0, None, ALU.max).then_inc(dve_set, 1)
            dve.wait_ge(pe_set, PE_SET)
            v.tensor_copy(t1T[:, :], ST[0][:, :].bitcast(BF16)[:, 0:HID])
            v.tensor_copy(t2T[:, :, :], ST[0][:, :].bitcast(BF16)[:, 2 * CHUNK:2 * CHUNK + HID].rearrange("p (k c) -> p k c", k=HT))
            v.tensor_copy(rwT[:, :], ST[1][:, 0:NE]).then_inc(dve_set, 1)
            link(v.tensor_copy(bias_gu[:, :], ST[1][:, CHUNK:CHUNK + 2 * NE * FT]))
            v.tensor_scalar(bias_gh[:, :], bias_gu[:, 0:NE * FT], 0.5, None, ALU.mult).then_inc(dve_set, 1)
            dve.wait_ge(dve_set, DVE_SET)
            dve.wait_ge(pool_set, POOL_SET)
            dve.wait_ge(act_set, ACT_SET)

            SOURCE = (x0, x1, x2, x3)
            OFF = (1, 0, -1, -2)

            def norm_statistics(t, site):
                src = SOURCE[site]
                if site == 0:
                    dve.wait_ge(x_in, t.done(1, 16) + BASE)
                elif site == 2:
                    dve.wait_ge(misc_free, t.bank())
                else:
                    dve.wait_ge(misc_free, t.use("proj0" if site == 1 else "proj1"))
                for q in range(QT):
                    s = v.bn_stats(stats[:, site, q, :], src[:, q, :])
                link(s)
                stand_alone(dve)
                for q in range(QT):
                    s = v.bn_aggr(mv[:, site, q, :], stats[:, site, q, :])
                s.then_inc(mean_ready[site], 1)

            def normalise(t, site):
                before = {0: "xT1", 1: "xT2"}.get(site)
                dve.wait_ge(misc_full, t.use(before) if before in t.position else t.bank())
                dve.wait_ge(rstd_ready[site], t.done(OFF[site]) + BASE)
                src = SOURCE[site]
                for q in range(QT):
                    s = v.tensor_scalar(xn[:, site % 2, q, :], src[:, q, :], mv[:, site, q, 0:1], rstd[:, site, q:q + 1],
                                        ALU.subtract, ALU.mult)
                s.then_inc(xn_ready[site], 1)

            def maximum(t, phase, job, n):
                k = job.mx0 + n
                dve.wait_ge(mx_full, t.before(phase, job.layer, *MAXIMA, k + 1 + BASE))
                bank = MX[k % MX_RING]
                if job.cross:
                    ins = v.reduce_max(mx[:, job.number % 2, n:n + 1], bank[:, 0:MXW[n % 4]], AX_X)
                else:
                    keys = (n % QT + 1) * P
                    stand_alone(dve)
                    ins = v.tensor_tensor_reduce(out=mxs[:, 0:keys], in0=bank[:, 0:keys], in1=causal[:, 2 * P - keys:2 * P],
                                                 scale=1.0, scalar=LOWEST, op0=ALU.add, op1=ALU.max,
                                                 accum_out=mx[:, job.number % 2, n:n + 1])
                ins.then_inc(mx_free, 1)
                if not job.cross:
                    dve.wait_ge(mx_free, t.before(phase, job.layer, *MAXIMA, k + 1 + MX_RING + BASE))
                if n == job.maxima - 1:
                    negate_maximum(t, phase, job)

            def negate_maximum(t, phase, job):
                k = job.number % 2
                dve.wait_ge(mx_free, t.before(phase, job.layer, *MAXIMA, job.mx0 + job.maxima + MX_RING + BASE))
                dve.wait_ge(nparts_ready, t.before(phase, job.layer, *NJ, max(job.number - 1, 0) + BASE))
                out = nm[:, k, :, :].rearrange("p t h -> p h t")
                if job.cross:
                    v.tensor_reduce(out, mx[:, k, :].rearrange("p (h t c) -> p h t c", h=HQ, t=QT), AX_X, ALU.max,
                                    negate=True).then_inc(nm_ready, 1)
                else:
                    v.tensor_scalar(out, mx[:, k, 0:HQ * QT].rearrange("p (h t) -> p h t", t=QT), -1.0, None,
                                    ALU.mult).then_inc(nm_ready, 1)

            def divide(t, name):
                job = JOBS[int(name[1])][int(name[3])]
                dve.wait_ge(misc_full, t.use(name))
                y = MS[:, 0:QT * P].rearrange("p (t j r) -> p t j r", t=QT, j=HQ)
                link(v.reciprocal(rden[:, :, :], y[:, :, :, D]))
                dst = yx[job.layer] if job.cross else ys
                v.tensor_tensor(dst[:, :, job.quad * HQ:(job.quad + 1) * HQ, :], y[:, :, :, 0:D],
                                rden[:, :, :].unsqueeze(3).broadcast_to([P, QT, HQ, D]), ALU.mult).then_inc(misc_free, 1)
                if name == "Y0.7":
                    dve.wait_ge(misc_free, t.use(name))
                    v.tensor_tensor(yx[0][:, :, :, :], yx[0][:, :, :, :], ys[:, :, :, :], ALU.add).then_inc(y_ready, 1)

            def project(t, layer, dst):
                dve.wait_ge(misc_full, t.use(f"proj{layer}"))
                dve.wait_ge(xb_ready[layer], t.done(-2 if layer else 0) + BASE)
                v.tensor_tensor(dst[:, :, :], MS[:, 0:T].rearrange("p (t c) -> p t c", t=QT), xb[:, layer, :, :],
                                ALU.add).then_inc(misc_free, 1)

            def quantise(site, xh, q, ready):
                link(v.tensor_reduce(amax[:, site, :], xh, AX_X, ALU.max, apply_absolute_value=True))
                link(v.tensor_scalar(amax[:, site, :], amax[:, site, :], EPS_Q, None, ALU.max))
                link(v.reciprocal(qs[:, site, :], amax[:, site, :]))
                link(v.tensor_scalar(qs[:, site, :], qs[:, site, :], 127.0, None, ALU.mult))
                back = wstat[:, 0:1] if site == 0 else ma2t[:, 0:1]
                v.tensor_scalar(dq[:, site, :], amax[:, site, :], 1.0 / 127.0, back, ALU.mult, ALU.mult)
                for i in range(QT):
                    s = v.tensor_scalar(xh[:, i, :], xh[:, i, :], qs[:, site, i:i + 1], MAGIC, ALU.mult, ALU.add)
                link(s)
                v.tensor_scalar(q, xh, MAGIC, None, ALU.subtract).then_inc(ready, 1)

            def quantised_tokens(t):
                dve.wait_ge(rms_ready[0], t.done(0) + BASE)
                for i in range(QT):
                    s = v.scalar_tensor_tensor(out=xh1[:, i, :], in0=xn[:, 1, i, :], scalar=rms[:, 0, i:i + 1],
                                               in1=nw1[:, :], op0=ALU.mult, op1=ALU.mult)
                link(s)
                quantise(0, xh1[:, :, :], a1[:, :, :], a1_ready)

            def quantised_hidden(t):
                dve.wait_ge(rms_ready[1], t.done(0) + BASE)
                for i in range(QT):
                    s = v.scalar_tensor_tensor(out=hr[:, i, :], in0=h2[:, i, :], scalar=rms[:, 1, i:i + 1],
                                               in1=nw2[:, :], op0=ALU.mult, op1=ALU.mult)
                link(s)
                quantise(1, hr[:, :, :], a2[:, :, :], a2_ready)

            def wide(ap):
                return ap.unsqueeze(2).broadcast_to([P, QT, NE])

            def logits(t):
                dve.wait_ge(misc_full, t.use("router"))
                L = MS[:, 0:QT * NE].rearrange("p (t e) -> p t e", t=QT)
                link(v.tensor_reduce(r1[:, 0, :], L, AX_X, ALU.max))
                v.tensor_tensor(lg[:, :, :], L, wide(r1[:, 0, :]), ALU.subtract).then_inc(misc_free, 1)

            def largest(n, src):
                index = index_score[:, :].unsqueeze(1).broadcast_to([P, QT, NE])
                link(v.tensor_reduce(r1[:, 3, :], src[:, :, :], AX_X, ALU.max))
                link(v.tensor_tensor(pick[:, :, :], src[:, :, :], wide(r1[:, 3, :]), ALU.is_ge))
                link(v.tensor_tensor(pick[:, :, :], pick[:, :, :], index, ALU.mult))
                link(v.tensor_reduce(r1[:, 4, :], pick[:, :, :], AX_X, ALU.max))
                link(v.tensor_tensor(hot[:, n, :, :], pick[:, :, :], wide(r1[:, 4, :]), ALU.is_equal))

            def route(t, step):
                if step == 1:
                    dve.wait_ge(e_ready, t.done(-2) + BASE)
                    link(v.tensor_reduce(r1[:, 1, :], lg[:, :, :], AX_X, ALU.add))
                    link(v.reciprocal(r1[:, 2, :], r1[:, 1, :]))
                    link(v.tensor_tensor(pr[:, :, :], lg[:, :, :], wide(r1[:, 2, :]), ALU.mult))
                elif step == 2:
                    largest(0, pr)
                    link(v.scalar_tensor_tensor(out=rest[:, :, :], in0=hot[:, 0, :, :], scalar=-2.0, in1=pr[:, :, :],
                                                op0=ALU.mult, op1=ALU.add))
                else:
                    largest(1, rest)
                    link(v.tensor_tensor(hot[:, 0, :, :], hot[:, 0, :, :], hot[:, 1, :, :], ALU.add))
                    link(v.tensor_tensor(pr[:, :, :], pr[:, :, :], hot[:, 0, :, :], ALU.mult))
                    link(v.tensor_reduce(r1[:, 1, :], pr[:, :, :], AX_X, ALU.add))
                    link(v.tensor_scalar(r1[:, 1, :], r1[:, 1, :], 1e-9, None, ALU.add))
                    link(v.reciprocal(r1[:, 2, :], r1[:, 1, :]))
                    v.tensor_tensor(wts[:, :, :], pr[:, :, :], wide(r1[:, 2, :]), ALU.mult).then_inc(wts_ready, 1)

            def expert_hidden(t, e):
                dve.wait_ge(misc_free, t.use(f"gate{e}"))
                link(v.scalar_tensor_tensor(out=tg, in0=tg, scalar=1.0, in1=gb, op0=ALU.add, op1=ALU.mult))
                dve.wait_ge(misc_full, t.use(f"up{e}"))
                for f in range(FT):
                    n = NE * FT + e * FT + f
                    s = v.scalar_tensor_tensor(out=hh[:, f, :], in0=MS[:, f * T:(f + 1) * T],
                                               scalar=bias_gu[:, n:n + 1], in1=tg[:, f, :], op0=ALU.add, op1=ALU.mult)
                s.then_inc(misc_free, 1)

            def expert_out(t, e):
                if e == 0:
                    dve.wait_ge(wts_ready, t.done(-2) + BASE)
                    dve.wait_ge(stored, t.done(-3, 16) + BASE)
                else:
                    dve.wait_ge(misc_free, t.use(f"down{e - 1}"))
                dve.wait_ge(misc_full, t.use(f"down{e}"))
                src = acc if e else x3
                for q in range(QT):
                    s = v.scalar_tensor_tensor(out=acc[:, q, :], in0=MS[:, q * C:(q + 1) * C],
                                               scalar=wts[:, q, e:e + 1], in1=src[:, q, :], op0=ALU.mult, op1=ALU.add)
                s.then_inc(misc_free, 1)

            def beside(t, name):
                if name[0] == "Y":
                    divide(t, name)
                elif name[0:2] == "ln":
                    (norm_statistics if name[3] == "a" else normalise)(t, int(name[2]))
                elif name == "proj0":
                    project(t, 0, x1)
                elif name == "proj1":
                    project(t, 1, x3)
                elif name == "v0":
                    dve.wait_ge(misc_full, t.use(name))
                    for q in range(QT):
                        s = v.tensor_tensor(VS[:, q, :, 0:D], MS[:, q * C:(q + 1) * C].rearrange("p (h d) -> p h d", d=D),
                                            bv0[:, :].rearrange("p (h d) -> p h d", d=D), ALU.add)
                    s.then_inc(misc_free, 1)
                elif name == "quant0":
                    quantised_tokens(t)
                elif name in ("hid.0", "hid.1"):
                    q = int(name[4])
                    dve.wait_ge(misc_full, t.use(name))
                    v.tensor_scalar(hr[:, q, :], MS[:, :], 0.0, dq[:, 0, q:q + 1], ALU.max, ALU.mult).then_inc(misc_free, 1)
                elif name == "quant1":
                    quantised_hidden(t)
                elif name == "ffn":
                    dve.wait_ge(misc_full, t.use(name))
                    dve.wait_ge(xb_ready[1], t.done(-1) + BASE)
                    for q in range(QT):
                        s = v.scalar_tensor_tensor(out=x2[:, q, :], in0=MS[:, q * C:(q + 1) * C], scalar=dq[:, 1, q:q + 1],
                                                   in1=x1[:, q, :], op0=ALU.mult, op1=ALU.add)
                    s.then_inc(misc_free, 1)
                elif name == "router":
                    logits(t)
                elif name[0:5] == "route":
                    route(t, int(name[5]))
                elif name[0:2] == "up":
                    expert_hidden(t, int(name[2]))
                elif name == "downb":
                    dve.wait_ge(misc_free, t.use(f"down{NE - 1}"))
                    dve.wait_ge(misc_full, t.use(name))
                    v.tensor_tensor(acc[:, :, :], MS[:, 0:T].rearrange("p (t c) -> p t c", t=QT), acc[:, :, :],
                                    ALU.add).then_inc(misc_free, 1)
                elif name[0:4] == "down":
                    expert_out(t, int(name[4]))

            def turn(t):
                for phase in range(2):
                    for slot in range(SLOTS[phase]):
                        for job, n in t.maxima(phase, slot):
                            maximum(t, phase, job, n)
                        for name in t.beside(phase, slot):
                            beside(t, name)

            run_turns(dve, turn, link)

        @block.tensor
        def _(pe):
            t_ = nc.tensor
            pe.sem_inc(probs_free, P_RING)
            pe.sem_inc(quad_scored, QUADS)
            pe.wait_ge(loaded, LOADED)
            pe.wait_ge(pool_set, POOL_SET)
            pe.wait_ge(dve_set, 2)
            t_.matmul(MX[0][:, 0:2], ones[:, :], wabs[:, :], start=True, stop=True).then_inc(pe_set, 1)
            pe.wait_ge(dve_set, 4)
            tern = ST[0][:, :].bitcast(BF16)
            for i in range(2):
                for k in range(HT):
                    at = 2 * CHUNK * i + k * P
                    t_.transpose(tern[:, at:at + P], wtern[:, i, k * P:(k + 1) * P], ident_b[:, :])
            t_.transpose(ST[1][:, 0:NE], rw[:, :], ident[0:NE, 0:NE])
            t_.transpose(ST[1][:, CHUNK:CHUNK + 2 * NE * FT], bias_rows[:, :],
                         ident[0:2 * NE * FT, 0:2 * NE * FT]).then_inc(pe_set, 1)
            pe.wait_ge(dve_set, DVE_SET)
            pe.wait_ge(act_set, ACT_SET)

            def maximum(t, phase, job, n):
                k = job.mx0 + n
                if n == 0:
                    off = t.at(phase, job.layer)
                    if job.cross:
                        pe.wait_ge(kx_in[job.quad], t.before(phase, job.layer, SENT, SENT, SENT + BASE))
                        pe.wait_ge(q_in[3 if job.layer else 0], t.done(off, SENT) + BASE)
                    elif job.quad == 0:
                        pe.wait_ge(q_in[1], t.done(off, SENT) + BASE)
                        pe.wait_ge(q_in[2], t.done(off, SENT) + BASE)
                pe.wait_ge(mx_free, t.before(phase, job.layer, *MAXIMA, k + 1 + BASE))
                if job.cross:
                    j, q, c = n // (QT * 4), n // 4 % QT, n % 4
                    h, keys, at, side = job.quad * HQ + j, MXW[c], MX0[c], QX[job.layer]
                    rhs = KX[0:FILL, h, at:at + keys]
                else:
                    j, q = n // QT, n % QT
                    h, keys, side = job.quad * HQ + j, (q + 1) * P, QS
                    rhs = KS[0:FILL, h, 0:keys]
                t_.matmul(MX[k % MX_RING][:, 0:keys], side[0:FILL, h, q * P:(q + 1) * P], rhs, start=True,
                          stop=True).then_inc(mx_full, 1)

            def score(t, phase, job, tile):
                k = job.tile0 + tile
                if tile == 0:
                    pe.wait_ge(max_in[job.number % 2],
                               t.before(phase, phase, 16 * NJ[0] // 2, 16 * NJ[1] // 2, 16 * (job.number // 2 + 1) + BASE))
                pe.wait_ge(exp_done, t.before(phase, phase, *SLOTS, k + 1 + BASE))
                for j in range(HQ):
                    h = job.quad * HQ + j
                    if job.cross:
                        n, lo, q, keys = (P if tile < FULL else TAIL), 0, QX[job.layer], KX
                    else:
                        n, lo, q, keys = P, tile * P, QS, KS
                    last = t_.matmul(ST[k % ST_RING][0:n, j * (T - lo):(j + 1) * (T - lo)], keys[:, h, tile * P:tile * P + n],
                                     q[:, h, lo:T], start=True, stop=True)
                last.then_inc(st_full, 1)

            def values(t, phase, job, tile):
                k = job.tile0 + tile
                if tile == 0:
                    pe.wait_ge(yt_ready, count_done(t, phase, job, *NJ, job.number + BASE))
                if job.cross:
                    pe.wait_ge(exp_done, count_done(t, phase, job, *SLOTS, k + 1 + ST_RING + BASE))
                else:
                    pe.wait_ge(masked, t.done(-1, QUADS * QT, job.quad * QT + tile + 1 + BASE))
                n = TAIL if job.cross and tile == FULL else P
                lo = 0 if job.cross else tile * P
                vals = VX[job.layer] if job.cross else VS
                for j in range(HQ):
                    h = job.quad * HQ + j
                    last = t_.matmul(PV[32 * j:32 * j + D + 1, lo:T], vals[0:n, tile, h, :],
                                     probs[0:n, k % P_RING, j * (T - lo):(j + 1) * (T - lo)],
                                     start=(tile == 0), stop=(tile == job.tiles - 1))
                    if tile == job.tiles - 1 and j == 0:
                        last.then_inc(quad_scored if job.cross else self_scored, 1)
                last.then_inc(probs_free, 1)

            def open_misc(t, name):
                assert t.names[t.next_use] == name
                t.next_use += 1
                pe.wait_ge(misc_free, t.bank(t.position[name]))

            def tokens_by_tile(rhs_of):
                for q in range(QT):
                    last = rhs_of(q)
                last.then_inc(misc_full, 1)

            def context(t, what, layer, c):
                tiles = range(4 * c, min(4 * c + 4, KT))
                at, n = CHUNKS[c]
                if what == "key":
                    t_.matmul(MS[:, 0:n], wck[layer][:, :], ctxT[:, at:at + n], start=True, stop=True).then_inc(misc_full, 1)
                    return
                if what == "ctxT":
                    if c == 0:
                        pe.wait_ge(ctx_in, t.before(1 - layer, layer, 32, 32, 32 + BASE))
                    stand_alone(pe)
                for k in tiles:
                    n = P if k < FULL else TAIL
                    if what == "ctxT":
                        last = t_.transpose(MS[0:CC, (k % 4) * P:(k % 4) * P + n], ctx[0:n, k * CC:(k + 1) * CC],
                                            ident[0:n, 0:n])
                    else:
                        last = t_.matmul(MS[0:n, (k % 4) * C:(k % 4 + 1) * C], ctxT[:, k * P:k * P + n], wcv[layer][:, :],
                                         start=True, stop=True)
                last.then_inc(misc_full, 1)

            def beside(t, phase, name):
                if not t.in_bank(name):
                    return
                open_misc(t, name)
                if name[0:2] == "nT":
                    job = JOBS[int(name[2])][int(name[4])]
                    pe.wait_ge(nparts_ready, t.before(phase, job.layer, *NJ, job.number + 1 + BASE))
                    for q in range(QT):
                        last = t_.transpose(MSB[0:PARTS * HQ, q * P:(q + 1) * P],
                                            npart[:, job.number % 2, q, :, :].rearrange("p r h -> p (r h)"), ident_b[:, :])
                    last.then_inc(misc_full, 1)
                elif name[0] == "Y":
                    job = JOBS[int(name[1])][int(name[3])]
                    pe.wait_ge(yt_ready, count_done(t, phase, job, *NJ, job.number + 1 + BASE))
                    tokens_by_tile(lambda q: t_.transpose(MS[:, q * P:(q + 1) * P],
                                                          yt[:, job.number % 2, q * P:(q + 1) * P], ident[:, :]))
                elif name[0:4] == "ctxT":
                    context(t, "ctxT", int(name[4]), int(name[6]))
                elif name[0:3] in ("key", "val"):
                    context(t, name[0:3], int(name[3]), int(name[5]))
                elif name in ("xT0", "xT1", "xT2"):
                    site = (0, 2, 3)[int(name[2])]
                    pe.wait_ge(xn_ready[site], t.done((1, 0, -1, -2)[site]) + BASE)
                    tokens_by_tile(lambda q: t_.transpose(MS[:, q * P:(q + 1) * P], xn[:, site % 2, q, :], ident[:, :]))
                elif name in ("qc0", "q0", "k0", "qc1"):
                    weight, site = {"qc0": (wcq0, 0), "q0": (wq0, 0), "k0": (wk0, 0), "qc1": (wq1, 1)}[name]
                    t_.matmul(MS[:, 0:T], weight[:, :], xnT[:, site, :], start=True, stop=True).then_inc(misc_full, 1)
                elif name == "v0":
                    tokens_by_tile(lambda q: t_.matmul(MS[:, q * C:(q + 1) * C], xnT[:, 0, q * P:(q + 1) * P], wv0[:, :],
                                                       start=True, stop=True))
                elif name in ("yT0", "yT1"):
                    layer = int(name[2])
                    if layer == 0:
                        pe.wait_ge(y_ready, t.done(0) + BASE)
                    y = yx[layer][:, :, :, :].rearrange("p t h d -> p t (h d)")
                    tokens_by_tile(lambda q: t_.transpose(MS[:, q * P:(q + 1) * P], y[:, q, :], ident[:, :]))
                elif name in ("proj0", "proj1"):
                    weight = wo1 if name == "proj1" else wp0
                    tokens_by_tile(lambda q: t_.matmul(MS[:, q * C:(q + 1) * C], yT[:, q * P:(q + 1) * P], weight[:, :],
                                                       start=True, stop=True))
                elif name == "a1T":
                    pe.wait_ge(a1_ready, t.done(0) + BASE)
                    tokens_by_tile(lambda q: t_.transpose(MSB[:, q * P:(q + 1) * P], a1[:, q, :], ident_b[:, :]))
                elif name in ("hid.0", "hid.1"):
                    q = int(name[4])
                    t_.matmul(MS[:, :], a1T[:, q * P:(q + 1) * P], t1T[:, :], start=True, stop=True).then_inc(misc_full, 1)
                elif name in ("a2T.0", "a2T.1"):
                    q = int(name[4])
                    pe.wait_ge(a2_ready, t.done(0) + BASE)
                    for k in range(HT):
                        last = t_.transpose(MSB[:, k * P:(k + 1) * P], a2[:, q, k * P:(k + 1) * P], ident_b[:, :])
                    last.then_inc(misc_full, 1)
                elif name == "ffn":
                    for q in range(QT):
                        for k in range(HT):
                            last = t_.matmul(MS[:, q * C:(q + 1) * C], a2T[:, q, k, :], t2T[:, k, :], start=(k == 0),
                                             stop=(k == HT - 1))
                    last.then_inc(misc_full, 1)
                elif name == "router":
                    tokens_by_tile(lambda q: t_.matmul(MS[:, q * NE:(q + 1) * NE], xnT[:, 2, q * P:(q + 1) * P], rwT[:, :],
                                                       start=True, stop=True))
                elif name == "prT":
                    pe.wait_ge(wts_ready, t.done(-2) + BASE)
                    tokens_by_tile(lambda q: t_.transpose(MS[0:NE, q * P:(q + 1) * P], wts[:, q, :], ident[:, :]))
                elif name == "downb":
                    tokens_by_tile(lambda q: t_.matmul(MS[:, q * C:(q + 1) * C], prT[:, q * P:(q + 1) * P], down_b[:, :],
                                                       start=True, stop=True))
                elif name[0:4] == "gate" or name[0:2] == "up":
                    e = int(name[-1])
                    weight = gate if name[0] == "g" else up
                    for f in range(FT):
                        last = t_.matmul(MS[:, f * T:(f + 1) * T], weight[:, e, f * P:(f + 1) * P], xnT[:, 2, :],
                                         start=True, stop=True)
                    last.then_inc(misc_full, 1)
                else:
                    assert name[0:4] == "down", name
                    e = int(name[4])
                    for q in range(QT):
                        for f in range(FT):
                            last = t_.matmul(MS[:, q * C:(q + 1) * C], hh[:, f, q * P:(q + 1) * P],
                                             down[:, e * FT + f, :], start=(f == 0), stop=(f == FT - 1))
                    last.then_inc(misc_full, 1)

            def turn(t):
                t.next_use = 0
                for phase in range(2):
                    for slot in range(SLOTS[phase]):
                        before = None
                        if slot == 0:
                            if t.attention0 if phase else t.experts:
                                job = JOBS[1 - phase][-1]
                                before = (job, job.tiles - 1)
                        elif t.attends(phase):
                            job = [j for j in JOBS[phase] if j.tile0 <= slot - 1][-1]
                            before = (job, slot - 1 - job.tile0)
                        if t.attends(phase):
                            job = [j for j in JOBS[phase] if j.tile0 <= slot][-1]
                            score(t, phase, job, slot - job.tile0)
                        if before:
                            values(t, phase, *before)
                        for job, n in t.maxima(phase, slot):
                            maximum(t, phase, job, n)
                        for name in t.beside(phase, slot):
                            beside(t, phase, name)

            run_turns(pe, turn)


_INS = ["x", "ctx_512", "g_xattn", "g_ffn",
        "L0_xattn_Wk", "L0_xattn_bk", "L0_xattn_Wq", "L0_xattn_bq", "L0_xattn_Wv", "L0_xattn_bv",
        "L0_xattn_Wck", "L0_xattn_bck", "L0_xattn_Wcq", "L0_xattn_bcq", "L0_xattn_Wcv", "L0_xattn_bcv",
        "L0_xattn_Wp", "L0_xattn_bp", "L0_ffn_norm1_w", "L0_ffn_w1", "L0_ffn_act_scale", "L0_ffn_act_bias",
        "L0_ffn_norm2_w", "L0_ffn_w2", "L1_xattn_Wq", "L1_xattn_bq", "L1_xattn_Wk", "L1_xattn_bk",
        "L1_xattn_Wv", "L1_xattn_bv", "L1_xattn_Wo", "L1_xattn_bo", "L1_ffn_router_w", "L1_ffn_gate_w",
        "L1_ffn_gate_b", "L1_ffn_up_w", "L1_ffn_up_b", "L1_ffn_down_w", "L1_ffn_down_b"]


def kernel(**inputs):
    import numpy as _np
    import concourse.bacc as _bacc
    from concourse import mybir as _mybir
    from concourse.bass_utils import run_bass_kernel_spmd as _run

    nc = _bacc.Bacc("TRN2", target_bir_lowering=False, num_devices=1)
    arrays, args = {}, {}
    for name in _INS:
        a = _np.ascontiguousarray(inputs[name])
        arrays[f"in_{name}"] = a
        args[name] = nc.dram_tensor(f"in_{name}", a.shape, _mybir.dt.from_np(a.dtype), kind="ExternalInput").ap()
    out = nc.dram_tensor("out_x", arrays["in_x"].shape, _mybir.dt.float32, kind="ExternalOutput").ap()
    x_d, ctx_d = args.pop("x"), args.pop("ctx_512")
    flamingo_gated_blocks(nc, args, x_d, ctx_d, out)
    r = _run(nc, [arrays], core_ids=[0])
    return r.results[0]["out_x"]
```

```python
from contextlib import ExitStack

import numpy as np

import concourse.bass as bass
from concourse import mybir

F32 = mybir.dt.float32
BF16 = mybir.dt.bfloat16
ALU = mybir.AluOpType
ACT = mybir.ActivationFunctionType
AX_X = mybir.AxisListType.X

P = 128
NB = 16
T = 256
QT = T // P
C = 128
H = 16
D = C // H
NK = 1601
CC = 64
KT = 13
FULL = KT - 1
TAIL = NK - FULL * P
HID = 512
HT = HID // P
NE = 8
FF = 256
FT = FF // P
QUADS = 4
HQ = H // QUADS
PARTS = 3
TERMS = PARTS * PARTS * D
FILL = 96
ROWS = FILL + PARTS
SCALE = float(np.float32(1.0 / np.sqrt(D)))
MASKED = -1e30
LOWEST = -3e38
MAGIC = 12582912.0
EPS_LN, EPS_NORM, EPS_Q = 1e-5, 1e-8, 1e-5
CHUNK = 512
CHUNKS = [(c * CHUNK, min(CHUNK, NK - c * CHUNK)) for c in range(4)]
MXW = [401, 401, 401, 398]
MX0 = [0, 401, 802, 1203]
P_RING, ST_RING, MX_RING = 2, 3, 3
TWO_ONES = float(np.array([0x3F803F80], np.uint32).view(np.float32)[0])
BASE = 1


class Job:

    def __init__(self, cross, layer, quad, number, tile0, mx0):
        self.cross, self.layer, self.quad, self.number = cross, layer, quad, number
        self.tiles = KT if cross else QT
        self.maxima = HQ * QT * (4 if cross else 1)
        self.tile0, self.mx0 = tile0, mx0


def plan():
    jobs = [[], []]
    for layer in range(2):
        tile = mx = 0
        for quad in range(QUADS):
            for cross in ((True, False) if layer == 0 else (True,)):
                j = Job(cross, layer, quad, len(jobs[layer]), tile, mx)
                jobs[layer].append(j)
                tile, mx = tile + j.tiles, mx + j.maxima
    return jobs


JOBS = plan()
SLOTS = [sum(j.tiles for j in jobs) for jobs in JOBS]
MAXIMA = [sum(j.maxima for j in jobs) for jobs in JOBS]
NJ = [len(jobs) for jobs in JOBS]
assert not any(n % 2 for n in SLOTS + NJ)
HALVES = 2
UNITS = [HALVES * n for n in SLOTS]


def ring_start(counts):
    return [max(0, 3 - min((n + count) - max(k for k in range(count) if k % 3 == n) for count in counts))
            for n in range(3)]


ST_EXTRA, MX_EXTRA = ring_start(UNITS), ring_start(MAXIMA)
LEAD = 9
TURN_AT = 6
LOOP = (2, NB - 1)
FIRST, LAST = -1, NB + 1

BESIDE = [{
    0: ["ctxT1.0", "ln2a"], 1: ["Y1.3"], 2: ["ctxT1.1", "ln2b"], 3: ["yT1"], 4: ["proj1"], 5: ["ln3a"],
    8: ["xT1", "ln3b"], 10: ["qc1"], 11: ["xT2"], 12: ["router"], 13: ["val1.0"], 15: ["key1.0"],
    16: ["route1"], 17: ["val1.1"], 18: ["key1.1"], 19: ["val1.2", "route2"], 20: ["val1.3"], 21: ["key1.2"],
    22: ["route3"], 25: ["key1.3"], 26: ["prT"], 59: ["downb"]}, {
    0: ["ctxT0.0", "ln0a"], 1: ["Y0.7"], 2: ["ctxT0.1", "ln0b"], 3: ["yT0"], 4: ["key0.0"],
    5: ["proj0"], 6: ["ln1a", "xb0"], 8: ["key0.1"], 9: ["xT0", "ln1b"], 10: ["qc0"], 11: ["key0.2"], 12: ["q0"],
    13: ["quant0"], 14: ["k0"], 15: ["quant1"], 16: ["v0"], 17: ["key0.3"], 18: ["a1T"], 19: ["hid.0"], 21: ["hid.1"],
    22: ["val0.0"], 23: ["val0.1"], 24: ["val0.2"], 25: ["val0.3"], 28: ["quant2"], 29: ["quant3"], 30: ["quant4"],
    31: ["quant5"], 33: ["quant6"], 35: ["a2T.0"], 36: ["a2T.1"], 37: ["ffn"]}]
for n, slot in enumerate((27, 28, 30, 32, 33, 34, 35, 36, 38, 40, 41, 42, 43, 45, 47, 48, 49, 50, 51, 53, 55, 56, 57, 58)):
    BESIDE[0].setdefault(slot, []).append(f"{('gate', 'up', 'down')[n % 3]}{n // 3}")
for _layer in range(2):
    for _job in JOBS[_layer]:
        if _job.number:
            BESIDE[_layer].setdefault(_job.tile0 + 1, []).insert(0, f"Y{_layer}.{_job.number - 1}")
        _slot, _phase = _job.tile0 - TURN_AT, _layer
        if _slot < 0:
            _phase = 1 - _layer
            _slot += SLOTS[_phase]
        BESIDE[_phase].setdefault(_slot, []).insert(0, f"nT{_layer}.{_job.number}")


def vector_load(phase, slot):
    loads = {"ln": 1, "Y": 1, "up": 2, "down": 1, "proj": 1, "route1": 1, "route2": 2, "route3": 3, "v0": 1, "hid": 1,
             "quant": 2, "ffn": 1, "downb": 1}
    return sum(next((load for start, load in loads.items() if name.startswith(start) and name != "router"), 0)
               for name in BESIDE[phase].get(slot, []))


def maximum_steps():
    at = [[[] for _ in range(n)] for n in SLOTS]
    turn = sum(SLOTS)
    before = SLOTS[0] + JOBS[1][-1].tile0 - LEAD - turn
    order = []
    for job in JOBS[0] + JOBS[1]:
        order += [(job, n) for n in range(job.maxima)]
        if not job.cross:
            continue
        deadline = SLOTS[0] * job.layer + job.tile0 - LEAD
        places = [((slot % turn) >= SLOTS[0], slot % turn - SLOTS[0] * ((slot % turn) >= SLOTS[0]))
                  for slot in range(before + 1, deadline + 1)]
        loads = [vector_load(*place) for place in places]
        level = 0.0
        while sum(max(0.0, level - load) for load in loads) < len(order):
            level += 0.01
        filled = 0.0
        for place, load in zip(places, loads):
            first = round(filled)
            filled += max(0.0, level - load)
            at[place[0]][place[1]] += order[first:round(filled)]
            last = round(filled)
        at[places[-1][0]][places[-1][1]] += order[last:]
        order, before = [], deadline
    return at


MAXIMUM_AT = maximum_steps()

SEND_AT = [{
    0: ["keys0.3"], 7: ["ctx0", "x"], 11: ["q3"], 13: ["Q3"], 26: ["keys1"], 28: ["keys1.0"], 30: ["keys1.1"],
    44: ["keys1.2"], 59: ["keys1.3", "out"]}, {
    5: ["ctx1"], 11: ["q0"], 13: ["Q0", "q1"], 15: ["q2"], 17: ["keys0"], 19: ["keys0.0"], 20: ["Q1"], 23: ["Q2"],
    28: ["keys0.1"], 40: ["keys0.2"]}]
MAX_IN_AFTER = 3

EXPERTS_FROM, EXPERTS_TO = 27, 14
LATE = {slot - EXPERTS_FROM + EXPERTS_TO: [n for n in names if n[0:4] in ("gate", "down") or n[0:2] == "up"]
        for slot, names in BESIDE[0].items() if slot >= EXPERTS_FROM}
LATE.update({1: ["yT1"], 2: ["proj1"], 3: ["ln3a"], 5: ["ln3b"], 6: ["xT2"], 7: ["router"], 9: ["route1"], 10: ["route2"],
             11: ["route3"], 13: ["prT"]})
LATE_OUT = SLOTS[0] - EXPERTS_FROM + EXPERTS_TO

OUT_NAMES = ("Y1.3", "yT1", "proj1", "ln3a", "ln3b", "xT2", "router", "route1", "route2", "route3", "prT", "downb", "out")
PRE1_NAMES = ("ln2a", "ln2b", "xT1", "qc1", "q3", "Q3")
FFN_NAMES = ("Y0.7", "yT0", "proj0", "ln1a", "ln1b", "a1T", "hid.0", "hid.1", "a2T.0", "a2T.1", "ffn",
             "ctx1")
PRE0_NAMES = ("ln0a", "ln0b", "xT0", "qc0", "q0", "k0", "v0", "q1", "q2", "Q0", "Q1", "Q2", "xb0", "ctx0", "x")


class Turn:

    def __init__(self, i, origin=0, uses_before=0):
        self.i, self.origin = i, origin
        self.looped = origin != 0
        n = LOOP[0] if self.looped else i
        self.number = n
        self.attention0 = 0 <= n < NB
        self.attention1 = 1 <= n <= NB
        self.experts = 2 <= n <= NB + 1
        self.next0 = n + 1 < NB
        self.names = [name for phase in range(2) for s in range(SLOTS[phase]) for name in self.beside(phase, s)
                      if self.in_bank(name)]
        self.uses_before, self.position = uses_before, {name: n for n, name in enumerate(self.names)}

    def value(self, scale, plus):
        if not self.looped:
            return scale * self.i + plus
        return scale * self.i + (scale * self.origin + plus)

    def done(self, off, scale=1, plus=0):
        if self.looped:
            return self.value(scale, scale * (off + 1) + plus)
        return scale * min(max(self.i + off + 1, 0), NB) + plus

    @staticmethod
    def in_bank(name):
        return name[0:2] not in ("ln", "xb") and name[0:5] not in ("route", "quant") or name == "router"

    def runs(self, name, phase):
        if name in OUT_NAMES or name[0:2] in ("ga", "up") or name[0:4] == "down":
            return self.experts
        if name in PRE1_NAMES:
            return self.attention1
        if name in FFN_NAMES or name[0:5] == "quant":
            return self.attention0
        if name in PRE0_NAMES:
            return self.next0
        if name == "keys0.3":
            return self.attention0
        for start in ("ctxT", "keys", "key", "val"):
            if name[0:len(start)] == start:
                return self.attention1 if name[len(start)] == "1" else self.next0
        layer = int(name[-3])
        if name[0] == "Y" or layer == 1:
            return (self.attention0, self.attention1)[layer]
        return self.next0 if phase == 1 else self.attention0

    def beside(self, phase, slot):
        names = [name for name in BESIDE[phase].get(slot, []) if self.runs(name, phase)]
        if self.number != NB:
            return names
        if phase == 0:
            return [name for name in names if name not in sum(LATE.values(), [])]
        return names + LATE.get(slot, [])

    def sends(self, phase, slot):
        names = [name for name in SEND_AT[phase].get(slot, []) if self.runs(name, phase)]
        if self.number != NB:
            return names
        return names + ["out"] if (phase, slot) == (1, LATE_OUT) else [name for name in names if name != "out"]

    def attends(self, phase):
        return (self.attention0, self.attention1)[phase]

    def at(self, phase, layer):
        return -1 if layer else phase

    def before(self, phase, layer, n0, n1, plus=0):
        off = self.at(phase, layer)
        if self.looped:
            l0, l1 = (1, -1) if layer else (off, off - 1)
            return self.value(n0 + n1, l0 * n0 + l1 * n1 + plus)
        b = self.i + off
        l0, l1 = (min(b + 2, NB), b) if layer else (b, max(b - 1, 0))
        return n0 * l0 + n1 * l1 + plus

    def use(self, name):
        return self.bank(self.position[name] + 1)

    def bank(self, plus=0):
        if not self.looped:
            return self.uses_before + plus + BASE
        return len(self.names) * self.i + (self.uses_before + plus + BASE)

    def maxima(self, phase, slot):
        return [(job, n) for job, n in MAXIMUM_AT[phase][slot]
                if (self.attention1 if job.layer else self.next0 if phase == 1 else self.attention0)]

    def job_before(self, phase, slot):
        for job in JOBS[phase]:
            if job.tile0 == slot and job.number and self.attends(phase):
                return JOBS[phase][job.number - 1]
        if slot == 0 and (self.attention0 if phase else self.experts):
            return JOBS[1 - phase][-1]
        return None


def count_done(t, phase, job, n0, n1, plus=0):
    if job.layer == phase:
        return t.before(phase, job.layer, n0, n1, plus)
    if phase == 1:
        return t.before(0, 0, n0, n1, plus)
    if t.looped:
        return t.value(n0 + n1, -2 * n1 + plus)
    b = t.i - 2
    return n0 * min(b + 2, NB) + n1 * b + plus


DVE_STEPS, ACT_STEPS, POOL_STEPS = 56, 0, 66


class Link:

    def __init__(self, eng, sem, per_turn, then=None):
        self.eng, self.sem, self.per_turn, self.base, self.n, self.turn = eng, sem, per_turn, 0, 0, None
        self.then = then

    def start_turn(self, turn):
        self.turn, self.base, self.n = turn, self.base + self.n, 0

    def __call__(self, ins):
        self.n += 1
        ins.then_inc(self.sem, 1)
        v = self.base + self.n
        looped = self.turn is not None and self.turn.looped
        self.eng.wait_ge(self.sem, self.turn.i * self.per_turn + v if looped else v)
        if self.then and looped:
            self.then()

    def end_turn(self):
        if self.turn.looped:
            assert self.n == self.per_turn, ("linked steps", self.sem, self.n, self.per_turn)
            self.n *= LOOP[1] - LOOP[0]


def run_turns(eng, turn, link=None):
    uses = 0

    def one(t):
        if link:
            link.start_turn(t)
        turn(t)
        if link:
            link.end_turn()

    for i in range(FIRST, LOOP[0]):
        t = Turn(i, uses_before=uses)
        one(t)
        uses += len(t.names)
    with eng.Fori(0, LOOP[1] - LOOP[0]) as i:
        t = Turn(i, origin=LOOP[0], uses_before=uses)
        one(t)
    uses += len(t.names) * (LOOP[1] - LOOP[0])
    for i in range(LOOP[1], LAST + 1):
        t = Turn(i, uses_before=uses)
        one(t)
        uses += len(t.names)


def flamingo_gated_blocks(nc, w, x_d, ctx_d, out_d):
    x_v = x_d.rearrange("b (t p) c -> b p t c", p=P)
    out_v = out_d.rearrange("b (t p) c -> b p t c", p=P)
    ctx_main = ctx_d[:, 0:FULL * P, :].rearrange("b (p t) c -> b p (t c)", t=FULL)
    ctx_tail = ctx_d[:, FULL * P:NK, :]

    with ExitStack() as stack:
        def sb(name, shape, dt=F32):
            return stack.enter_context(nc.sbuf_tensor(name, shape, dt))

        def sem(name):
            return stack.enter_context(nc.semaphore(name))

        ident = sb("ident", [P, P])
        ident_b = sb("ident_b", [P, P], BF16)
        causal = sb("causal", [P, 2 * P])
        minus_half = sb("minus_half", [P, 4])
        index_score = sb("index_score", [P, NE])
        gx = sb("gx", [P, 2])
        gf = sb("gf", [P, 2])
        tx = sb("tx", [P, 2])
        tf = sb("tf", [P, 2])
        tf_half = sb("tf_half", [P, 1])
        wq0, wk0, wv0, wcq0, wp0 = (sb(n, [P, C]) for n in ("wq0", "wk0", "wv0", "wcq0", "wp0"))
        wq1, wo1 = (sb(n, [P, C]) for n in ("wq1", "wo1"))
        wck = [sb(f"wck{i}", [CC + 1, C]) for i in range(2)]
        wcv = [sb(f"wcv{i}", [CC + 1, C]) for i in range(2)]
        bias_col = sb("bias_col", [P, 4])
        bv0 = sb("bv0", [P, C])
        bp = [sb(f"bp{i}", [P, C]) for i in range(2)]
        nw1 = sb("nw1", [P, C])
        nw2 = sb("nw2", [P, HID])
        act_s = sb("act_s", [P, 1])
        act_b = sb("act_b", [P, 1])
        wide_a = sb("wide_a", [P, 2, HID])
        wide_b = sb("wide_b", [P, 2, HID])
        ones = wide_b[:, 0, 0:P]
        wraw = wide_a
        wabs = sb("wabs", [P, 2])
        wstat = sb("wstat", [P, 4])
        a2 = sb("a2", [P, QT, HID], BF16)
        wtern = a2
        t1T = sb("t1T", [P, HID], BF16)
        t2T = sb("t2T", [P, HT, C], BF16)
        ma2t = sb("ma2t", [P, 1])
        rw = sb("rw", [NE, C])
        rwT = sb("rwT", [P, NE])
        gate = sb("gate", [P, NE, FF])
        up = sb("up", [P, NE, FF])
        down = sb("down", [P, NE * FT, C])
        bias_rows = sb("bias_rows", [2 * NE * FT, P])
        bias_gu = sb("bias_gu", [P, 2 * NE * FT])
        down_b = sb("down_b", [NE, C])

        ctx = sb("ctx", [P, KT * CC])
        ctxT = sb("ctxT", [CC + 1, NK])
        kf = sb("kf", [P, CHUNK])
        kres = sb("kres", [P, CHUNK])
        kpart = [sb(f"kpart{i}", [P, NK], BF16) for i in range(PARTS)]
        KX_rows = sb("KX", [ROWS, H * NK], BF16)
        KS_rows, QS_rows = (sb(n, [ROWS, H * T], BF16) for n in ("KS", "QS"))
        QX_rows = [sb(f"QX{i}", [ROWS, H * T], BF16) for i in range(2)]
        KX, KS, QS, *QX = (rows[:, :].rearrange("r (h n) -> r h n", h=H) for rows in (KX_rows, KS_rows, QS_rows, *QX_rows))
        VX = [sb(f"VX{i}", [P, KT, H, D + 1]) for i in range(2)]
        VS = sb("VS", [P, QT, H, D + 1])
        qf = sb("qf", [P, 2, T])
        qres = sb("qres", [P, T])
        qpart = sb("qpart", [P, 3, PARTS, T], BF16)
        x0 = sb("x0", [P, QT, C])
        x1 = sb("x1", [P, QT, C])
        x2 = sb("x2", [P, QT, C])
        x3 = x1
        xb = sb("xb", [P, 2, QT, C])
        stats = sb("stats", [P, 4, QT, 6])
        mv = sb("mv", [P, 4, QT, 2])
        rstd = sb("rstd", [P, 4, QT])
        xn = sb("xn", [P, 2, QT, C])
        xnT = sb("xnT", [P, 3, T])
        probs = sb("probs", [P, P_RING, HQ * T])
        mx = sb("mx", [P, 2, HQ * QT * 4])
        mxs = sb("mxs", [P, T], BF16)
        nm = sb("nm", [P, 2, QT, HQ])
        nres = sb("nres", [P, 2, QT, HQ])
        npart = sb("npart", [P, 2, QT, PARTS, HQ], BF16)
        nT = sb("nT", [PARTS * HQ, 2, T], BF16)
        yt = sb("yt", [P, 2, T])
        rden = sb("rden", [P, QT, HQ])
        yx = [sb(f"yx{i}", [P, QT, H, D]) for i in range(2)]
        ys = sb("ys", [P, QT, H, D])
        yT = sb("yT", [P, T])
        ssq = sb("ssq", [P, 2, QT])
        rms = sb("rms", [P, 2, QT])
        amax = sb("amax", [P, 2, QT])
        qs = sb("qs", [P, 2, QT])
        dq = sb("dq", [P, 2, QT])
        xh1 = sb("xh1", [P, QT, C])
        a1 = sb("a1", [P, QT, C], BF16)
        a1T = sb("a1T", [P, T], BF16)
        hr, h2 = wide_a, wide_b
        a2T = wide_b[:, 1, :].bitcast(BF16).rearrange("p (t k q) -> p t k q", t=QT, k=HT)
        lg = sb("lg", [P, QT, NE])
        pr = sb("pr", [P, QT, NE])
        pick = sb("pick", [P, QT, NE])
        hot = sb("hot", [P, 2, QT, NE])
        rest = sb("rest", [P, QT, NE])
        wts = sb("wts", [P, QT, NE])
        r1 = sb("r1", [P, 6, QT])
        prT = wide_b[0:NE, 1, 0:T]
        tg, gb, hh = (ap.rearrange("p (t n) -> p t n", t=FT) for ap in (wide_a[:, 0, :], wide_a[:, 1, :], wide_b[:, 0, :]))
        acc = sb("acc", [P, QT, C])

        ST = [stack.enter_context(nc.psum_tensor(f"ST{i}", [P, CHUNK], F32)) for i in range(ST_RING)]
        MX = [stack.enter_context(nc.psum_tensor(f"MX{i}", [P, CHUNK], F32)) for i in range(MX_RING)]
        PV = stack.enter_context(nc.psum_tensor("PV", [P, CHUNK], F32))
        MS = stack.enter_context(nc.psum_tensor("MS", [P, CHUNK], F32))
        MSB = MS[:, :].bitcast(BF16)

        first_loaded = sem("first_loaded")
        loaded = sem("loaded")
        pool_set, dve_set, act_set, pe_set = sem("pool_set"), sem("dve_set"), sem("act_set"), sem("pe_set")
        dve_step, act_step, pool_step = sem("dve_step"), sem("act_step"), sem("pool_step")
        passed = sem("passed")
        misc_full = sem("misc_full")
        misc_free = sem("misc_free")
        ctx_in, x_in, stored = sem("ctx_in"), sem("x_in"), sem("stored")
        kparts_ready = sem("kparts_ready")
        kx_in = [sem(f"kx_in{g}") for g in range(QUADS)]
        q_in = [sem(f"q_in{i}") for i in range(4)]
        qparts_ready = [sem(f"qparts_ready{i}") for i in range(4)]
        quad_scored = sem("quad_scored")
        self_scored = sem("self_scored")
        mean_ready, rstd_ready, xn_ready = ([sem(f"{n}{i}") for i in range(4)] for n in ("mean_ready", "rstd_ready", "xn_ready"))
        mx_full, mx_free = sem("mx_full"), sem("mx_free")
        nm_ready, nparts_ready = sem("nm_ready"), sem("nparts_ready")
        max_in = [sem(f"max_in{i}") for i in range(2)]
        st_full, exp_done, masked, probs_free = sem("st_full"), sem("exp_done"), sem("masked"), sem("probs_free")
        yt_ready, y_ready = sem("yt_ready"), sem("y_ready")
        xb_ready = [sem(f"xb_ready{i}") for i in range(2)]
        ssq_ready, rms_ready = ([sem(f"{n}{i}") for i in range(2)] for n in ("ssq_ready", "rms_ready"))
        a1_ready, a2_ready, sq_ready, h2_ready = sem("a1_ready"), sem("a2_ready"), sem("sq_ready"), sem("h2_ready")
        e_ready, wts_ready, tg_ready = sem("e_ready"), sem("wts_ready"), sem("tg_ready")

        counted = [misc_full, misc_free, ctx_in, x_in, stored, kparts_ready, *kx_in, *q_in, *qparts_ready, quad_scored,
                   self_scored, *mean_ready, *rstd_ready, *xn_ready, mx_full, mx_free, nm_ready, nparts_ready, *max_in,
                   st_full, exp_done, masked, probs_free, yt_ready, y_ready, *xb_ready, *ssq_ready, *rms_ready, a1_ready,
                   a2_ready, sq_ready, h2_ready, e_ready, wts_ready, tg_ready]
        key_rows = nc.dram_tensor("key_rows", [2, PARTS, P, NK], BF16, kind="Internal").ap()
        query_rows = nc.dram_tensor("query_rows", [4, PARTS, P, T], BF16, kind="Internal").ap()
        max_rows = nc.dram_tensor("max_rows", [2, PARTS * HQ, T], BF16, kind="Internal").ap()
        key_out, max_out = sem("key_out"), [sem(f"max_out{i}") for i in range(2)]
        q_out = [sem(f"q_out{i}") for i in range(4)]

        counted += [key_out, *max_out, *q_out]
        block = stack.enter_context(nc.Block())

        def stand_alone(eng):
            eng.sem_inc(passed, 1)

        def pairs(rows, first, end):
            return rows[first:end, :].bitcast(F32)

        first_loads = [
            (wraw[:, 0, :].rearrange("p (t d) -> p t d", t=HT), w["L0_ffn_w1"].rearrange("(t p) d -> p t d", p=P)),
            (wraw[:, 1, :], w["L0_ffn_w2"]),
            (rw[:, :], w["L1_ffn_router_w"]),
            (bias_rows[0:NE * FT, :], w["L1_ffn_gate_b"].rearrange("e (t p) -> (e t) p", p=P)),
            (bias_rows[NE * FT:2 * NE * FT, :], w["L1_ffn_up_b"].rearrange("e (t p) -> (e t) p", p=P)),
        ]
        loads = [
            (gx[:, :], w["g_xattn"].partition_broadcast(P)), (gf[:, :], w["g_ffn"].partition_broadcast(P)),
            (wq0[:, :], w["L0_xattn_Wq"]), (wk0[:, :], w["L0_xattn_Wk"]), (wv0[:, :], w["L0_xattn_Wv"]),
            (wcq0[:, :], w["L0_xattn_Wcq"]), (wp0[:, :], w["L0_xattn_Wp"]),
            (wq1[:, :], w["L1_xattn_Wq"]), (wo1[:, :], w["L1_xattn_Wo"]),
            (wck[0][0:CC, :], w["L0_xattn_Wck"]), (wck[0][CC:CC + 1, :], w["L0_xattn_bck"].unsqueeze(0)),
            (wcv[0][0:CC, :], w["L0_xattn_Wcv"]), (wcv[0][CC:CC + 1, :], w["L0_xattn_bcv"].unsqueeze(0)),
            (wck[1][0:CC, :], w["L1_xattn_Wk"]), (wck[1][CC:CC + 1, :], w["L1_xattn_bk"].unsqueeze(0)),
            (wcv[1][0:CC, :], w["L1_xattn_Wv"]), (wcv[1][CC:CC + 1, :], w["L1_xattn_bv"].unsqueeze(0)),
            (bias_col[:, 0:1], w["L0_xattn_bcq"].unsqueeze(1)), (bias_col[:, 1:2], w["L0_xattn_bq"].unsqueeze(1)),
            (bias_col[:, 2:3], w["L0_xattn_bk"].unsqueeze(1)), (bias_col[:, 3:4], w["L1_xattn_bq"].unsqueeze(1)),
            (bv0[:, :], w["L0_xattn_bv"].partition_broadcast(P)),
            (bp[0][:, :], w["L0_xattn_bp"].partition_broadcast(P)), (bp[1][:, :], w["L1_xattn_bo"].partition_broadcast(P)),
            (nw1[:, :], w["L0_ffn_norm1_w"].partition_broadcast(P)), (nw2[:, :], w["L0_ffn_norm2_w"].partition_broadcast(P)),
            (act_s[:, :], w["L0_ffn_act_scale"].partition_broadcast(P)), (act_b[:, :], w["L0_ffn_act_bias"].partition_broadcast(P)),
            (gate[:, :, :], w["L1_ffn_gate_w"].rearrange("e d f -> d e f")),
            (up[:, :, :], w["L1_ffn_up_w"].rearrange("e d f -> d e f")),
            (down[:, :, :], w["L1_ffn_down_w"].rearrange("e (t p) d -> p (e t) d", p=P)),
            (down_b[:, :], w["L1_ffn_down_b"]),
        ]
        FIRST_LOADED, LOADED = 16 * len(first_loads), 16 * len(loads)
        POOL_SET, DVE_SET, ACT_SET, PE_SET = 9, 6, 4, 2
        SENT = 16 * PARTS * PARTS

        @block.sync
        def _(sp):
            for dst, src in first_loads:
                sp.dma_start(dst, src).then_inc(first_loaded, 16)
            for dst, src in loads:
                sp.dma_start(dst, src).then_inc(loaded, 16)
            for s in counted:
                sp.sem_inc(s, BASE)

            def hold(sem_, value):
                sp.wait_ge(sem_, value)
                stand_alone(sp)

            def load_context(t, layer):
                users = [name for name in ("ctxT1.1", "ctxT0.1")[:layer + 1] if name in t.position]
                hold(misc_full, t.use(users[-1]) if users else t.bank())
                b = t.value(1, 1 - layer)
                sp.dma_start(ctx[:, 0:FULL * CC], ctx_main[b]).then_inc(ctx_in, 16)
                sp.dma_start(ctx[0:TAIL, FULL * CC:KT * CC], ctx_tail[b]).then_inc(ctx_in, 16)

            def load_tokens(t):
                hold(xb_ready[0], t.done(0) + BASE)
                hold(xn_ready[0], t.done(0) + BASE)
                sp.dma_start(x0[:, :, :], x_v[t.value(1, 1)]).then_inc(x_in, 16)

            def send_keys(t, layer):
                phase = 1 - layer
                n = lambda scale, plus: t.before(phase, layer, scale, scale, plus)
                hold(kparts_ready, n(len(CHUNKS), len(CHUNKS) + BASE))
                turned = not t.looped and t.number in (FIRST, 0, NB)
                for g in range(QUADS):
                    hold(kx_in[g], n(SENT, (0 if turned else -SENT) + BASE))
                for i in range(PARTS):
                    sp.dma_start(key_rows[layer, i], kpart[i][:, :]).then_inc(key_out, 16)

            def send_quad(t, layer, g, phase):
                n = lambda scale, plus: t.before(phase, layer, scale, scale, plus)
                hold(key_out, n(16 * PARTS, 16 * PARTS + BASE))
                hold(quad_scored, n(QUADS, g + 1 + BASE))
                for i in range(PARTS):
                    src = key_rows[layer, i, g * HQ * D:(g + 1) * HQ * D, :].rearrange("(h d) n -> d h n", d=D)
                    for r in range(PARTS):
                        row = (i * PARTS + r) * D
                        sp.dma_start(KX[row:row + D, g * HQ:(g + 1) * HQ, :], src).then_inc(kx_in[g], 16)

            def send_queries(t, which):
                off = -1 if which == 3 else 1
                hold(qparts_ready[which], t.done(off) + BASE)
                hold(q_in[which], t.done(off - 1, SENT) + BASE)
                sp.dma_start(query_rows[which].rearrange("r p n -> p r n"), qpart[:, which % 3, :, :]).then_inc(q_out[which], 16)

            def take_queries(t, which):
                off = -1 if which == 3 else 1
                dst, key_side = (QX[0], QS, KS, QX[1])[which], which == 2
                hold(q_out[which], t.done(off, 16) + BASE)
                if which in (1, 2):
                    hold(self_scored, t.done(off - 1, QUADS) + BASE)
                elif t.looped or t.i + off > 0:
                    if which == 3:
                        hold(quad_scored, count_done(t, 0, JOBS[1][-1], QUADS, QUADS, 2 * QUADS + BASE))
                    else:
                        hold(quad_scored, t.before(0, 0, QUADS, QUADS, 2 * QUADS + BASE))
                for j in range(PARTS):
                    src = query_rows[which, j].rearrange("(h d) n -> d h n", d=D)
                    for i in range(PARTS):
                        row = ((j * PARTS + i) if key_side else (i * PARTS + j)) * D
                        sp.dma_start(dst[row:row + D, :, :], src).then_inc(q_in[which], 16)

            def turn(t):
                for phase in range(2):
                    for slot in range(SLOTS[phase]):
                        for name in t.sends(phase, slot):
                            if name in ("ctx0", "ctx1"):
                                load_context(t, int(name[3]))
                            elif name == "x":
                                load_tokens(t)
                            elif name in ("keys0", "keys1"):
                                send_keys(t, int(name[4]))
                            elif name[0:4] == "keys":
                                send_quad(t, int(name[4]), int(name[6]), phase)
                            elif name[0] == "q":
                                send_queries(t, int(name[1]))
                            elif name[0] == "Q":
                                take_queries(t, int(name[1]))
                            elif name == "out":
                                hold(misc_free, t.use("downb"))
                                sp.dma_start(out_v[t.value(1, -2)], acc[:, :, :]).then_inc(stored, 16)

            run_turns(sp, turn)
            sp.wait_ge(stored, 16 * NB + BASE)

        @block.gpsimd
        def _(pool):
            link = Link(pool, pool_step, POOL_STEPS, lambda: stand_alone(pool))
            g = nc.gpsimd
            link(g.memset(ident[:, :], 0.0))
            link(g.memset(causal[:, :], 0.0))
            link(g.affine_select(out=ident[:, :], in_=ident[:, :], pattern=[[1, P]], compare_op=ALU.not_equal, fill=1.0,
                                 base=0, channel_multiplier=-1))
            g.tensor_copy(ident_b[:, :], ident[:, :]).then_inc(pool_set, 1)
            g.affine_select(out=causal[:, P:2 * P], in_=causal[:, P:2 * P], pattern=[[-1, P]], compare_op=ALU.is_ge,
                            fill=MASKED, base=0, channel_multiplier=1).then_inc(pool_set, 1)
            g.memset(ones[:, :], 1.0).then_inc(pool_set, 1)
            g.memset(minus_half[:, :], -0.5).then_inc(pool_set, 1)
            for e in range(NE):
                m = g.memset(index_score[:, e:e + 1], float(NE - e))
            m.then_inc(pool_set, 1)
            pool.wait_ge(pool_set, 5)
            g.memset(ctxT[CC:CC + 1, :], 1.0).then_inc(pool_set, 1)
            pool.wait_ge(pool_set, 6)
            for rows in (KS_rows, *QX_rows, QS_rows):
                link(g.memset(pairs(rows, 64, FILL), 0.0))
            link(g.memset(pairs(KX_rows, FILL, ROWS), TWO_ONES))
            g.memset(KS[FILL:ROWS, :, :], 1.0).then_inc(pool_set, 1)
            pool.wait_ge(pool_set, 7)
            g.memset(VX[0][:, :, :, D:D + 1], 1.0)
            g.memset(VX[1][:, :, :, D:D + 1], 1.0).then_inc(pool_set, 1)
            g.memset(VS[:, :, :, D:D + 1], 1.0).then_inc(pool_set, 1)
            pool.wait_ge(pool_set, POOL_SET)
            pool.wait_ge(loaded, LOADED)
            pool.wait_ge(act_set, ACT_SET)
            pool.wait_ge(dve_set, DVE_SET)

            OFF = (1, 0, -1, -2)

            def hold(sem_, value):
                pool.wait_ge(sem_, value)
                stand_alone(pool)

            def rsqrt_norm(t, site):
                hold(mean_ready[site], t.done(OFF[site]) + BASE)
                link(g.tensor_scalar(rstd[:, site, :], mv[:, site, :, 1], EPS_LN, 1.0, ALU.add, ALU.mult))
                g.tensor_tensor(rstd[:, site, :], rstd[:, site, :], minus_half[:, 0:QT], ALU.pow).then_inc(rstd_ready[site], 1)

            def rsqrt_rms(t, site):
                hold(ssq_ready[site], t.done(0) + BASE)
                link(g.tensor_scalar(rms[:, site, :], ssq[:, site, :], 1.0 / (HID if site else C), EPS_NORM,
                                     ALU.mult, ALU.add))
                g.tensor_tensor(rms[:, site, :], rms[:, site, :], minus_half[:, 0:QT], ALU.pow).then_inc(rms_ready[site], 1)

            def split_keys(t, layer, c):
                at, n = CHUNKS[c]
                s = slice(at, at + n)
                hold(misc_free, t.use(f"key{layer}.{c}"))
                link(g.tensor_tensor(kpart[1][:, s], kf[:, 0:n], kpart[0][:, s], ALU.subtract))
                link(g.tensor_tensor(kres[:, 0:n], kf[:, 0:n], kpart[0][:, s], ALU.subtract))
                g.tensor_tensor(kpart[2][:, s], kres[:, 0:n], kpart[1][:, s], ALU.subtract).then_inc(kparts_ready, 1)
                hold(kparts_ready, t.before(1 - layer, layer, len(CHUNKS), len(CHUNKS), c + 1 + BASE))

            def split_queries(t, which):
                off = -1 if which == 3 else 1
                hold(misc_free, t.use(("qc0", "q0", "k0", "qc1")[which]))
                w = which % 3
                link(g.tensor_tensor(qpart[:, w, 1, :], qf[:, which % 2, :], qpart[:, w, 0, :], ALU.subtract))
                link(g.tensor_tensor(qres[:, :], qf[:, which % 2, :], qpart[:, w, 0, :], ALU.subtract))
                g.tensor_tensor(qpart[:, w, 2, :], qres[:, :], qpart[:, w, 1, :], ALU.subtract).then_inc(qparts_ready[which], 1)
                hold(qparts_ready[which], t.done(off) + BASE)

            def split_maximum(t, phase, job):
                k = job.number % 2
                hold(nm_ready, t.before(phase, job.layer, *NJ, job.number + 1 + BASE))
                hold(max_out[k], t.before(phase, job.layer, 16 * NJ[0] // 2, 16 * NJ[1] // 2, 16 * (job.number // 2) + BASE))
                link(g.tensor_copy(npart[:, k, :, 0, :], nm[:, k, :, :]))
                link(g.tensor_tensor(nres[:, k, :, :], nm[:, k, :, :], npart[:, k, :, 0, :], ALU.subtract))
                link(g.tensor_copy(npart[:, k, :, 1, :], nres[:, k, :, :]))
                g.tensor_tensor(npart[:, k, :, 2, :], nres[:, k, :, :], npart[:, k, :, 1, :],
                                ALU.subtract).then_inc(nparts_ready, 1)

            def mask_probs(t, job, tile):
                k = job.tile0 + tile
                hold(exp_done, t.before(0, 0, *UNITS, HALVES * (k + 1) + ST_RING + BASE))
                v = probs[:, k % P_RING, :]
                if tile == 0:
                    v = v.rearrange("p (j q) -> p j q", j=HQ)[:, :, 0:P]
                else:
                    v = v[:, 0:HQ * P].rearrange("p (j q) -> p j q", j=HQ)
                g.affine_select(out=v, in_=v, pattern=[[0, HQ], [1, P]], compare_op=ALU.is_ge, fill=0.0, base=0,
                                channel_multiplier=-1).then_inc(masked, 1)

            def residual_bias(t, layer):
                if layer == 0:
                    hold(x_in, t.done(1, 16) + BASE)
                else:
                    hold(misc_free, t.bank())
                before = f"proj{layer}"
                if before in t.position:
                    hold(misc_free, t.use(before))
                src = x2 if layer else x0
                bb = bp[layer][:, :].unsqueeze(1).broadcast_to([P, QT, C])
                g.tensor_tensor(xb[:, layer, :, :], src[:, :, :], bb, ALU.add).then_inc(xb_ready[layer], 1)

            def turn(t):
                for phase in range(2):
                    for slot in range(SLOTS[phase]):
                        if phase == 0 and t.attention0:
                            for job in JOBS[0]:
                                if not job.cross and job.tile0 <= slot < job.tile0 + job.tiles:
                                    mask_probs(t, job, slot - job.tile0)
                        for job, n in t.maxima(phase, slot):
                            if n == job.maxima - 1:
                                split_maximum(t, phase, job)
                        for name in t.beside(phase, slot):
                            if name[0:3] == "key":
                                split_keys(t, int(name[3]), int(name[5]))
                            elif name in ("qc0", "q0", "k0", "qc1"):
                                split_queries(t, ("qc0", "q0", "k0", "qc1").index(name))
                            elif name[0:2] == "ln" and name[3] == "a":
                                rsqrt_norm(t, int(name[2]))
                            elif name == "xb0":
                                residual_bias(t, 0)
                        if (phase, slot) == ((1, 3) if t.number == NB else (0, 6)) and t.attention1:
                            residual_bias(t, 1)
                        if phase == 1 and t.attention0:
                            if slot == 9:
                                rsqrt_rms(t, 0)
                            elif slot == 22:
                                hold(sq_ready, t.done(0) + BASE)
                                g.tensor_scalar(h2[:, :, :], h2[:, :, :], act_s[:, 0:1], act_b[:, 0:1], ALU.mult,
                                                ALU.add).then_inc(h2_ready, 1)
                            elif slot == 26:
                                rsqrt_rms(t, 1)

            run_turns(pool, turn, link)

        @block.scalar
        def _(act):
            a = nc.scalar
            link = Link(act, act_step, ACT_STEPS)
            act.sem_inc(exp_done, ST_RING)
            act.wait_ge(loaded, LOADED)
            act.wait_ge(pool_set, POOL_SET)
            link(a.activation(tx[:, :], gx[:, :], ACT.Tanh))
            link(a.activation(tf[:, :], gf[:, :], ACT.Tanh))
            act.wait_ge(dve_set, DVE_SET)
            for wt in (wq0, wcq0, wq1):
                a.mul(wt[:, :], wt[:, :], SCALE)
            for n in (0, 1, 3):
                a.mul(bias_col[:, n:n + 1], bias_col[:, n:n + 1], SCALE)
            a.mul(wp0[:, :], wp0[:, :], tx[:, 0:1])
            link(a.mul(wo1[:, :], wo1[:, :], tx[:, 1:2]))
            a.mul(bp[0][:, :], bp[0][:, :], tx[:, 0:1]).then_inc(act_set, 1)
            a.mul(bp[1][:, :], bp[1][:, :], tx[:, 1:2]).then_inc(act_set, 1)
            link(a.mul(tf_half[:, :], tf[:, 1:2], 0.5))
            link(a.mul(down[:, :, :], down[:, :, :], tf_half[:, 0:1]))
            a.mul(down_b[:, :], down_b[:, :], tf[0:NE, 1:2]).then_inc(act_set, 1)
            a.mul(ma2t[:, :], wstat[:, 1:2], tf[:, 0:1]).then_inc(act_set, 1)
            act.wait_ge(act_set, ACT_SET)

            def filled(t, name):
                act.wait_ge(misc_full, t.use(name))

            def turned(t, name, dst, src):
                filled(t, name)
                a.copy(dst, src).then_inc(misc_free, 1)

            def context(t, what, layer, c):
                name = f"{what}{layer}.{c}"
                at, n = CHUNKS[c]
                phase = 1 - layer
                if what == "ctxT":
                    filled(t, name)
                    pairs_in = 4 if c == 0 else FULL // 2 - 4
                    first, n = 4 * 2 * P * c, pairs_in * P
                    dst = ctxT[0:CC, first:first + 2 * n].rearrange("c (k o p) -> c k o p", o=2, p=P)
                    if c:
                        a.copy(ctxT[0:CC, FULL * P:NK], MS[0:CC, n:n + TAIL])
                    for odd in range(2):
                        last = a.copy(dst[:, :, odd, :], MS[odd * CC:(odd + 1) * CC, 0:n].rearrange("c (k p) -> c k p", p=P))
                    last.then_inc(misc_free, 1)
                elif what == "key":
                    filled(t, name)
                    act.wait_ge(kparts_ready, t.before(phase, layer, len(CHUNKS), len(CHUNKS), c + BASE))
                    if c == 0:
                        act.wait_ge(key_out, t.before(phase, layer, 16 * PARTS, 16 * PARTS, BASE))
                    a.copy(kf[:, 0:n], MS[:, 0:n])
                    a.copy(kpart[0][:, at:at + n], MS[:, 0:n]).then_inc(misc_free, 1)
                else:
                    t0, rows = 4 * c, (P if c < 3 else TAIL)
                    t1 = min(t0 + 4, KT)
                    turned(t, name, VX[layer][0:rows, t0:t1, :, 0:D],
                           MS[0:rows, 0:(t1 - t0) * C].rearrange("p (t h d) -> p t h d", h=H, d=D))

            def queries(t, which, name, bias):
                filled(t, name)
                user, off = ((2, 0), (3, -1), (0, 1), (1, 0))[which]
                act.wait_ge(qparts_ready[user], t.done(off) + BASE)
                user, off = ((3, -1), (1, 0), (2, 0), (0, 0))[which]
                act.wait_ge(q_out[user], t.done(off, 16) + BASE)
                v = bias_col[:, bias:bias + 1]
                a.activation(qf[:, which % 2, :], MS[:, 0:T], ACT.Identity, bias=v)
                a.activation(qpart[:, which % 3, 0, :], MS[:, 0:T], ACT.Identity, bias=v).then_inc(misc_free, 1)

            def turn_maximum(t, phase, name):
                job = JOBS[int(name[-3])][int(name[-1])]
                filled(t, name)
                act.wait_ge(max_out[job.number % 2],
                            t.before(phase, job.layer, 16 * NJ[0] // 2, 16 * NJ[1] // 2, 16 * (job.number // 2) + BASE))
                a.copy(nT[:, job.number % 2, :], MSB[0:PARTS * HQ, 0:T]).then_inc(misc_free, 1)

            def hold(sem_, value):
                act.wait_ge(sem_, value)
                stand_alone(act)

            def maximum_out(t, phase, name, job):
                hold(misc_free, t.use(name))
                k = job.number % 2
                hold(max_in[k], t.before(phase, job.layer, 16 * NJ[0] // 2, 16 * NJ[1] // 2, 16 * (job.number // 2) + BASE))
                act.dma_start(max_rows[k], nT[:, k, :]).then_inc(max_out[k], 16)

            def maximum_in(t, phase, job):
                k = job.number % 2
                hold(max_out[k], t.before(phase, job.layer, 16 * NJ[0] // 2, 16 * NJ[1] // 2, 16 * (job.number // 2 + 1) + BASE))
                q = QX[job.layer] if job.cross else QS
                act.dma_start(q[FILL:ROWS, job.quad * HQ:(job.quad + 1) * HQ, :],
                             max_rows[k].rearrange("(r h) n -> r h n", h=HQ)).then_inc(max_in[k], 16)

            def take_values(t, phase, job):
                act.wait_ge(probs_free, count_done(t, phase, job, *SLOTS, job.tile0 + job.tiles + P_RING + BASE))
                a.copy(yt[:, job.number % 2, :], PV[:, 0:T]).then_inc(yt_ready, 1)

            def exponentials(t, phase, slot):
                job = [j for j in JOBS[phase] if j.tile0 <= slot][-1]
                tile = slot - job.tile0
                rows = TAIL if job.cross and tile == FULL else P
                cols = HQ // HALVES * (T if job.cross or tile == 0 else P)
                act.wait_ge(probs_free, t.before(phase, phase, *SLOTS, slot + 1 + BASE))
                for half in range(HALVES):
                    k = HALVES * slot + half
                    act.wait_ge(st_full, t.before(phase, phase, *UNITS, k + 1 + BASE))
                    a.activation(probs[0:rows, slot % P_RING, half * cols:(half + 1) * cols], ST[k % ST_RING][0:rows, 0:cols],
                                 ACT.Exp).then_inc(exp_done, 1)

            def turn(t):
                for phase in range(2):
                    for slot in range(SLOTS[phase]):
                        if t.attends(phase):
                            exponentials(t, phase, slot)
                        job = t.job_before(phase, slot)
                        if job:
                            take_values(t, phase, job)
                        for name in t.beside(phase, slot):
                            if name[0:2] == "nT":
                                turn_maximum(t, phase, name)
                                maximum_out(t, phase, name, JOBS[int(name[2])][int(name[4])])
                            elif name[0:4] == "ctxT":
                                context(t, "ctxT", int(name[4]), int(name[6]))
                            elif name[0:3] in ("key", "val"):
                                context(t, name[0:3], int(name[3]), int(name[5]))
                            elif name in ("yT0", "yT1"):
                                turned(t, name, yT[:, :], MS[:, 0:T])
                            elif name in ("xT0", "xT1", "xT2"):
                                turned(t, name, xnT[:, int(name[2]), :], MS[:, 0:T])
                            elif name in ("qc0", "q0", "k0", "qc1"):
                                which = ("qc0", "q0", "k0", "qc1").index(name)
                                queries(t, which, name, which)
                            elif name == "a1T":
                                turned(t, name, a1T[:, :], MSB[:, 0:T])
                            elif name in ("a2T.0", "a2T.1"):
                                turned(t, name, a2T[:, int(name[4]), :, :], MSB[:, 0:HID].rearrange("p (k q) -> p k q", k=HT))
                            elif name == "ln1b":
                                act.wait_ge(xn_ready[1], t.done(0) + BASE)
                                for q in range(QT):
                                    sq = a.activation(h2[:, q, 0:C], xn[:, 1, q, :], ACT.Square, accum_out=ssq[:, 0, q:q + 1])
                                sq.then_inc(ssq_ready[0], 1)
                            elif name == "route1":
                                act.wait_ge(misc_free, t.use("router"))
                                a.activation(lg[:, :, :], lg[:, :, :], ACT.Exp).then_inc(e_ready, 1)
                            elif name == "prT":
                                turned(t, name, prT, MS[0:NE, 0:T])
                            elif name[0:4] == "gate":
                                filled(t, name)
                                for f in range(FT):
                                    n = int(name[4]) * FT + f
                                    last = a.activation(gb[:, f, :], MS[:, f * T:(f + 1) * T], ACT.Identity,
                                                        bias=bias_gu[:, n:n + 1])
                                last.then_inc(misc_free, 1)
                                act.wait_ge(misc_free, t.use(name))
                                a.activation(tg, gb, ACT.Tanh, scale=0.5).then_inc(tg_ready, 1)
                        for name in t.beside(phase, slot - MAX_IN_AFTER):
                            if name[0:2] == "nT":
                                maximum_in(t, phase, JOBS[int(name[2])][int(name[4])])
                        if phase == 1 and t.attention0:
                            if slot == 22:
                                act.wait_ge(misc_free, t.use("hid.1"))
                                a.activation(h2[:, :, :], hr[:, :, :], ACT.Square).then_inc(sq_ready, 1)
                            elif slot == 25:
                                act.wait_ge(h2_ready, t.done(0) + BASE)
                                for q in range(QT):
                                    sq = a.activation(hr[:, q, :], h2[:, q, :], ACT.Square, accum_out=ssq[:, 1, q:q + 1])
                                sq.then_inc(ssq_ready[1], 1)

            run_turns(act, turn, link)

        @block.vector
        def _(dve):
            v = nc.vector
            link = Link(dve, dve_step, DVE_STEPS)
            dve.sem_inc(mx_free, MX_RING)
            v.memset(PV[:, :], 0.0).then_inc(dve_set, 1)
            dve.wait_ge(first_loaded, FIRST_LOADED)
            v.tensor_reduce(wabs[:, :], wraw[:, :, :], AX_X, ALU.add, apply_absolute_value=True).then_inc(dve_set, 1)
            dve.wait_ge(pe_set, 1)
            link(v.tensor_scalar(wstat[:, 0:2], MX[0][:, 0:2], 1.0 / (HID * C), EPS_Q, ALU.mult, ALU.max))
            link(v.reciprocal(wstat[:, 2:4], wstat[:, 0:2]))
            for i in range(2):
                link(v.tensor_scalar(wraw[:, i, :], wraw[:, i, :], wstat[:, 2 + i:3 + i], MAGIC, ALU.mult, ALU.add))
                link(v.tensor_scalar(wraw[:, i, :], wraw[:, i, :], MAGIC, 1.0, ALU.subtract, ALU.min))
                v.tensor_scalar(wtern[:, i, :], wraw[:, i, :], -1.0, None, ALU.max).then_inc(dve_set, 1)
            link(v.memset(pairs(KX_rows, 64, FILL), 0.0))
            dve.wait_ge(pe_set, PE_SET)
            v.tensor_copy(t1T[:, :], ST[0][:, :].bitcast(BF16)[:, 0:HID])
            v.tensor_copy(t2T[:, :, :], ST[1][:, :].bitcast(BF16)[:, 0:HID].rearrange("p (k c) -> p k c", k=HT))
            v.tensor_copy(rwT[:, :], ST[2][:, 0:NE]).then_inc(dve_set, 1)
            v.tensor_copy(bias_gu[:, :], MX[1][:, 0:2 * NE * FT]).then_inc(dve_set, 1)
            dve.wait_ge(dve_set, DVE_SET)
            dve.wait_ge(loaded, LOADED)
            dve.wait_ge(pool_set, POOL_SET)
            dve.wait_ge(act_set, ACT_SET)

            SOURCE = (x0, x1, x2, x3)
            OFF = (1, 0, -1, -2)

            def norm_statistics(t, site):
                src = SOURCE[site]
                if site == 0:
                    dve.wait_ge(x_in, t.done(1, 16) + BASE)
                elif site == 2:
                    dve.wait_ge(misc_free, t.bank())
                else:
                    dve.wait_ge(misc_free, t.use("proj0" if site == 1 else "proj1"))
                for q in range(QT):
                    s = v.bn_stats(stats[:, site, q, :], src[:, q, :])
                link(s)
                stand_alone(dve)
                for q in range(QT):
                    s = v.bn_aggr(mv[:, site, q, :], stats[:, site, q, :])
                s.then_inc(mean_ready[site], 1)

            def normalise(t, site):
                before = {0: "xT1", 1: "xT2"}.get(site)
                dve.wait_ge(misc_full, t.use(before) if before in t.position else t.bank())
                dve.wait_ge(rstd_ready[site], t.done(OFF[site]) + BASE)
                src = SOURCE[site]
                for q in range(QT):
                    s = v.tensor_scalar(xn[:, site % 2, q, :], src[:, q, :], mv[:, site, q, 0:1], rstd[:, site, q:q + 1],
                                        ALU.subtract, ALU.mult)
                s.then_inc(xn_ready[site], 1)

            def maximum(t, phase, job, n):
                k = job.mx0 + n
                dve.wait_ge(mx_full, t.before(phase, job.layer, *MAXIMA, k + 1 + BASE))
                bank = MX[k % MX_RING]
                if job.cross:
                    ins = v.reduce_max(mx[:, job.number % 2, n:n + 1], bank[:, 0:MXW[n % 4]], AX_X)
                else:
                    keys = (n % QT + 1) * P
                    stand_alone(dve)
                    ins = v.tensor_tensor_reduce(out=mxs[:, 0:keys], in0=bank[:, 0:keys], in1=causal[:, 2 * P - keys:2 * P],
                                                 scale=1.0, scalar=LOWEST, op0=ALU.add, op1=ALU.max,
                                                 accum_out=mx[:, job.number % 2, n:n + 1])
                ins.then_inc(mx_free, 1)
                if not job.cross:
                    dve.wait_ge(mx_free, t.before(phase, job.layer, *MAXIMA, k + 1 + MX_RING + BASE))
                if n == job.maxima - 1:
                    negate_maximum(t, phase, job)

            def negate_maximum(t, phase, job):
                k = job.number % 2
                dve.wait_ge(mx_free, t.before(phase, job.layer, *MAXIMA, job.mx0 + job.maxima + MX_RING + BASE))
                dve.wait_ge(nparts_ready, t.before(phase, job.layer, *NJ, max(job.number - 1, 0) + BASE))
                out = nm[:, k, :, :].rearrange("p t h -> p h t")
                if job.cross:
                    v.tensor_reduce(out, mx[:, k, :].rearrange("p (h t c) -> p h t c", h=HQ, t=QT), AX_X, ALU.max,
                                    negate=True).then_inc(nm_ready, 1)
                else:
                    v.tensor_scalar(out, mx[:, k, 0:HQ * QT].rearrange("p (h t) -> p h t", t=QT), -1.0, None,
                                    ALU.mult).then_inc(nm_ready, 1)

            def divide(t, name):
                job = JOBS[int(name[1])][int(name[3])]
                dve.wait_ge(misc_full, t.use(name))
                y = MS[:, 0:QT * HQ * (D + 1)].rearrange("p (t j r) -> p t j r", t=QT, j=HQ)
                link(v.reciprocal(rden[:, :, :], y[:, :, :, D]))
                dst = yx[job.layer] if job.cross else ys
                v.tensor_tensor(dst[:, :, job.quad * HQ:(job.quad + 1) * HQ, :], y[:, :, :, 0:D],
                                rden[:, :, :].unsqueeze(3).broadcast_to([P, QT, HQ, D]), ALU.mult).then_inc(misc_free, 1)
                if name == "Y0.7":
                    dve.wait_ge(misc_free, t.use(name))
                    v.tensor_tensor(yx[0][:, :, :, :], yx[0][:, :, :, :], ys[:, :, :, :], ALU.add).then_inc(y_ready, 1)

            def project(t, layer, dst):
                dve.wait_ge(misc_full, t.use(f"proj{layer}"))
                dve.wait_ge(xb_ready[layer], t.done(-2 if layer else 0) + BASE)
                v.tensor_tensor(dst[:, :, :], MS[:, 0:T].rearrange("p (t c) -> p t c", t=QT), xb[:, layer, :, :],
                                ALU.add).then_inc(misc_free, 1)

            def quantise(t, step):
                site = int(step >= 2)
                src, xh, weight = ((xn[:, 1, :, :], xh1, nw1), (h2[:, :, :], hr, nw2))[site]
                if step in (0, 2):
                    dve.wait_ge(rms_ready[site], t.done(0) + BASE)
                    for i in range(QT):
                        s = v.scalar_tensor_tensor(out=xh[:, i, :], in0=src[:, i, :], scalar=rms[:, site, i:i + 1],
                                                   in1=weight[:, :], op0=ALU.mult, op1=ALU.mult)
                    link(s)
                if step in (0, 3):
                    link(v.tensor_reduce(amax[:, site, :], xh[:, :, :], AX_X, ALU.max, apply_absolute_value=True))
                if step in (1, 4):
                    link(v.tensor_scalar(amax[:, site, :], amax[:, site, :], EPS_Q, None, ALU.max))
                    link(v.reciprocal(qs[:, site, :], amax[:, site, :]))
                    link(v.tensor_scalar(qs[:, site, :], qs[:, site, :], 127.0, None, ALU.mult))
                    back = wstat[:, 0:1] if site == 0 else ma2t[:, 0:1]
                    v.tensor_scalar(dq[:, site, :], amax[:, site, :], 1.0 / 127.0, back, ALU.mult, ALU.mult)
                if step in (1, 5):
                    for i in range(QT):
                        s = v.tensor_scalar(xh[:, i, :], xh[:, i, :], qs[:, site, i:i + 1], MAGIC, ALU.mult, ALU.add)
                    link(s)
                if step in (1, 6):
                    q, ready = ((a1, a1_ready), (a2, a2_ready))[site]
                    v.tensor_scalar(q[:, :, :], xh[:, :, :], MAGIC, None, ALU.subtract).then_inc(ready, 1)

            def wide(ap):
                return ap.unsqueeze(2).broadcast_to([P, QT, NE])

            def logits(t):
                dve.wait_ge(misc_full, t.use("router"))
                L = MS[:, 0:QT * NE].rearrange("p (t e) -> p t e", t=QT)
                link(v.tensor_reduce(r1[:, 0, :], L, AX_X, ALU.max))
                v.tensor_tensor(lg[:, :, :], L, wide(r1[:, 0, :]), ALU.subtract).then_inc(misc_free, 1)

            def largest(n, src):
                index = index_score[:, :].unsqueeze(1).broadcast_to([P, QT, NE])
                link(v.tensor_reduce(r1[:, 3, :], src[:, :, :], AX_X, ALU.max))
                link(v.tensor_tensor(pick[:, :, :], src[:, :, :], wide(r1[:, 3, :]), ALU.is_ge))
                link(v.tensor_tensor(pick[:, :, :], pick[:, :, :], index, ALU.mult))
                link(v.tensor_reduce(r1[:, 4, :], pick[:, :, :], AX_X, ALU.max))
                link(v.tensor_tensor(hot[:, n, :, :], pick[:, :, :], wide(r1[:, 4, :]), ALU.is_equal))

            def route(t, step):
                if step == 1:
                    dve.wait_ge(e_ready, t.done(-2) + BASE)
                    link(v.tensor_reduce(r1[:, 1, :], lg[:, :, :], AX_X, ALU.add))
                    link(v.reciprocal(r1[:, 2, :], r1[:, 1, :]))
                    link(v.tensor_tensor(pr[:, :, :], lg[:, :, :], wide(r1[:, 2, :]), ALU.mult))
                elif step == 2:
                    largest(0, pr)
                    link(v.scalar_tensor_tensor(out=rest[:, :, :], in0=hot[:, 0, :, :], scalar=-2.0, in1=pr[:, :, :],
                                                op0=ALU.mult, op1=ALU.add))
                else:
                    largest(1, rest)
                    link(v.tensor_tensor(hot[:, 0, :, :], hot[:, 0, :, :], hot[:, 1, :, :], ALU.add))
                    link(v.tensor_tensor(pr[:, :, :], pr[:, :, :], hot[:, 0, :, :], ALU.mult))
                    link(v.tensor_reduce(r1[:, 1, :], pr[:, :, :], AX_X, ALU.add))
                    link(v.tensor_scalar(r1[:, 1, :], r1[:, 1, :], 1e-9, None, ALU.add))
                    link(v.reciprocal(r1[:, 2, :], r1[:, 1, :]))
                    v.tensor_tensor(wts[:, :, :], pr[:, :, :], wide(r1[:, 2, :]), ALU.mult).then_inc(wts_ready, 1)

            def expert_hidden(t, e):
                dve.wait_ge(tg_ready, t.done(-3, NE, e + 1 + BASE))
                link(v.scalar_tensor_tensor(out=tg, in0=tg, scalar=1.0, in1=gb, op0=ALU.add, op1=ALU.mult))
                dve.wait_ge(misc_full, t.use(f"up{e}"))
                for f in range(FT):
                    n = NE * FT + e * FT + f
                    s = v.scalar_tensor_tensor(out=hh[:, f, :], in0=MS[:, f * T:(f + 1) * T],
                                               scalar=bias_gu[:, n:n + 1], in1=tg[:, f, :], op0=ALU.add, op1=ALU.mult)
                s.then_inc(misc_free, 1)

            def expert_out(t, e):
                if e == 0:
                    dve.wait_ge(wts_ready, t.done(-2) + BASE)
                    dve.wait_ge(stored, t.done(-3, 16) + BASE)
                else:
                    dve.wait_ge(misc_free, t.use(f"down{e - 1}"))
                dve.wait_ge(misc_full, t.use(f"down{e}"))
                src = acc if e else x3
                for q in range(QT):
                    s = v.scalar_tensor_tensor(out=acc[:, q, :], in0=MS[:, q * C:(q + 1) * C],
                                               scalar=wts[:, q, e:e + 1], in1=src[:, q, :], op0=ALU.mult, op1=ALU.add)
                s.then_inc(misc_free, 1)

            def beside(t, name):
                if name[0] == "Y":
                    divide(t, name)
                elif name[0:2] == "ln":
                    (norm_statistics if name[3] == "a" else normalise)(t, int(name[2]))
                elif name == "proj0":
                    project(t, 0, x1)
                elif name == "proj1":
                    project(t, 1, x3)
                elif name == "v0":
                    dve.wait_ge(misc_full, t.use(name))
                    for q in range(QT):
                        s = v.tensor_tensor(VS[:, q, :, 0:D], MS[:, q * C:(q + 1) * C].rearrange("p (h d) -> p h d", d=D),
                                            bv0[:, :].rearrange("p (h d) -> p h d", d=D), ALU.add)
                    s.then_inc(misc_free, 1)
                elif name[0:5] == "quant":
                    quantise(t, int(name[5]))
                elif name in ("hid.0", "hid.1"):
                    q = int(name[4])
                    dve.wait_ge(misc_full, t.use(name))
                    v.tensor_scalar(hr[:, q, :], MS[:, :], 0.0, dq[:, 0, q:q + 1], ALU.max, ALU.mult).then_inc(misc_free, 1)
                elif name == "ffn":
                    dve.wait_ge(misc_full, t.use(name))
                    dve.wait_ge(xb_ready[1], t.done(-1) + BASE)
                    for q in range(QT):
                        s = v.scalar_tensor_tensor(out=x2[:, q, :], in0=MS[:, q * C:(q + 1) * C], scalar=dq[:, 1, q:q + 1],
                                                   in1=x1[:, q, :], op0=ALU.mult, op1=ALU.add)
                    s.then_inc(misc_free, 1)
                elif name == "router":
                    logits(t)
                elif name[0:5] == "route":
                    route(t, int(name[5]))
                elif name[0:2] == "up":
                    expert_hidden(t, int(name[2]))
                elif name == "downb":
                    dve.wait_ge(misc_free, t.use(f"down{NE - 1}"))
                    dve.wait_ge(misc_full, t.use(name))
                    v.tensor_tensor(acc[:, :, :], MS[:, 0:T].rearrange("p (t c) -> p t c", t=QT), acc[:, :, :],
                                    ALU.add).then_inc(misc_free, 1)
                elif name[0:4] == "down":
                    expert_out(t, int(name[4]))

            def turn(t):
                for phase in range(2):
                    for slot in range(SLOTS[phase]):
                        for job, n in t.maxima(phase, slot):
                            maximum(t, phase, job, n)
                        for name in t.beside(phase, slot):
                            beside(t, name)

            run_turns(dve, turn, link)

        @block.tensor
        def _(pe):
            t_ = nc.tensor
            pe.sem_inc(probs_free, P_RING)
            pe.sem_inc(quad_scored, QUADS)
            pe.wait_ge(first_loaded, FIRST_LOADED)
            pe.wait_ge(pool_set, 3)
            pe.wait_ge(dve_set, 2)
            t_.matmul(MX[0][:, 0:2], ones[:, :], wabs[:, :], start=True, stop=True).then_inc(pe_set, 1)
            pe.wait_ge(dve_set, 4)
            for i in range(2):
                for k in range(HT):
                    t_.transpose(ST[i][:, :].bitcast(BF16)[:, k * P:(k + 1) * P], wtern[:, i, k * P:(k + 1) * P], ident_b[:, :])
            t_.transpose(ST[2][:, 0:NE], rw[:, :], ident[0:NE, 0:NE])
            t_.transpose(MX[1][:, 0:2 * NE * FT], bias_rows[:, :],
                         ident[0:2 * NE * FT, 0:2 * NE * FT]).then_inc(pe_set, 1)
            pe.wait_ge(dve_set, DVE_SET)
            pe.wait_ge(act_set, ACT_SET)
            pe.wait_ge(pool_set, POOL_SET)
            pe.wait_ge(loaded, LOADED)

            def maximum(t, phase, job, n):
                k = job.mx0 + n
                if n == 0:
                    off = t.at(phase, job.layer)
                    if job.cross:
                        pe.wait_ge(kx_in[job.quad], t.before(phase, job.layer, SENT, SENT, SENT + BASE))
                        pe.wait_ge(q_in[3 if job.layer else 0], t.done(off, SENT) + BASE)
                    elif job.quad == 0:
                        pe.wait_ge(q_in[1], t.done(off, SENT) + BASE)
                        pe.wait_ge(q_in[2], t.done(off, SENT) + BASE)
                extra = MX_EXTRA[k] if k < MX_RING else 0
                pe.wait_ge(mx_free, t.before(phase, job.layer, *MAXIMA, k + 1 + extra + BASE))
                if job.cross:
                    j, q, c = n // (QT * 4), n // 4 % QT, n % 4
                    h, keys, at, side = job.quad * HQ + j, MXW[c], MX0[c], QX[job.layer]
                    rhs = KX[0:FILL, h, at:at + keys]
                else:
                    j, q = n // QT, n % QT
                    h, keys, side = job.quad * HQ + j, (q + 1) * P, QS
                    rhs = KS[0:FILL, h, 0:keys]
                t_.matmul(MX[k % MX_RING][:, 0:keys], side[0:FILL, h, q * P:(q + 1) * P], rhs, start=True,
                          stop=True).then_inc(mx_full, 1)

            def score(t, phase, job, tile, half):
                k = HALVES * (job.tile0 + tile) + half
                if tile == 0 and half == 0:
                    pe.wait_ge(max_in[job.number % 2],
                               t.before(phase, phase, 16 * NJ[0] // 2, 16 * NJ[1] // 2, 16 * (job.number // 2 + 1) + BASE))
                extra = ST_EXTRA[k] if k < ST_RING else 0
                pe.wait_ge(exp_done, t.before(phase, phase, *UNITS, k + 1 + extra + BASE))
                for j in range(HQ // HALVES):
                    h = job.quad * HQ + half * (HQ // HALVES) + j
                    if job.cross:
                        n, lo, q, keys = (P if tile < FULL else TAIL), 0, QX[job.layer], KX
                    else:
                        n, lo, q, keys = P, tile * P, QS, KS
                    last = t_.matmul(ST[k % ST_RING][0:n, j * (T - lo):(j + 1) * (T - lo)], keys[:, h, tile * P:tile * P + n],
                                     q[:, h, lo:T], start=True, stop=True)
                last.then_inc(st_full, 1)

            def values(t, phase, job, tile):
                k = job.tile0 + tile
                if tile == 0:
                    pe.wait_ge(yt_ready, count_done(t, phase, job, *NJ, job.number + BASE))
                if job.cross:
                    pe.wait_ge(exp_done, count_done(t, phase, job, *UNITS, HALVES * (k + 1) + ST_RING + BASE))
                else:
                    pe.wait_ge(masked, t.done(-1, QUADS * QT, job.quad * QT + tile + 1 + BASE))
                n = TAIL if job.cross and tile == FULL else P
                lo = 0 if job.cross else tile * P
                vals = VX[job.layer] if job.cross else VS
                for j in range(HQ):
                    h = job.quad * HQ + j
                    last = t_.matmul(PV[32 * j:32 * j + D + 1, lo:T], vals[0:n, tile, h, :],
                                     probs[0:n, k % P_RING, j * (T - lo):(j + 1) * (T - lo)],
                                     start=(tile == 0), stop=(tile == job.tiles - 1))
                    if tile == job.tiles - 1 and j == 0:
                        last.then_inc(quad_scored if job.cross else self_scored, 1)
                last.then_inc(probs_free, 1)

            def open_misc(t, name):
                assert t.names[t.next_use] == name
                t.next_use += 1
                pe.wait_ge(misc_free, t.bank(t.position[name]))

            def tokens_by_tile(rhs_of):
                for q in range(QT):
                    last = rhs_of(q)
                last.then_inc(misc_full, 1)

            def context(t, what, layer, c):
                tiles = range(4 * c, min(4 * c + 4, KT))
                at, n = CHUNKS[c]
                if what == "key":
                    t_.matmul(MS[:, 0:n], wck[layer][:, :], ctxT[:, at:at + n], start=True, stop=True).then_inc(misc_full, 1)
                    return
                if what == "ctxT":
                    if c == 0:
                        pe.wait_ge(ctx_in, t.before(1 - layer, layer, 32, 32, 32 + BASE))
                    stand_alone(pe)
                    for n, k in enumerate(range(4 * c, min(4 * c + 4, FULL // 2))):
                        last = t_.transpose(MS[:, n * P:(n + 1) * P], ctx[:, 2 * k * CC:(2 * k + 2) * CC], ident[:, :])
                    if c:
                        last = t_.transpose(MS[0:CC, (n + 1) * P:(n + 1) * P + TAIL], ctx[0:TAIL, FULL * CC:KT * CC],
                                            ident[0:TAIL, 0:TAIL])
                    last.then_inc(misc_full, 1)
                    return
                for k in tiles:
                    n = P if k < FULL else TAIL
                    last = t_.matmul(MS[0:n, (k % 4) * C:(k % 4 + 1) * C], ctxT[:, k * P:k * P + n], wcv[layer][:, :],
                                     start=True, stop=True)
                last.then_inc(misc_full, 1)

            def beside(t, phase, name):
                if not t.in_bank(name):
                    return
                open_misc(t, name)
                if name[0:2] == "nT":
                    job = JOBS[int(name[2])][int(name[4])]
                    pe.wait_ge(nparts_ready, t.before(phase, job.layer, *NJ, job.number + 1 + BASE))
                    for q in range(QT):
                        last = t_.transpose(MSB[0:PARTS * HQ, q * P:(q + 1) * P],
                                            npart[:, job.number % 2, q, :, :].rearrange("p r h -> p (r h)"), ident_b[:, :])
                    last.then_inc(misc_full, 1)
                elif name[0] == "Y":
                    job = JOBS[int(name[1])][int(name[3])]
                    pe.wait_ge(yt_ready, count_done(t, phase, job, *NJ, job.number + 1 + BASE))
                    pick_rows = ident[:, :].rearrange("p (j r) -> p j r", j=HQ)[:, :, 0:D + 1]
                    n = HQ * (D + 1)
                    tokens_by_tile(lambda q: t_.matmul(MS[:, q * n:(q + 1) * n], yt[:, job.number % 2, q * P:(q + 1) * P],
                                                       pick_rows, start=True, stop=True))
                elif name[0:4] == "ctxT":
                    context(t, "ctxT", int(name[4]), int(name[6]))
                elif name[0:3] in ("key", "val"):
                    context(t, name[0:3], int(name[3]), int(name[5]))
                elif name in ("xT0", "xT1", "xT2"):
                    site = (0, 2, 3)[int(name[2])]
                    pe.wait_ge(xn_ready[site], t.done((1, 0, -1, -2)[site]) + BASE)
                    tokens_by_tile(lambda q: t_.transpose(MS[:, q * P:(q + 1) * P], xn[:, site % 2, q, :], ident[:, :]))
                elif name in ("qc0", "q0", "k0", "qc1"):
                    weight, site = {"qc0": (wcq0, 0), "q0": (wq0, 0), "k0": (wk0, 0), "qc1": (wq1, 1)}[name]
                    t_.matmul(MS[:, 0:T], weight[:, :], xnT[:, site, :], start=True, stop=True).then_inc(misc_full, 1)
                elif name == "v0":
                    tokens_by_tile(lambda q: t_.matmul(MS[:, q * C:(q + 1) * C], xnT[:, 0, q * P:(q + 1) * P], wv0[:, :],
                                                       start=True, stop=True))
                elif name in ("yT0", "yT1"):
                    layer = int(name[2])
                    if layer == 0:
                        pe.wait_ge(y_ready, t.done(0) + BASE)
                    y = yx[layer][:, :, :, :].rearrange("p t h d -> p t (h d)")
                    tokens_by_tile(lambda q: t_.transpose(MS[:, q * P:(q + 1) * P], y[:, q, :], ident[:, :]))
                elif name in ("proj0", "proj1"):
                    weight = wo1 if name == "proj1" else wp0
                    tokens_by_tile(lambda q: t_.matmul(MS[:, q * C:(q + 1) * C], yT[:, q * P:(q + 1) * P], weight[:, :],
                                                       start=True, stop=True))
                elif name == "a1T":
                    pe.wait_ge(a1_ready, t.done(0) + BASE)
                    tokens_by_tile(lambda q: t_.transpose(MSB[:, q * P:(q + 1) * P], a1[:, q, :], ident_b[:, :]))
                elif name in ("hid.0", "hid.1"):
                    q = int(name[4])
                    t_.matmul(MS[:, :], a1T[:, q * P:(q + 1) * P], t1T[:, :], start=True, stop=True).then_inc(misc_full, 1)
                elif name in ("a2T.0", "a2T.1"):
                    q = int(name[4])
                    pe.wait_ge(a2_ready, t.done(0) + BASE)
                    for k in range(HT):
                        last = t_.transpose(MSB[:, k * P:(k + 1) * P], a2[:, q, k * P:(k + 1) * P], ident_b[:, :])
                    last.then_inc(misc_full, 1)
                elif name == "ffn":
                    for q in range(QT):
                        for k in range(HT):
                            last = t_.matmul(MS[:, q * C:(q + 1) * C], a2T[:, q, k, :], t2T[:, k, :], start=(k == 0),
                                             stop=(k == HT - 1))
                    last.then_inc(misc_full, 1)
                elif name == "router":
                    tokens_by_tile(lambda q: t_.matmul(MS[:, q * NE:(q + 1) * NE], xnT[:, 2, q * P:(q + 1) * P], rwT[:, :],
                                                       start=True, stop=True))
                elif name == "prT":
                    pe.wait_ge(wts_ready, t.done(-2) + BASE)
                    tokens_by_tile(lambda q: t_.transpose(MS[0:NE, q * P:(q + 1) * P], wts[:, q, :], ident[:, :]))
                elif name == "downb":
                    tokens_by_tile(lambda q: t_.matmul(MS[:, q * C:(q + 1) * C], prT[:, q * P:(q + 1) * P], down_b[:, :],
                                                       start=True, stop=True))
                elif name[0:4] == "gate" or name[0:2] == "up":
                    e = int(name[-1])
                    weight = gate if name[0] == "g" else up
                    for f in range(FT):
                        last = t_.matmul(MS[:, f * T:(f + 1) * T], weight[:, e, f * P:(f + 1) * P], xnT[:, 2, :],
                                         start=True, stop=True)
                    last.then_inc(misc_full, 1)
                else:
                    assert name[0:4] == "down", name
                    e = int(name[4])
                    for q in range(QT):
                        for f in range(FT):
                            last = t_.matmul(MS[:, q * C:(q + 1) * C], hh[:, f, q * P:(q + 1) * P],
                                             down[:, e * FT + f, :], start=(f == 0), stop=(f == FT - 1))
                    last.then_inc(misc_full, 1)

            def turn(t):
                t.next_use = 0
                for phase in range(2):
                    for slot in range(SLOTS[phase]):
                        before = None
                        if slot == 0:
                            if t.attention0 if phase else t.experts:
                                job = JOBS[1 - phase][-1]
                                before = (job, job.tiles - 1)
                        elif t.attends(phase):
                            job = [j for j in JOBS[phase] if j.tile0 <= slot - 1][-1]
                            before = (job, slot - 1 - job.tile0)
                        steps = t.maxima(phase, slot)
                        job = [j for j in JOBS[phase] if j.tile0 <= slot][-1]
                        for half in range(HALVES):
                            if t.attends(phase):
                                score(t, phase, job, slot - job.tile0, half)
                            for step in steps[half:half + 1]:
                                maximum(t, phase, *step)
                        if before:
                            values(t, phase, *before)
                        for step in steps[2:3]:
                            maximum(t, phase, *step)
                        for name in t.beside(phase, slot):
                            beside(t, phase, name)
                        for step in steps[3:]:
                            maximum(t, phase, *step)

            run_turns(pe, turn)


_INS = ["x", "ctx_512", "g_xattn", "g_ffn",
        "L0_xattn_Wk", "L0_xattn_bk", "L0_xattn_Wq", "L0_xattn_bq", "L0_xattn_Wv", "L0_xattn_bv",
        "L0_xattn_Wck", "L0_xattn_bck", "L0_xattn_Wcq", "L0_xattn_bcq", "L0_xattn_Wcv", "L0_xattn_bcv",
        "L0_xattn_Wp", "L0_xattn_bp", "L0_ffn_norm1_w", "L0_ffn_w1", "L0_ffn_act_scale", "L0_ffn_act_bias",
        "L0_ffn_norm2_w", "L0_ffn_w2", "L1_xattn_Wq", "L1_xattn_bq", "L1_xattn_Wk", "L1_xattn_bk",
        "L1_xattn_Wv", "L1_xattn_bv", "L1_xattn_Wo", "L1_xattn_bo", "L1_ffn_router_w", "L1_ffn_gate_w",
        "L1_ffn_gate_b", "L1_ffn_up_w", "L1_ffn_up_b", "L1_ffn_down_w", "L1_ffn_down_b"]


def kernel(**inputs):
    import numpy as _np
    import concourse.bacc as _bacc
    from concourse import mybir as _mybir
    from concourse.bass_utils import run_bass_kernel_spmd as _run

    nc = _bacc.Bacc("TRN2", target_bir_lowering=False, num_devices=1)
    arrays, args = {}, {}
    for name in _INS:
        a = _np.ascontiguousarray(inputs[name])
        arrays[f"in_{name}"] = a
        args[name] = nc.dram_tensor(f"in_{name}", a.shape, _mybir.dt.from_np(a.dtype), kind="ExternalInput").ap()
    out = nc.dram_tensor("out_x", arrays["in_x"].shape, _mybir.dt.float32, kind="ExternalOutput").ap()
    x_d, ctx_d = args.pop("x"), args.pop("ctx_512")
    flamingo_gated_blocks(nc, args, x_d, ctx_d, out)
    r = _run(nc, [arrays], core_ids=[0])
    return r.results[0]["out_x"]
```
